# Optimizing a Trainium2 kernel written in Bass

```python
import numpy as np
import jax
import jax.numpy as jnp

def _softmax(x, axis=-1):
    return jax.nn.softmax(x, axis=axis)

def _gelu(x):
    return jax.nn.gelu(x, approximate=True)

def _silu(x):
    return jax.nn.silu(x)

def _sigmoid(x):
    return jax.nn.sigmoid(x)

def _layernorm(x, axis=-1, eps=1e-05):
    m = jnp.mean(x, axis=axis, keepdims=True)
    v = jnp.var(x, axis=axis, keepdims=True)
    return (x - m) / jnp.sqrt(v + eps)

def _scatter_add(tgt, idx, src, axis=0):
    return tgt.at[idx].add(src)

def _segment_sum(src, seg, n):
    return jax.ops.segment_sum(src, seg, n)
kernel_name = 'mk_vit_tower_d1_tok_img2048_r4_af148f'

def setup_inputs(seed: int=0):
    np.random.seed(seed)
    _w = jnp.asarray

    def _rec_inputs():
        import jax
        import jax.numpy as jnp
        _rk = jax.random.key(seed)
        x = -0.00178296 + 0.498989 * jax.random.normal(jax.random.fold_in(_rk, 1), (8, 256, 64, 2), jnp.float32)
        return x
    x = _rec_inputs()

    def _L0_tok_setup():
        import jax, jax.numpy as jnp
        import numpy as np
        H, N, CCH, LLEN = (256, 64, 1, 512)
        key = jax.random.key(seed)
        k1, k2 = jax.random.split(key, 2)
        log_dt = jax.random.uniform(k1, (H,), jnp.float32, float(np.log(0.001)), float(np.log(0.1)))
        C = 0.5 * jax.random.normal(k2, (CCH, H, N, 2), jnp.float32)
        log_w_real = jnp.full((H, N), float(np.log(0.5)), jnp.float32)
        w_imag = jnp.broadcast_to(np.pi * jnp.arange(N, dtype=jnp.float32), (H, N)) + jnp.zeros((H, N), jnp.float32)
        return {'C': C, 'log_dt': log_dt, 'log_w_real': log_w_real, 'w_imag': w_imag, 'L': LLEN}
    _L0_tok_all = _L0_tok_setup()
    _L0_tok_in = {k: v for k, v in _L0_tok_all.items() if k in ('log_dt', 'log_w_real', 'w_imag')}
    del _L0_tok_all

    def _L0_attn_setup():
        import jax, jax.numpy as jnp
        import numpy as np
        B, S, HID = (1, 512, 512)
        NH, NKV, HD = (16, 4, 128)
        WIN = 256
        THETA = 10000.0

        def _rotate_half(x):
            h = x.shape[-1] // 2
            return jnp.concatenate((-x[..., h:], x[..., :h]), axis=-1)

        def _rope_cos_sin(seq_len, dtype):
            inv_freq = 1.0 / THETA ** (jnp.arange(0, HD, 2, dtype=jnp.float32) / HD)
            t = jnp.arange(seq_len, dtype=jnp.float32)
            freqs = jnp.outer(t, inv_freq)
            emb = jnp.concatenate((freqs, freqs), axis=-1)
            return (jnp.cos(emb).astype(dtype)[None, None], jnp.sin(emb).astype(dtype)[None, None])
        key = jax.random.key(seed)
        ks = jax.random.split(key, 5)
        return {'hidden_states': jax.random.normal(ks[0], (B, S, HID), dtype=jnp.float32), 'w_q': jax.random.normal(ks[1], (HID, NH * HD), dtype=jnp.float32) * 0.02, 'w_k': jax.random.normal(ks[2], (HID, NKV * HD), dtype=jnp.float32) * 0.02, 'w_v': jax.random.normal(ks[3], (HID, NKV * HD), dtype=jnp.float32) * 0.02, 'w_o': jax.random.normal(ks[4], (NH * HD, HID), dtype=jnp.float32) * 0.02}
    _L0_attn_all = _L0_attn_setup()
    _L0_attn_in = {k: v for k, v in _L0_attn_all.items() if k in ('w_q', 'w_k', 'w_v', 'w_o')}
    del _L0_attn_all

    def _L0_ffn_setup():
        import jax, jax.numpy as jnp
        import numpy as np
        B, T, D = (4, 256, 512)
        N, S, H = (8, 8, 8)
        ETA = 1.0
        key = jax.random.key(seed)
        ks = jax.random.split(key, 9)
        return {'x': jax.random.normal(ks[0], (B, T, D), jnp.float32), 'select_weight': jax.random.normal(ks[1], (N, D, S), jnp.float32) / D, 'select_mean_diff': jax.random.normal(ks[2], (N, D), jnp.float32) / D, 'imp_center': jax.random.normal(ks[3], (N,), jnp.float32), 'imp_slope': jax.random.normal(ks[4], (N,), jnp.float32) * 5.0, 'lora_update': jax.random.normal(ks[5], (N, D, H), jnp.float32) * 0.02, 'lora_degen': jax.random.normal(ks[6], (N, D, H), jnp.float32) * 0.02, 'bias_w': jax.random.normal(ks[7], (N, D), jnp.float32) * 0.02, 'debias_w': jax.random.normal(ks[8], (N, D), jnp.float32) * 0.02}
    _L0_ffn_all = _L0_ffn_setup()
    _L0_ffn_in = {k: v for k, v in _L0_ffn_all.items() if k in ('select_weight', 'select_mean_diff', 'imp_center', 'imp_slope', 'lora_update', 'lora_degen', 'bias_w', 'debias_w')}
    del _L0_ffn_all
    return {'x': x, 'L0_tok_log_dt': _L0_tok_in['log_dt'], 'L0_tok_log_w_real': _L0_tok_in['log_w_real'], 'L0_tok_w_imag': _L0_tok_in['w_imag'], 'L0_attn_w_q': _L0_attn_in['w_q'], 'L0_attn_w_k': _L0_attn_in['w_k'], 'L0_attn_w_v': _L0_attn_in['w_v'], 'L0_attn_w_o': _L0_attn_in['w_o'], 'L0_ffn_select_weight': _L0_ffn_in['select_weight'], 'L0_ffn_select_mean_diff': _L0_ffn_in['select_mean_diff'], 'L0_ffn_imp_center': _L0_ffn_in['imp_center'], 'L0_ffn_imp_slope': _L0_ffn_in['imp_slope'], 'L0_ffn_lora_update': _L0_ffn_in['lora_update'], 'L0_ffn_lora_degen': _L0_ffn_in['lora_degen'], 'L0_ffn_bias_w': _L0_ffn_in['bias_w'], 'L0_ffn_debias_w': _L0_ffn_in['debias_w']}

def reference(x, L0_tok_log_dt, L0_tok_log_w_real, L0_tok_w_imag, L0_attn_w_q, L0_attn_w_k, L0_attn_w_v, L0_attn_w_o, L0_ffn_select_weight, L0_ffn_select_mean_diff, L0_ffn_imp_center, L0_ffn_imp_slope, L0_ffn_lora_update, L0_ffn_lora_degen, L0_ffn_bias_w, L0_ffn_debias_w):
    import jax
    import jax.numpy as jnp

    def _L0_tok_ref(C, log_dt, log_w_real, w_imag, L):
        import jax, jax.numpy as jnp
        import numpy as np
        H, N, CCH, LLEN = (256, 64, 1, 512)
        dt = jnp.exp(log_dt)
        Cc = C[..., 0] + 1j * C[..., 1]
        w = -jnp.exp(log_w_real) + 1j * w_imag
        dtA = w * dt[:, None]
        K = dtA[:, :, None] * jnp.arange(L)
        Cm = Cc * (jnp.exp(dtA) - 1.0) / w
        K = jnp.einsum('chn,hnl->chl', Cm, jnp.exp(K))
        return 2 * K.real

    def _L0_attn_ref(hidden_states, w_q, w_k, w_v, w_o):
        import jax, jax.numpy as jnp
        import numpy as np
        B, S, HID = (1, 512, 512)
        NH, NKV, HD = (16, 4, 128)
        WIN = 256
        THETA = 10000.0

        def _rotate_half(x):
            h = x.shape[-1] // 2
            return jnp.concatenate((-x[..., h:], x[..., :h]), axis=-1)

        def _rope_cos_sin(seq_len, dtype):
            inv_freq = 1.0 / THETA ** (jnp.arange(0, HD, 2, dtype=jnp.float32) / HD)
            t = jnp.arange(seq_len, dtype=jnp.float32)
            freqs = jnp.outer(t, inv_freq)
            emb = jnp.concatenate((freqs, freqs), axis=-1)
            return (jnp.cos(emb).astype(dtype)[None, None], jnp.sin(emb).astype(dtype)[None, None])
        b, s, _ = hidden_states.shape
        dt = hidden_states.dtype
        q = (hidden_states @ w_q).reshape(b, s, NH, HD).transpose(0, 2, 1, 3)
        k = (hidden_states @ w_k).reshape(b, s, NKV, HD).transpose(0, 2, 1, 3)
        v = (hidden_states @ w_v).reshape(b, s, NKV, HD).transpose(0, 2, 1, 3)
        cos, sin = _rope_cos_sin(s, dt)
        q = q * cos + _rotate_half(q) * sin
        k = k * cos + _rotate_half(k) * sin
        rep = NH // NKV
        k = jnp.repeat(k, rep, axis=1)
        v = jnp.repeat(v, rep, axis=1)
        qpos = jnp.arange(s) + (s - s)
        kpos = jnp.arange(s)
        dist = qpos[:, None] - kpos[None, :]
        bad = (dist < 0) | (dist > WIN)
        bias = jnp.where(bad, jnp.finfo(dt).min, jnp.zeros((), dt))[None, None]
        scores = jnp.einsum('bhqd,bhkd->bhqk', q, k) / jnp.sqrt(jnp.asarray(HD, dt))
        probs = jax.nn.softmax(scores + bias, axis=-1)
        out = jnp.einsum('bhqk,bhkd->bhqd', probs, v)
        out = out.transpose(0, 2, 1, 3).reshape(b, s, NH * HD)
        return out @ w_o

    def _L0_ffn_ref(x, select_weight, select_mean_diff, imp_center, imp_slope, lora_update, lora_degen, bias_w, debias_w):
        import jax, jax.numpy as jnp
        import numpy as np
        B, T, D = (4, 256, 512)
        N, S, H = (8, 8, 8)
        ETA = 1.0
        x_diff = x[:, None, :, :] - select_mean_diff[None, :, None, :]
        x_diff = x_diff / jnp.linalg.norm(x_diff, axis=3, keepdims=True)
        cont = jnp.einsum('nds,bntd->bnts', select_weight, x_diff) ** 2
        score = cont.sum(axis=-1)
        gate = jax.nn.sigmoid(imp_slope[None, :, None] * (score - imp_center[None, :, None]))
        sel_scale = gate.max(axis=1)[..., None]
        sel_idx = gate.argmax(axis=1)
        debias = jnp.take(debias_w, sel_idx, axis=0)
        bias = jnp.take(bias_w, sel_idx, axis=0)
        upd = jnp.take(lora_update, sel_idx, axis=0)
        dgn = jnp.take(lora_degen, sel_idx, axis=0)
        x_debias = x - debias
        mod_x = jnp.einsum('btdh,btd->bth', upd, x_debias)
        degen_up = jnp.einsum('btdh,bth->btd', dgn, mod_x)
        mod_x_bias = ETA * (bias + degen_up)
        return (1.0 - sel_scale) * x + sel_scale * mod_x_bias
    h = _L0_tok_ref(x, L0_tok_log_dt, L0_tok_log_w_real, L0_tok_w_imag, 512)
    h = h + _L0_attn_ref(_layernorm(h, axis=-1), L0_attn_w_q, L0_attn_w_k, L0_attn_w_v, L0_attn_w_o)
    h = h + _L0_ffn_ref(_layernorm(h, axis=-1), L0_ffn_select_weight, L0_ffn_select_mean_diff, L0_ffn_imp_center, L0_ffn_imp_slope, L0_ffn_lora_update, L0_ffn_lora_degen, L0_ffn_bias_w, L0_ffn_debias_w)
    return h

_drawn_inputs = setup_inputs


def setup_inputs(seed=0):
    import zlib

    import numpy as np

    out = dict(_drawn_inputs(seed))
    spreads = {'L0_tok_log_w_real': (-0.6931471824645996, 0.2)}
    factors = {'L0_ffn_debias_w': 8.0}
    for name, (base, spread) in spreads.items():
        noise = np.random.default_rng([zlib.crc32(name.encode()), seed]).standard_normal(out[name].shape)
        drawn = base * np.exp(spread * noise) if base else spread * noise
        out[name] = jnp.asarray(drawn.astype(out[name].dtype))
    for name, factor in factors.items():
        out[name] = (out[name] * factor).astype(out[name].dtype)
    return out
```

```python
from contextlib import ExitStack

import numpy as np
import concourse.bass as bass
from concourse import mybir

F32 = mybir.dt.float32
F32R = mybir.dt.float32r
I32 = mybir.dt.int32
ALU = mybir.AluOpType
ACT = mybir.ActivationFunctionType
AX = mybir.AxisListType

P = 128
NB = 8
S = 256
D = 512
NS = 64
NH, NKV, HD = 16, 4, 128
NG = NKV
QH = NH // NKV
KC = D // P
TT = S // P
WC = HD + HD + QH * HD
NE, SE, HE = 8, 8, 8
FC = NE * SE + NE + NE * HE
MC = NE * HE + NE
LA, LB1, LB2 = 8, 8, 8
NL = LA + LB1 + LB2
CH = 16
NCH = S // CH
EPS = 1e-5
SCALE = float(HD) ** -0.5
MASKED = -1e30
ROUND = 1.5 * 2.0 ** 23

C_COS, C_SIN, C_MASK, C_ID, C_L, C_RANK, C_ONES, C_QUARTER, C_POW = 0, 256, 512, 768, 896, 920, 928, 1056, 1057
C_ALL = 1059


def constants():
    inv = (1.0 / 10000.0 ** (np.arange(0, HD, 2) / HD)).astype(np.float32)
    ang = (np.arange(S, dtype=np.float32)[None, :] * np.concatenate([inv, inv])[:, None]).astype(np.float32)
    c = np.zeros((P, C_ALL), np.float32)
    c[:, C_COS:C_COS + S] = np.cos(ang.astype(np.float64))
    sign = np.where(np.arange(HD) < HD // 2, -1.0, 1.0)[:, None]
    c[:, C_SIN:C_SIN + S] = sign * np.sin(ang.astype(np.float64))
    q, k = np.arange(P)[:, None], np.arange(P)[None, :]
    c[:, C_MASK + P:C_MASK + 2 * P] = np.where(k <= q, 0.0, MASKED)
    c[:, C_ID:C_ID + P] = np.eye(P)
    c[:, C_L:C_L + NL] = np.concatenate([np.arange(8), 8 * np.arange(8), 64 * np.arange(8)])[None, :]
    c[:, C_RANK:C_RANK + NE] = (NE - np.arange(NE))[None, :]
    c[:, C_ONES:C_ONES + P] = 1.0
    c[:, C_QUARTER] = np.pi / 2
    c[:, C_POW:C_POW + TT] = -0.5
    return c


NCK = KC + QH

CH_RHO, CH_TURN, CH_ABS = 16, 21, 43
GATE, GATE_Z = 15, 7


def rope_view(j):
    if j == 0:
        return (lambda t: t[:, 0, :]), (lambda c: c), (lambda t: t[:, 0, :]), (lambda t: t[:, 0:S])
    h = slice(2 * j - 1, 2 * j + 1)
    return ((lambda t: t[:, h, :]), (lambda c: c.unsqueeze(1).to_broadcast([P, 2, S])), (lambda t: t[:, h, P:S]),
            (lambda t: t[:, j * S:(j + 1) * S].rearrange("p (h q) -> p h q", h=2)))


RUNS = [
    [(0, 1), (1, 2), (2, 5), (5, 6), (6, 7), (7, 8)],
    [(0, 1), (1, 6), (6, 7), (7, 8)],
    [(0, 1), (1, 6), (6, 7), (7, 8)],
    [(0, 1), (1, 2), (2, 3), (3, 7), (7, 8)],
]


def steps(engine, body):
    for g in range(NG):
        for lo, hi in RUNS[g]:
            if hi - lo == 1:
                body(g, lo, lo)
            else:
                with engine.Fori(lo, hi) as b:
                    body(g, b, lo)


def needs_xt(g, at):
    return g == 0 and at <= 5


def needs_norm1(g, at):
    return g == 0 and at <= 4


def needs_ffn(g, at):
    return g == NG - 1 and at >= 2


def needs_norm2(g, at):
    return g == NG - 1 and at >= 1


def needs_finish(g, at):
    return g == NG - 1 and at >= 3


def tower(nc, mix_c, mix_s, log_dt, log_wr, w_im, w_qkv, w_o, w_gate, w_gmul, w_upd, centers, slopes, consts, out):
    x_dram = nc.dram_tensor("mixed", [S, NB, D], F32, kind="Internal").ap()
    top = ExitStack()
    with top:
        def sem(name):
            return top.enter_context(nc.semaphore(name))

        def sb(name, shape, dt=F32, stack=top):
            return stack.enter_context(nc.sbuf_tensor(name, shape, dt))

        banks = [top.enter_context(nc.psum_tensor(f"bank{k}", [P, 512], F32)) for k in range(8)]

        x = sb("x", [P, TT, NB, D])
        wk = sb("w_hi", [P, KC, WC], F32R)
        wl = sb("w_lo", [P, KC, WC], F32R)
        raw = sb("raw", [P, 2, WC])
        cst = sb("cst", [P, C_ALL])
        cosT = cst[:, C_COS:C_COS + S]
        sinT = cst[:, C_SIN:C_SIN + S]
        mask = cst[:, C_MASK:C_MASK + 2 * P]
        ident = cst[:, C_ID:C_ID + P]
        ones = cst[:, C_ONES:C_ONES + P]
        fw = sb("fw", [P, KC, FC])
        dw = sb("dw", [MC, D])
        cw = sb("cw", [P, FC])
        dbs = sb("dbs", [P, KC, NE])
        spare = sb("spare", [1, 9])
        ctr = sb("ctr", [P, NE])
        slp = sb("slp", [P, NE])

        mixer = ExitStack()
        ta = [sb(f"ta{k}", [P, 8, S], F32, mixer) for k in range(6)]
        re1, im1, u2, v2, pre, pim = ta
        mc = sb("mc", [P, S, NB], F32, mixer)
        ms = sb("ms", [P, S, NB], F32, mixer)
        ang = sb("ang", [P, NL, P], F32, mixer)
        sn = sb("sn", [P, NL, P], F32, mixer)
        mag = sb("mag", [P, NL, P], F32, mixer)
        bt = [sb(f"bt{k}", [P, CH, 64], F32, mixer) for k in range(2)]
        g1 = [sb(f"g1{k}", [P, CH, 64], F32, mixer) for k in range(2)]
        g2 = [sb(f"g2{k}", [P, CH, 64], F32, mixer) for k in range(2)]
        tmp = sb("tmp", [P, CH, 64], F32, mixer)
        st = [sb(f"st{k}", [P, CH // 2, 64], F32, mixer) for k in range(2)]
        mixer.close()

        small = ExitStack()
        hold = [sb(f"hold{k}", [P, 8, S], F32, small) for k in range(6)]
        hold += [sb(f"holdm{k}", [P, S, NB], F32, small) for k in range(2)]
        hold += [sb(f"holdn{k}", [P, NL, P], F32, small) for k in range(3)]
        lg = sb("lg", [P, 2, P], F32, small)
        ex = sb("ex", [P, 2, P], F32, small)
        kk = sb("kk", [P, 2, P], F32, small)
        rr = sb("rr", [P, 2, P], F32, small)
        qq = sb("qq", [P, 2, P], F32, small)
        ki = sb("ki", [P, 2, P], I32, small)
        wim = sb("wim", [P, P], F32, small)
        rho = sb("rho", [P, P], F32, small)
        turn = sb("turn", [P, P], F32, small)
        em1 = sb("em1", [P, P], F32, small)
        half = sb("half", [P, P], F32, small)
        ar = sb("ar", [P, P], F32, small)
        ai = sb("ai", [P, P], F32, small)
        dr = sb("dr", [P, P], F32, small)
        di = sb("di", [P, P], F32, small)
        nrm = sb("nrm", [P, P], F32, small)
        t0 = sb("t0", [P, P], F32, small)
        neg2 = sb("neg2", [P, 8, P], F32, small)
        pt2 = sb("pt2", [P, 8, P], F32, small)
        small.close()

        xt_h = sb("xt_hi", [P, NB, KC, S], F32R)
        xt_l = sb("xt_lo", [P, NB, KC, S], F32R)
        woh = sb("wo_hi", [P, QH, D], F32R)
        wol = sb("wo_lo", [P, QH, D], F32R)
        kq = sb("kq", [P, 1 + QH, S])
        kh = sb("kq_hi", [P, S + QH * P], F32R)
        kl = sb("kq_lo", [P, S + QH * P], F32R)
        sw = sb("swap", [P, 1 + QH, S])
        sm = sb("sm", [P, QH, 3 * P])
        pth = sb("pt_hi", [P, 3, 512], F32R)
        ptl = sb("pt_lo", [P, 3, 512], F32R)
        vt = sb("vt", [P, S])
        vh = sb("v_hi", [P, TT, HD], F32R)
        vl = sb("v_lo", [P, TT, HD], F32R)
        oth = sb("ot_hi", [P, QH, S], F32R)
        otl = sb("ot_lo", [P, QH, S], F32R)
        norm_mem = sb("norm_mem", [P, 2 * TT * D])
        xn = norm_mem[:, 0:TT * D].rearrange("p (t d) -> p t d", t=TT)
        xnt = norm_mem[:, TT * D:2 * TT * D].rearrange("p (k s) -> p k s", k=KC)
        stats = sb("stats", [P, TT, 6])
        mv = sb("mv", [P, TT, 2])
        rstd = sb("rstd", [P, TT])
        mx = sb("mx", [P, 2 * QH])
        rsum = sb("rsum", [P, 2 * QH])
        rinv = sb("rinv", [P, 2 * QH])
        gu = sb("gu", [P, TT, NE * SE])
        gm = sb("gm", [P, TT, NE * HE])
        mm = sb("mm", [P, TT, MC])
        mt = sb("mt", [MC, S])
        gs = [sb(f"gs{k}", [P, TT, NE]) for k in range(3)]
        g1x = [sb(f"gx{k}", [P, TT]) for k in range(4)]

        pw = x[:, TT - 1, NB - KC:NB, 0:FC]

        def raw_slot(n):
            if n < NCK:
                return n % 2
            return (n - NCK) % 4

        def raw_chunk(n):
            width = WC if n % NCK < KC else D
            k = raw_slot(n)
            return raw[:, k, 0:width] if k < 2 else norm_mem[:, (k - 2) * WC:(k - 2) * WC + width]

        def raw_turn(n):
            return sum(raw_slot(m) == raw_slot(n) for m in range(n + 1))

        cst_in, par_in, mix_in, gate_in = sem("cst_in"), sem("par_in"), sem("mix_in"), sem("gate_in")
        raw_in = [sem(f"raw_in{k}") for k in range(4)]
        w_hi, w_lo = sem("w_hi_done"), sem("w_lo_done")
        chain = sem("dve_chain")
        act_tab, tab_ready, tab_in, p_ready, p_in = (
            sem("act_tables"), sem("tables_ready"), sem("tables_in"), sem("p_ready"), sem("p_in"))
        pool_tab = sem("pool_tables")
        t2_done = sem("t2_done")
        t1_done = sem("t1_done")
        b_ready, g2_ready, mixed, evac, xd_out, x_in = (
            sem("b_ready"), sem("g2_ready"), sem("mixed_ready"), sem("evacuated"), [sem("xd_out0"), sem("xd_out1")],
            sem("x_in"))
        pw_done, cw_mm, cw_done = sem("pw_done"), sem("cw_mm"), sem("cw_done")
        ln_st, ln_var, ln_pool, ln_rstd, xn_ready = (
            sem("ln_stats"), sem("ln_var"), sem("ln_pool"), sem("ln_rstd"), sem("xn_ready"))
        xt_ready, xt_hi, xt_lo = sem("xt_ready"), sem("xt_hi_done"), sem("xt_lo_done")
        proj, swapped, kq_cos, rot_sin, kq_rot, kq_hi, kq_lo = (
            sem("proj_ready"), sem("swapped"), sem("kq_cos"), sem("rot_sin"), sem("kq_rotated"), sem("kq_hi_done"),
            sem("kq_lo_done"))
        s_ready, s_masked, p_exp, r_ready, p_norm = (
            sem("scores_ready"), sem("scores_masked"), sem("p_exp"), sem("rinv_ready"), sem("p_norm"))
        tr_ready, pt_hi, pt_lo = sem("tr_ready"), sem("pt_hi_done"), sem("pt_lo_done")
        vt_ready, v_hi, v_lo = sem("vt_ready"), sem("v_hi_done"), sem("v_lo_done")
        pv_ready, ot_hi, ot_lo = sem("pv_ready"), sem("ot_hi_done"), sem("ot_lo_done")
        o_ready, x_added = sem("o_ready"), sem("x_added")
        f_ready, f_read, gate, e_ready, m_ready = (
            sem("f_ready"), sem("f_read"), sem("gate_chain"), sem("gate_exp"), sem("m_ready"))
        xn_scaled, xn_added = sem("xn_scaled"), sem("xn_added")
        mt_ready, mt_done, d_ready, out_ready, stored = (
            sem("mt_ready"), sem("mt_done"), sem("d_ready"), sem("out_ready"), sem("stored"))

        block = top.enter_context(nc.Block())

        def wait_apart(engine, signal, value, slot):
            engine.wait_ge(signal, value)
            if signal in (ln_var, r_ready, gate):
                nc.gpsimd.tensor_tensor(spare[:, slot:slot + 1], cst[0:1, 0:1], cst[0:1, 0:1], ALU.add)
            else:
                nc.vector.tensor_copy(spare[:, slot:slot + 1], cst[0:1, 0:1])

        @block.sync
        def _(sp):
            sp.dma_start(cst[:], consts).then_inc(cst_in, 16)
            for hh in range(2):
                sp.dma_start(lg[hh * NS:(hh + 1) * NS, 0, :],
                             log_dt[hh * P:(hh + 1) * P].unsqueeze(0).to_broadcast([NS, P])).then_inc(par_in, 16)
            sp.dma_start(lg[:, 1, :], log_wr).then_inc(par_in, 16)
            sp.dma_start(wim[:], w_im).then_inc(par_in, 16)

            def load_raw(n):
                g, k = divmod(n, NCK)
                before = [m for m in range(n) if raw_slot(m) == raw_slot(n)]
                if before:
                    sp.wait_ge(w_lo, before[-1] + 1)
                elif n >= NCK:
                    sp.wait_ge(xt_ready, 2 * NB)
                src = w_qkv[g, k] if k < KC else w_o[g, k - KC]
                sp.dma_start(raw_chunk(n), src).then_inc(raw_in[raw_slot(n)], 16)

            load_raw(0)
            load_raw(1)
            sp.dma_start(mc[:], mix_c).then_inc(mix_in, 16)
            sp.dma_start(ms[:], mix_s).then_inc(mix_in, 16)
            sp.dma_start(fw[:], w_gate).then_inc(gate_in, 16)
            sp.dma_start(dw[:], w_upd).then_inc(gate_in, 16)
            sp.dma_start(dbs[:], w_gmul).then_inc(gate_in, 16)
            sp.dma_start(ctr[:], centers.unsqueeze(0).to_broadcast([P, NE])).then_inc(gate_in, 16)
            sp.dma_start(slp[:], slopes.unsqueeze(0).to_broadcast([P, NE])).then_inc(gate_in, 16)
            load_raw(2)
            load_raw(3)

            def spread(dst, src, e0, halves, signal):
                for ri in halves:
                    for hh in range(2):
                        sp.dma_start(dst[ri * NS:(ri + 1) * NS, :, hh * P:(hh + 1) * P],
                                     src[hh * NS:(hh + 1) * NS, e0:e0 + 8, :]).then_inc(signal, 16)

            sp.wait_ge(tab_ready, 3)
            spread(re1, ang, 8, (0, 1), tab_in)
            spread(im1, sn, 8, (0, 1), tab_in)
            spread(u2, ang, 0, (0,), tab_in)
            spread(u2, sn, 0, (1,), tab_in)
            spread(v2, neg2, 0, (0,), tab_in)
            spread(v2, ang, 0, (1,), tab_in)
            sp.wait_ge(p_ready, 3)
            spread(pre, mag, 16, (0,), p_in)
            spread(pre, ang, 16, (1,), p_in)
            spread(pim, sn, 16, (0, 1), p_in)

            with sp.Fori(0, NCH // 2) as it:
                for s in range(2):
                    sp.wait_ge(evac, it * 2 + (s + 1))
                    for h2 in range(2):
                        rows = x_dram.rearrange("(q m t) c (a j) -> q t (c a) m j", m=CH // 2, t=2, j=64)
                        sp.dma_start(rows[it * 2 + s, h2], st[s][h2 * 64:(h2 + 1) * 64, :, :]).then_inc(xd_out[s], 16)
            for s in range(2):
                sp.wait_ge(xd_out[s], 16 * NCH)
            sp.wait_ge(cw_mm, 1)
            for t in range(TT):
                sp.dma_start(x[:, t, :, :], x_dram[t * P:(t + 1) * P]).then_inc(x_in, 16)

            for n in range(4, NCK * NG):
                load_raw(n)
            with sp.Fori(0, NB) as bb:
                for t in range(TT):
                    sp.wait_ge(out_ready, bb * 2 + (t + 1))
                    sp.dma_start(out[bb, t * P:(t + 1) * P, :], x[:, t, bb, :]).then_inc(stored, 16)
            sp.wait_ge(stored, 16 * NB * TT)

        @block.gpsimd
        def _(pool):
            def split_lo(n):
                k = n % NCK
                pool.wait_ge(w_hi, n + 1)
                if k < KC:
                    hi, lo = wk[:, k, :], wl[:, k, :]
                else:
                    hi, lo = woh[:, k - KC, :], wol[:, k - KC, :]
                nc.gpsimd.tensor_tensor(lo, raw_chunk(n), hi.bitcast(F32), ALU.subtract).then_inc(w_lo, 1)

            for n in range(2):
                split_lo(n)
            pool.wait_ge(chain, CH_RHO)
            nc.gpsimd.tensor_tensor(mag[:], rho[:].unsqueeze(1).to_broadcast([P, NL, P]),
                                    cst[:, C_L:C_L + NL].unsqueeze(2).to_broadcast([P, NL, P]),
                                    ALU.mult).then_inc(pool_tab, 1)
            for n in range(2, KC):
                split_lo(n)

            pool.wait_ge(p_in, 16 * 8)
            pool.wait_ge(mix_in, 32)
            def chunk(it, s):
                hs = bass.ds(it * (2 * CH) + s * CH, CH)
                nc.gpsimd.tensor_tensor(
                    g2[s][:].rearrange("p h (c a) -> p h c a", c=NB),
                    ms[:, hs, :].unsqueeze(3).to_broadcast([P, CH, NB, LA]),
                    pim[:, :, hs].rearrange("p a h -> p h a").unsqueeze(2).to_broadcast([P, CH, NB, LA]),
                    ALU.mult).then_inc(g2_ready, 1)

            for s in range(2):
                chunk(0, s)
            with pool.Fori(1, NCH // 2) as it:
                for s in range(2):
                    pool.wait_ge(mixed, it * 4 + (2 * s - 2))
                    chunk(it, s)

            pool.wait_ge(x_in, 32)

            def norm(m):
                wait_apart(pool, ln_var, m + 1, 8)
                nc.gpsimd.tensor_scalar(rstd[:], mv[:, :, 1], EPS, 1.0, ALU.add, ALU.mult).then_inc(ln_pool, 1)
                pool.wait_ge(ln_pool, m + 1)
                nc.gpsimd.tensor_tensor(rstd[:], rstd[:], cst[:, C_POW:C_POW + TT], ALU.pow).then_inc(ln_rstd, 1)

            def rotate(s):
                for j in range(3):
                    view, table, _, _ = rope_view(j)
                    pool.wait_ge(swapped, s * 3 + (j + 1))
                    nc.gpsimd.tensor_tensor(view(sw), view(sw), table(sinT), ALU.mult).then_inc(rot_sin, 1)
                for j in range(3):
                    _, _, part, flat = rope_view(j)
                    pool.wait_ge(kq_hi, s * 3 + (j + 1))
                    nc.gpsimd.tensor_tensor(flat(kl), part(kq), flat(kh).bitcast(F32), ALU.subtract).then_inc(kq_lo, 1)

            for m in range(3):
                norm(m)
            rotate(0)

            def add_normed(bb):
                wait_apart(pool, gate, bb * GATE + GATE, 8)
                for t in range(TT):
                    nc.gpsimd.tensor_scalar(xn[:, t, :], xn[:, t, :], g1x[0][:, t:t + 1], 1.0, ALU.mult,
                                            ALU.mult).then_inc(xn_scaled, 1)
                for t in range(TT):
                    pool.wait_ge(xn_scaled, bb * 2 + (t + 1))
                    nc.gpsimd.tensor_tensor(x[:, t, bb, :], x[:, t, bb, :], xn[:, t, :], ALU.add).then_inc(xn_added, 1)

            def step(g, b, at):
                i = b + 8 * g
                if needs_norm1(g, at):
                    norm(b + 3)
                for j in range(QH):
                    if j % 2 == 0:
                        wait_apart(pool, r_ready, i * 2 + (j // 2 + 1), 6 + j // 2)
                    for t, cols in ((0, slice(0, P)), (1, slice(P, 3 * P))):
                        last = nc.gpsimd.tensor_scalar(sm[:, j, cols], sm[:, j, cols], rinv[:, 2 * j + t:2 * j + t + 1],
                                                       1.0, ALU.mult, ALU.mult)
                    last.then_inc(p_norm, 1)
                if not (g == NG - 1 and at == NB - 1):
                    rotate(i + 1)
                if needs_ffn(g, at):
                    add_normed(b - 2)
                if needs_norm2(g, at):
                    norm(b + (NB - 1))
                if g < NG - 1 and at == NB - 2:
                    for k in range(KC):
                        split_lo((g + 1) * NCK + k)
                if at == 0:
                    for k in range(KC, NCK):
                        split_lo(g * NCK + k)

            steps(pool, step)
            add_normed(NB - 2)
            norm(2 * NB - 1)
            add_normed(NB - 1)

        @block.scalar
        def _(act):
            def split_hi(n):
                k = n % NCK
                act.wait_ge(raw_in[raw_slot(n)], 16 * raw_turn(n))
                dst = wk[:, k, :] if k < KC else woh[:, k - KC, :]
                nc.scalar.activation(dst, raw_chunk(n), ACT.Copy).then_inc(w_hi, 1)

            for n in range(2):
                split_hi(n)
            TWO_PI = 6.283185
            act.wait_ge(chain, CH_TURN)
            nc.scalar.activation(sn[:], ang[:], ACT.Sin, scale=TWO_PI).then_inc(act_tab, 1)
            nc.scalar.activation(half[:], ang[:, 1, :], ACT.Sin, scale=TWO_PI / 2).then_inc(act_tab, 1)
            act.wait_ge(chain, CH_ABS)
            nc.scalar.activation(ang[:], ang[:], ACT.Sin, scale=-TWO_PI, bias=cst[:, C_QUARTER:C_QUARTER + 1]).then_inc(act_tab, 1)
            act.wait_ge(pool_tab, 1)
            nc.scalar.activation(mag[:], mag[:], ACT.Exp).then_inc(act_tab, 1)
            for n in range(2, KC):
                split_hi(n)

            def evacuate(it, s):
                for q in range(2):
                    act.wait_ge(mixed, it * 4 + (s * 2 + q + 1))
                    for h2 in range(2):
                        rows = slice(h2 * 64, h2 * 64 + 64)
                        src = banks[2 * s + q][rows, :].rearrange("p (m t j) -> p m t j", t=2, j=64)[:, :, h2, :]
                        last = nc.scalar.activation(st[s][rows, q * 4:q * 4 + 4, :], src, ACT.Copy)
                last.then_inc(evac, 1)

            act.wait_ge(cw_mm, 1)
            nc.scalar.activation(cw[:], banks[7][:, 0:FC], ACT.Copy).then_inc(cw_done, 1)
            for s in range(2):
                evacuate(0, s)
            with act.Fori(1, NCH // 2) as it:
                for s in range(2):
                    act.wait_ge(xd_out[s], it * 32)
                    evacuate(it, s)

            def xt1(b):
                for q in range(2):
                    act.wait_ge(xt_ready, b * 2 + (q + 1))
                    nc.scalar.activation(xt_h[:, b, 2 * q:2 * q + 2, :].rearrange("p k s -> p (k s)"),
                                         banks[5 + q][:], ACT.Copy).then_inc(xt_hi, 1)

            def xt2(bb):
                for q in range(2):
                    act.wait_ge(xt_ready, bb * 2 + (2 * NB + q + 1))
                    nc.scalar.activation(xnt[:, 2 * q:2 * q + 2, :].rearrange("p k s -> p (k s)"),
                                         banks[5 + q][:], ACT.Copy).then_inc(xt_hi, 1)

            def swap(s, parts=range(3)):
                for j in parts:
                    view, _, _, _ = rope_view(j)
                    act.wait_ge(proj, s * 3 + (j + 1))
                    if j == 0 and (not isinstance(s, int) or s):
                        act.wait_ge(kq_rot, s * 3)
                        act.wait_ge(vt_ready, s)
                    src = banks[j][:, 0:S] if j == 0 else banks[j][:].rearrange("p (h s) -> p h s", h=2)
                    nc.scalar.activation(view(sw)[0:64], src[64:128], ACT.Copy)
                    last = nc.scalar.activation(view(sw)[64:128], src[0:64], ACT.Copy)
                    if j == 0:
                        last = nc.scalar.activation(vt[:], banks[0][:, S:2 * S], ACT.Copy)
                    last.then_inc(swapped, 1)

            def round_kq(s):
                for j in range(3):
                    _, _, part, flat = rope_view(j)
                    act.wait_ge(kq_rot, s * 3 + (j + 1))
                    if j == 0 and (not isinstance(s, int) or s):
                        act.wait_ge(s_ready, s * 4)
                    nc.scalar.activation(flat(kh), part(kq), ACT.Copy).then_inc(kq_hi, 1)

            def round_v(s):
                act.wait_ge(vt_ready, s + 1)
                nc.scalar.activation(vh[:].rearrange("p t d -> p (t d)"), banks[2][:, 0:S], ACT.Copy).then_inc(v_hi, 1)

            act.wait_ge(x_in, 32)
            for b in range(2):
                xt1(b)
            swap(0)
            round_kq(0)
            round_v(0)

            def gate_exp(bb):
                act.wait_ge(gate, bb * GATE + GATE_Z)
                nc.scalar.activation(gs[1][:], gs[1][:], ACT.Exp, scale=-1.0).then_inc(e_ready, 1)

            def mt_evac(bb):
                act.wait_ge(mt_ready, bb + 1)
                nc.scalar.activation(mt[:], banks[7][0:MC, 0:S], ACT.Copy).then_inc(mt_done, 1)

            def step(g, b, at):
                i = b + 8 * g
                for j in range(QH):
                    act.wait_ge(s_masked, i * 4 + (j + 1))
                    for t, cols in ((0, slice(0, P)), (1, slice(P, 3 * P))):
                        n = 2 * j + t
                        last = nc.scalar.activation(sm[:, j, cols], sm[:, j, cols], ACT.Exp, scale=-1.0,
                                                    bias=mx[:, n:n + 1], accum_out=rsum[:, n:n + 1])
                    last.then_inc(p_exp, 1)
                final = g == NG - 1 and at == NB - 1
                if needs_xt(g, at):
                    xt1(b + 2)
                if not final:
                    swap(i + 1, range(2))
                if needs_ffn(g, at):
                    xt2(b - 2)
                if not final:
                    swap(i + 1, (2,))
                for j in range(3):
                    act.wait_ge(tr_ready, i * 3 + (j + 1))
                    nc.scalar.activation(pth[:, j, :], banks[5 + j][:], ACT.Copy).then_inc(pt_hi, 1)
                if not final:
                    round_kq(i + 1)
                if g < NG - 1 and at == NB - 2:
                    act.wait_ge(proj, (8 * (g + 1)) * 3)
                    for k in range(KC):
                        split_hi((g + 1) * NCK + k)
                if at == 0:
                    if g > 0:
                        act.wait_ge(o_ready, 8 * g * 2)
                    for k in range(KC, NCK):
                        split_hi(g * NCK + k)
                if needs_ffn(g, at):
                    gate_exp(b - 2)
                for j in range(2):
                    act.wait_ge(pv_ready, i * 2 + (j + 1))
                    nc.scalar.activation(oth[:, 2 * j:2 * j + 2, :].rearrange("p h s -> p (h s)"),
                                         banks[j][:], ACT.Copy).then_inc(ot_hi, 1)
                if not final:
                    round_v(i + 1)
                if needs_ffn(g, at):
                    mt_evac(b - 2)

            steps(act, step)
            for bb in (NB - 2, NB - 1):
                xt2(bb)
                gate_exp(bb)
                mt_evac(bb)

        @block.vector
        def _(dve):
            links = [0]

            def link(ins):
                links[0] += 1
                ins.then_inc(chain, 1)
                dve.wait_ge(chain, links[0])

            v = nc.vector

            def expm1_parts(xin, n):
                k, r, q, p2 = (t[:].rearrange("p a b -> p (a b)")[:, 0:n] for t in (kk, rr, qq, ki))
                link(v.tensor_scalar(xin, xin, -87.0, 88.0, ALU.max, ALU.min))
                link(v.tensor_scalar(k, xin, 1.4426950408889634, ROUND, ALU.mult, ALU.add))
                link(v.tensor_scalar(k, k, ROUND, None, ALU.subtract))
                link(v.scalar_tensor_tensor(r, k, -0.693359375, xin, ALU.mult, ALU.add))
                link(v.scalar_tensor_tensor(r, k, 2.12194440e-4, r, ALU.mult, ALU.add))
                link(v.tensor_scalar(q, r, 1.0 / 5040, None, ALU.mult))
                for c in (1.0 / 720, 1.0 / 120, 1.0 / 24, 1.0 / 6, 0.5, 1.0):
                    link(v.scalar_tensor_tensor(q, q, c, r, ALU.add, ALU.mult))
                link(v.tensor_scalar(p2, k, 127.0, 8388608.0, ALU.add, ALU.mult))
                return q, p2.bitcast(F32)

            dve.wait_ge(par_in, 64)
            dve.wait_ge(cst_in, 16)
            flat = lg[:].rearrange("p a b -> p (a b)")
            q, p2 = expm1_parts(flat, 2 * P)
            exf = ex[:].rearrange("p a b -> p (a b)")
            link(v.tensor_tensor(exf, q, p2, ALU.mult))
            link(v.tensor_tensor(exf, exf, p2, ALU.add))
            dt, mw = ex[:, 0, :], ex[:, 1, :]
            link(v.scalar_tensor_tensor(rho[:], mw, -1.0, dt, ALU.mult, ALU.mult))
            assert links[0] == CH_RHO, links
            link(v.tensor_tensor(turn[:], wim[:], dt, ALU.mult))
            link(v.tensor_scalar(turn[:], turn[:], 0.15915494309189535, None, ALU.mult))
            link(v.tensor_tensor(ang[:], turn[:].unsqueeze(1).to_broadcast([P, NL, P]),
                                 cst[:, C_L:C_L + NL].unsqueeze(2).to_broadcast([P, NL, P]), ALU.mult))
            link(v.tensor_scalar(sn[:], ang[:], ROUND, ROUND, ALU.add, ALU.subtract))
            link(v.tensor_tensor(ang[:], ang[:], sn[:], ALU.subtract))
            assert links[0] == CH_TURN, links
            link(v.tensor_copy(t0[:], rho[:]))
            q, p2 = expm1_parts(t0[:], P)
            link(v.tensor_tensor(em1[:], q, p2, ALU.mult))
            link(v.scalar_tensor_tensor(em1[:], p2, -1.0, em1[:], ALU.add, ALU.add))
            link(v.tensor_tensor(nrm[:], mw, mw, ALU.mult))
            link(v.tensor_tensor(t0[:], wim[:], wim[:], ALU.mult))
            link(v.tensor_tensor(nrm[:], nrm[:], t0[:], ALU.add))
            link(v.reciprocal(nrm[:], nrm[:]))
            link(v.tensor_scalar(nrm[:], nrm[:], 2.0, None, ALU.mult))
            dve.wait_ge(act_tab, 2)
            link(v.scalar_tensor_tensor(ang[:], ang[:], -1.0, ang[:], ALU.mult, ALU.max))
            assert links[0] == CH_ABS, links
            link(v.tensor_tensor(t0[:], half[:], half[:], ALU.mult))
            link(v.scalar_tensor_tensor(ai[:], em1[:], 1.0, sn[:, 1, :], ALU.add, ALU.mult))
            dve.wait_ge(act_tab, 3)
            link(v.tensor_tensor(ar[:], em1[:], ang[:, 1, :], ALU.mult))
            link(v.scalar_tensor_tensor(ar[:], t0[:], -2.0, ar[:], ALU.mult, ALU.add))
            link(v.tensor_tensor(dr[:], ai[:], wim[:], ALU.mult))
            link(v.tensor_tensor(t0[:], ar[:], mw, ALU.mult))
            link(v.tensor_tensor(dr[:], dr[:], t0[:], ALU.subtract))
            link(v.tensor_tensor(dr[:], dr[:], nrm[:], ALU.mult))
            link(v.tensor_tensor(di[:], ai[:], mw, ALU.mult))
            link(v.tensor_tensor(t0[:], ar[:], wim[:], ALU.mult))
            link(v.tensor_tensor(di[:], di[:], t0[:], ALU.add))
            link(v.scalar_tensor_tensor(di[:], di[:], -1.0, nrm[:], ALU.mult, ALU.mult))
            dve.wait_ge(act_tab, 4)
            lb = slice(0, LB1 + LB2)
            v.tensor_tensor(ang[:, lb, :], ang[:, lb, :], mag[:, lb, :], ALU.mult).then_inc(tab_ready, 1)
            v.tensor_tensor(sn[:, lb, :], sn[:, lb, :], mag[:, lb, :], ALU.mult).then_inc(tab_ready, 1)
            dve.wait_ge(tab_ready, 2)
            v.tensor_scalar(neg2[:], sn[:, 0:8, :], -1.0, None, ALU.mult).then_inc(tab_ready, 1)
            la = slice(LB1 + LB2, NL)
            drb = dr[:].unsqueeze(1).to_broadcast([P, LA, P])
            dib = di[:].unsqueeze(1).to_broadcast([P, LA, P])
            link(v.tensor_tensor(ang[:, la, :], ang[:, la, :], mag[:, la, :], ALU.mult))
            link(v.tensor_tensor(sn[:, la, :], sn[:, la, :], mag[:, la, :], ALU.mult))
            link(v.tensor_tensor(mag[:, la, :], ang[:, la, :], drb, ALU.mult))
            link(v.tensor_tensor(pt2[:], sn[:, la, :], dib, ALU.mult))
            v.tensor_tensor(mag[:, la, :], mag[:, la, :], pt2[:], ALU.subtract).then_inc(p_ready, 1)
            link(v.tensor_tensor(sn[:, la, :], sn[:, la, :], drb, ALU.mult))
            dve.wait_ge(p_ready, 1)
            link(v.tensor_tensor(pt2[:], ang[:, la, :], dib, ALU.mult))
            v.tensor_scalar(ang[:, la, :], mag[:, la, :], -1.0, None, ALU.mult).then_inc(p_ready, 1)
            v.scalar_tensor_tensor(sn[:, la, :].rearrange("p a h -> p (a h)"), sn[:, la, :].rearrange("p a h -> p (a h)"),
                                   -1.0, pt2[:].rearrange("p a h -> p (a h)"), ALU.mult, ALU.subtract).then_inc(p_ready, 1)

            dve.wait_ge(gate_in, 80)
            for k in range(KC):
                sel = fw[:, k, 0:NE * SE].rearrange("p (n s) -> p n s", n=NE)
                mean = fw[:, k, NE * SE:NE * SE + NE]
                upd = fw[:, k, NE * SE + NE:FC].rearrange("p (n h) -> p n h", n=NE)
                row = pw[:, k, 0:FC]
                v.tensor_tensor(row[:, 0:64].rearrange("p (n s) -> p n s", n=NE), sel,
                                mean.unsqueeze(2).to_broadcast([P, NE, SE]), ALU.mult)
                v.tensor_tensor(row[:, 64:72], mean, mean, ALU.mult)
                v.tensor_tensor(row[:, 72:FC].rearrange("p (n h) -> p n h", n=NE), upd,
                                dbs[:, k, :].unsqueeze(2).to_broadcast([P, NE, HE]), ALU.mult).then_inc(pw_done, 1)

            dve.wait_ge(tab_in, 16 * 16)
            dve.wait_ge(p_in, 16 * 8)
            dve.wait_ge(mix_in, 32)
            def chunk(it, s):
                hs = bass.ds(it * (2 * CH) + s * CH, CH)

                def outer(left, right):
                    return (left[:, :, hs].rearrange("p e h -> p h e").unsqueeze(3).to_broadcast([P, CH, LB1, LB2]),
                            right[:, :, hs].rearrange("p e h -> p h e").unsqueeze(2).to_broadcast([P, CH, LB1, LB2]))

                grid = lambda t: t[:].rearrange("p h (i j) -> p h i j", i=LB1)
                v.tensor_tensor(grid(bt[s]), *outer(re1, u2), ALU.mult)
                if not isinstance(it, int) or s:
                    dve.wait_ge(b_ready, it * 2 + s)
                v.tensor_tensor(grid(tmp), *outer(im1, v2), ALU.mult).then_inc(t2_done, 1)
                v.tensor_tensor(g1[s][:].rearrange("p h (c a) -> p h c a", c=NB),
                                mc[:, hs, :].unsqueeze(3).to_broadcast([P, CH, NB, LA]),
                                pre[:, :, hs].rearrange("p a h -> p h a").unsqueeze(2).to_broadcast([P, CH, NB, LA]),
                                ALU.mult)
                dve.wait_ge(t2_done, it * 2 + (s + 1))
                v.tensor_tensor(bt[s][:], bt[s][:], tmp[:], ALU.add).then_inc(b_ready, 1)

            for s in range(2):
                chunk(0, s)
            with dve.Fori(1, NCH // 2) as it:
                for s in range(2):
                    dve.wait_ge(mixed, it * 4 + (2 * s - 2))
                    chunk(it, s)

            dve.wait_ge(x_in, 32)
            def norm_stats(src, m):
                for t in range(TT):
                    v.bn_stats(stats[:, t, :], src(t)).then_inc(ln_st, 1)
                wait_apart(dve, ln_st, m * 2 + 2, 4)
                for t in range(TT):
                    last = v.bn_aggr(mv[:, t, :], stats[:, t, :])
                last.then_inc(ln_var, 1)

            def norm_apply(src, m, second=False):
                dve.wait_ge(ln_rstd, m + 1)
                if second:
                    if isinstance(m, int) and m == NB:
                        dve.wait_ge(w_lo, NCK * NG)
                    else:
                        dve.wait_ge(xn_added, m * 2 - 2 * NB)
                if not isinstance(m, int) or m:
                    dve.wait_ge(xt_ready, m * 2)
                for t in range(TT):
                    last = v.tensor_scalar(xn[:, t, :], src(t), mv[:, t, 0:1], rstd[:, t:t + 1], ALU.subtract, ALU.mult)
                last.then_inc(xn_ready, 1)

            def tokens(b):
                return lambda t: x[:, t, b, :]

            def xt_rest(b):
                for q in range(2):
                    dve.wait_ge(xt_hi, b * 2 + (q + 1))
                    v.tensor_tensor(xt_l[:, b, 2 * q:2 * q + 2, :].rearrange("p k s -> p (k s)"), banks[5 + q][:],
                                    xt_h[:, b, 2 * q:2 * q + 2, :].rearrange("p k s -> p (k s)").bitcast(F32),
                                    ALU.subtract).then_inc(xt_lo, 1)

            def rope(s, j):
                view, table, _, _ = rope_view(j)
                src = banks[j][:, 0:S] if j == 0 else banks[j][:].rearrange("p (h s) -> p h s", h=2)
                dve.wait_ge(swapped, s * 3 + (j + 1))
                v.tensor_tensor(view(kq), src, table(cosT), ALU.mult).then_inc(kq_cos, 1)

            def rope_add(s, j):
                view, _, _, _ = rope_view(j)
                dve.wait_ge(rot_sin, s * 3 + (j + 1))
                dve.wait_ge(kq_cos, s * 3 + (j + 1))
                v.tensor_tensor(view(kq), view(kq), view(sw), ALU.add).then_inc(kq_rot, 1)

            def v_rest(s):
                dve.wait_ge(v_hi, s + 1)
                v.tensor_tensor(vl[:].rearrange("p t d -> p (t d)"), banks[2][:, 0:S],
                                vh[:].rearrange("p t d -> p (t d)").bitcast(F32), ALU.subtract).then_inc(v_lo, 1)

            for b in range(3):
                norm_stats(tokens(b), b)
                norm_apply(tokens(b), b)
                if b < 2:
                    xt_rest(b)
            for j in range(3):
                rope(0, j)
                rope_add(0, j)

            def add_output(i, b):
                for t in range(TT):
                    dve.wait_ge(o_ready, i * 2 + (t + 1))
                    v.tensor_tensor(x[:, t, b, :], banks[3 + t][:], x[:, t, b, :], ALU.add).then_inc(x_added, 1)

            def gate_read(bb):
                f = banks[0][:].rearrange("p (t c) -> p t c", t=TT)
                dve.wait_ge(cw_done, 1)
                dve.wait_ge(f_ready, bb + 1)
                v.tensor_tensor(gu[:], f[:, :, 0:64], cw[:, 0:64].unsqueeze(1).to_broadcast([P, TT, 64]), ALU.subtract)
                v.scalar_tensor_tensor(gs[0][:], f[:, :, 64:72], -2.0, cw[:, 64:72].unsqueeze(1).to_broadcast([P, TT, NE]),
                                       ALU.mult, ALU.add)
                v.tensor_tensor(gm[:], f[:, :, 72:FC], cw[:, 72:FC].unsqueeze(1).to_broadcast([P, TT, 64]),
                                ALU.subtract).then_inc(f_read, 1)

            def gates(bb):
                n = [0]

                def then(ins):
                    n[0] += 1
                    ins.then_inc(gate, 1)
                    dve.wait_ge(gate, bb * GATE + n[0])

                score, z, rank = gs[0][:], gs[1][:], gs[2][:]
                one_minus, ssq, best, first = (t[:] for t in g1x)
                bc = lambda t: t.unsqueeze(2).to_broadcast([P, TT, NE])
                dve.wait_ge(f_read, bb + 1)
                v.tensor_tensor(gu[:], gu[:], gu[:], ALU.mult)
                then(v.tensor_tensor(ssq, rstd[:], rstd[:], ALU.mult))
                v.tensor_reduce(z, gu[:].rearrange("p t (n s) -> p t n s", n=NE), AX.X, ALU.add)
                then(v.scalar_tensor_tensor(ssq, mv[:, :, 1], float(D), ssq, ALU.mult, ALU.mult))
                then(v.tensor_tensor(score, score, bc(ssq), ALU.add))
                then(v.reciprocal(score, score))
                then(v.tensor_tensor(z, z, score, ALU.mult))
                then(v.tensor_tensor(z, z, ctr[:].unsqueeze(1).to_broadcast([P, TT, NE]), ALU.subtract))
                then(v.tensor_tensor(z, z, slp[:].unsqueeze(1).to_broadcast([P, TT, NE]), ALU.mult))
                assert n[0] == GATE_Z
                dve.wait_ge(e_ready, bb + 1)
                then(v.tensor_scalar(z, z, 1.0, None, ALU.add))
                then(v.reciprocal(z, z))
                then(v.tensor_reduce(best, z, AX.X, ALU.max))
                then(v.tensor_tensor(rank, z, bc(best), ALU.is_equal))
                then(v.tensor_tensor(rank, rank, cst[:, C_RANK:C_RANK + NE].unsqueeze(1).to_broadcast([P, TT, NE]),
                                     ALU.mult))
                then(v.tensor_reduce(first, rank, AX.X, ALU.max))
                onehot = mm[:, :, 64:72]
                then(v.tensor_tensor(onehot, rank, bc(first), ALU.is_equal))
                then(v.tensor_scalar(one_minus, best, -1.0, 1.0, ALU.mult, ALU.add))
                v.tensor_tensor(mm[:, :, 0:64].rearrange("p t (n h) -> p t n h", n=NE),
                                gm[:].rearrange("p t (n h) -> p t n h", n=NE),
                                onehot.unsqueeze(3).to_broadcast([P, TT, NE, HE]), ALU.mult).then_inc(m_ready, 1)
                assert n[0] == GATE, n

            def finish(bb):
                best = g1x[2]
                dve.wait_ge(xn_added, bb * 2 + 2)
                for t in range(TT):
                    dve.wait_ge(d_ready, bb * 2 + (t + 1))
                    v.scalar_tensor_tensor(x[:, t, bb, :], banks[5 + t][:], best[:, t:t + 1], x[:, t, bb, :],
                                           ALU.mult, ALU.add).then_inc(out_ready, 1)

            def attn_rest(i, j):
                dve.wait_ge(ot_hi, i * 2 + (j + 1))
                hs = slice(2 * j, 2 * j + 2)
                v.tensor_tensor(otl[:, hs, :].rearrange("p h s -> p (h s)"), banks[j][:],
                                oth[:, hs, :].rearrange("p h s -> p (h s)").bitcast(F32),
                                ALU.subtract).then_inc(ot_lo, 1)

            def step(g, b, at):
                i = b + 8 * g
                final = g == NG - 1 and at == NB - 1
                for j in range(QH):
                    wait_apart(dve, s_ready, i * 4 + (j + 1), j)
                    for t, cols, m in ((0, slice(0, P), mask[:, P:2 * P]), (1, slice(P, 3 * P), mask)):
                        n = 2 * j + t
                        last = v.tensor_tensor_reduce(out=sm[:, j, cols], in0=banks[3 + j % 2][:, cols], in1=m,
                                                      scale=-SCALE, scalar=3.0e38, op0=ALU.add, op1=ALU.min,
                                                      accum_out=mx[:, n:n + 1])
                    last.then_inc(s_masked, 1)
                    if j == 1 and (g or at):
                        attn_rest(i - 1, 1)
                v_rest(i)
                if needs_norm1(g, at):
                    norm_stats(tokens(b + 3), b + 3)
                if needs_ffn(g, at):
                    norm_apply(tokens(b - 2), b + (NB - 2), second=True)
                if needs_finish(g, at):
                    finish(b - 3)
                dve.wait_ge(p_exp, i * 4 + 2)
                v.reciprocal(rinv[:, 0:4], rsum[:, 0:4]).then_inc(r_ready, 1)
                dve.wait_ge(p_exp, i * 4 + 4)
                v.reciprocal(rinv[:, 4:8], rsum[:, 4:8]).then_inc(r_ready, 1)
                if needs_xt(g, at):
                    xt_rest(b + 2)
                if not final:
                    rope(i + 1, 0)
                    rope(i + 1, 1)
                    rope_add(i + 1, 0)
                    rope(i + 1, 2)
                    rope_add(i + 1, 1)
                    rope_add(i + 1, 2)
                if needs_norm1(g, at):
                    norm_apply(tokens(b + 3), b + 3)
                if needs_ffn(g, at):
                    gate_read(b - 2)
                for j in range(3):
                    dve.wait_ge(pt_hi, i * 3 + (j + 1))
                    v.tensor_tensor(ptl[:, j, :], banks[5 + j][:], pth[:, j, :].bitcast(F32),
                                    ALU.subtract).then_inc(pt_lo, 1)
                if needs_ffn(g, at):
                    gates(b - 2)
                if not (g == 0 and at == 0):
                    add_output(i - 1, (b - 1) if at else NB - 1)
                if needs_norm2(g, at):
                    wait_apart(dve, x_added, i * 2, 5)
                    norm_stats(tokens(b - 1), b + (NB - 1))
                attn_rest(i, 0)

            steps(dve, step)
            last = NG * NB - 1
            attn_rest(last, 1)
            norm_apply(tokens(NB - 2), 2 * NB - 2, second=True)
            finish(NB - 3)
            gate_read(NB - 2)
            gates(NB - 2)
            add_output(last, NB - 1)
            dve.wait_ge(x_added, 2 * last + 2)
            norm_stats(tokens(NB - 1), 2 * NB - 1)
            norm_apply(tokens(NB - 1), 2 * NB - 1, second=True)
            finish(NB - 2)
            gate_read(NB - 1)
            gates(NB - 1)
            finish(NB - 1)

        @block.tensor
        def _(pe):
            mmul = nc.tensor.matmul

            def split_product(dst, parts, start=True, stop=True):
                n = len(parts)
                for k, (lh, ll, rh, rl) in enumerate(parts):
                    mmul(dst, lh, rh, start=start and k == 0, stop=False, skip_group_check=True)
                    mmul(dst, ll, rh, start=False, stop=False, skip_group_check=True)
                    last = mmul(dst, lh, rl, start=False, stop=stop and k == n - 1, skip_group_check=True)
                return last

            pe.wait_ge(pw_done, KC)
            for k in range(KC):
                last = mmul(banks[7][:, 0:FC], ones[:], pw[:, k, 0:FC], start=k == 0, stop=k == KC - 1)
            last.then_inc(cw_mm, 1)

            def chunk(s):
                for m in range(CH // 2):
                    hs = slice(2 * m, 2 * m + 2)
                    flat = lambda t: t[:, hs, :].rearrange("p h j -> p (h j)")
                    dst = banks[2 * s + m // 4][:, (m % 4) * P:(m % 4 + 1) * P]
                    mmul(dst, flat(g1[s]), flat(bt[s]), start=m % 4 == 0, stop=False, skip_group_check=True)
                    last = mmul(dst, flat(g2[s]), flat(bt[s]), start=False, stop=m % 4 == 3, skip_group_check=True)
                    if m % 4 == 3:
                        last.then_inc(mixed, 1)

            for s in range(2):
                pe.wait_ge(b_ready, s + 1)
                pe.wait_ge(g2_ready, s + 1)
                chunk(s)
            with pe.Fori(1, NCH // 2) as it:
                for s in range(2):
                    pe.wait_ge(b_ready, it * 2 + (s + 1))
                    pe.wait_ge(g2_ready, it * 2 + (s + 1))
                    pe.wait_ge(evac, it * 2 + (s - 1))
                    chunk(s)

            def transpose_tokens(m):
                for q in range(2):
                    for k in range(2):
                        for t in range(TT):
                            col = (2 * q + k) * P
                            last = nc.tensor.transpose(banks[5 + q][:, k * S + t * P:k * S + (t + 1) * P],
                                                       xn[:, t, col:col + P], ident)
                    last.then_inc(xt_ready, 1)

            def project(s, b, first, between=None):
                def parts(c):
                    cols = slice(c * HD, (c + 1) * HD)
                    return [(wk[:, k, cols], wl[:, k, cols], xt_h[:, b, k, :], xt_l[:, b, k, :]) for k in range(KC)]
                if not first:
                    pe.wait_ge(ot_lo, s * 2 - 3)
                split_product(banks[0][:, 0:S], parts(0))
                split_product(banks[0][:, S:2 * S], parts(1)).then_inc(proj, 1)
                for j in range(2):
                    if j == 0 and not first:
                        pe.wait_ge(ot_lo, s * 2 - 2)
                    if j == 1 and (not isinstance(s, int) or s):
                        pe.wait_ge(v_lo, s)
                    if j == 1 and between:
                        between()
                    for h in range(2):
                        last = split_product(banks[1 + j][:, h * S:(h + 1) * S], parts(2 + 2 * j + h))
                    last.then_inc(proj, 1)

            def transpose_v(s):
                pe.wait_ge(swapped, s * 3 + 3)
                pe.wait_ge(kq_cos, s * 3 + 3)
                for t in range(TT):
                    last = nc.tensor.transpose(banks[2][:, t * P:(t + 1) * P], vt[:, t * P:(t + 1) * P], ident)
                last.then_inc(vt_ready, 1)

            def gate_product(bb):
                for t in range(TT):
                    for k in range(KC):
                        last = mmul(banks[0][:, t * S:t * S + FC], xnt[:, k, t * P:(t + 1) * P], fw[:, k, :],
                                    start=k == 0, stop=k == KC - 1)
                last.then_inc(f_ready, 1)

            def update_rows(bb):
                pe.wait_ge(m_ready, bb + 1)
                for t in range(TT):
                    last = nc.tensor.transpose(banks[7][0:MC, t * P:(t + 1) * P], mm[:, t, :], ident)
                last.then_inc(mt_ready, 1)

            def update_product(bb):
                pe.wait_ge(mt_done, bb + 1)
                for t in range(TT):
                    mmul(banks[5 + t][:], mt[:, t * P:(t + 1) * P], dw[:], start=True, stop=True).then_inc(d_ready, 1)

            def out_product(i):
                for t in range(TT):
                    parts = [(oth[:, h, t * P:(t + 1) * P], otl[:, h, t * P:(t + 1) * P], woh[:, h, :], wol[:, h, :])
                             for h in range(QH)]
                    split_product(banks[3 + t][:], parts).then_inc(o_ready, 1)

            pe.wait_ge(cst_in, 16)
            for b in range(2):
                pe.wait_ge(xn_ready, b + 1)
                if b:
                    pe.wait_ge(xt_lo, 2 * b)
                transpose_tokens(b)
            pe.wait_ge(w_lo, KC)
            pe.wait_ge(xt_lo, 2)
            project(0, 0, True)
            transpose_v(0)

            def step(g, b, at):
                i = b + 8 * g
                final = g == NG - 1 and at == NB - 1
                pe.wait_ge(kq_lo, i * 3 + 3)
                for j in range(QH):
                    if j == 0 and (g or at > 1):
                        pe.wait_ge(x_added, i * 2 - 2)
                    if j >= 2:
                        pe.wait_ge(s_masked, i * 4 + (j - 1))
                    bank = banks[3 + j % 2]
                    mmul(bank[:, 0:P], kq[:, 1 + j, 0:P], kq[:, 0, 0:P], start=True, stop=True, skip_group_check=True)
                    qs = slice(S + j * P, S + (j + 1) * P)
                    split_product(bank[:, P:3 * P], [(kh[:, qs], kl[:, qs], kh[:, 0:S], kl[:, 0:S])]).then_inc(s_ready, 1)
                if needs_xt(g, at):
                    pe.wait_ge(xn_ready, b + 3)
                    if at:
                        pe.wait_ge(pt_lo, i * 3)
                    else:
                        pe.wait_ge(xt_lo, 4)
                    transpose_tokens(b + 2)
                if needs_finish(g, at):
                    pe.wait_ge(pt_lo, i * 3)
                    update_product(b - 3)

                def tokens_again():
                    pe.wait_ge(xn_ready, b + (NB - 1))
                    if at > 2:
                        pe.wait_ge(out_ready, b * 2 - 4)
                    else:
                        pe.wait_ge(pt_lo, i * 3)
                    transpose_tokens(b + (NB - 2))

                if not final:
                    if g == 0 and at < NB - 1:
                        pe.wait_ge(xt_lo, b * 2 + 4)
                    if at == NB - 1:
                        pe.wait_ge(w_lo, (g + 1) * NCK + KC)
                    project(i + 1, (b + 1) if at < NB - 1 else 0, g == 0 and at == 0,
                            tokens_again if needs_ffn(g, at) else None)
                elif needs_ffn(g, at):
                    tokens_again()
                if needs_ffn(g, at):
                    pe.wait_ge(xt_hi, b * 2 + (2 * NB - 2))
                    if final:
                        pe.wait_ge(ot_lo, i * 2)
                    else:
                        pe.wait_ge(swapped, i * 3 + 4)
                        pe.wait_ge(kq_cos, i * 3 + 4)
                    gate_product(b - 2)
                for j in range(2):
                    pe.wait_ge(p_norm, i * 4 + (2 * j + 2))
                    if j == 0:
                        if g or at:
                            pe.wait_ge(pt_lo, i * 3)
                        if needs_xt(g, at):
                            pe.wait_ge(xt_lo, b * 2 + 6)
                        if needs_ffn(g, at):
                            pe.wait_ge(xt_hi, b * 2 + (2 * NB - 2))
                    for h in range(2):
                        for t in range(2):
                            last = nc.tensor.transpose(banks[5 + j][:, h * S + t * P:h * S + (t + 1) * P],
                                                       sm[:, 2 * j + h, t * P:(t + 1) * P], ident)
                    last.then_inc(tr_ready, 1)
                for h in range(QH):
                    last = nc.tensor.transpose(banks[7][:, h * P:(h + 1) * P], sm[:, h, 2 * P:3 * P], ident)
                last.then_inc(tr_ready, 1)
                if g or at:
                    pe.wait_ge(s_masked, i * 4 + 4)
                    pe.wait_ge(ot_lo, i * 2)
                    if at == 1:
                        pe.wait_ge(w_lo, g * NCK + NCK)
                    out_product(i - 1)
                if not final:
                    transpose_v(i + 1)
                pe.wait_ge(pt_lo, i * 3 + 3)
                pe.wait_ge(v_lo, i + 1)
                if not final:
                    pe.wait_ge(swapped, i * 3 + 6)
                    pe.wait_ge(kq_cos, i * 3 + 6)
                elif g or at:
                    pe.wait_ge(ot_lo, i * 2)
                if needs_ffn(g, at):
                    pe.wait_ge(f_read, b - 1)
                for j in range(2):
                    split_product(banks[j][:], [(vh[:, 0, :], vl[:, 0, :], pth[:, j, :], ptl[:, j, :])], stop=False)
                    second = banks[j][:].rearrange("p (h s) -> p h s", h=2)[:, :, P:S]
                    cols = slice(j * S, (j + 1) * S)
                    split_product(second, [(vh[:, 1, :], vl[:, 1, :], pth[:, 2, cols].rearrange("p (h s) -> p h s", h=2),
                                            ptl[:, 2, cols].rearrange("p (h s) -> p h s", h=2))],
                                  start=False).then_inc(pv_ready, 1)
                if needs_ffn(g, at):
                    update_rows(b - 2)

            steps(pe, step)
            last = NG * NB - 1
            update_product(NB - 3)
            for bb in (NB - 2, NB - 1):
                pe.wait_ge(xn_ready, NB + bb + 1)
                pe.wait_ge(out_ready, 2 * bb)
                transpose_tokens(NB + bb)
                pe.wait_ge(xt_hi, 2 * (NB + bb) + 2)
                pe.wait_ge(ot_lo, 2 * last + 2)
                pe.wait_ge(f_read, bb)
                gate_product(bb)
                if bb == NB - 2:
                    out_product(last)
                update_rows(bb)
                update_product(bb)


def kernel(x, L0_tok_log_dt, L0_tok_log_w_real, L0_tok_w_imag, L0_attn_w_q, L0_attn_w_k, L0_attn_w_v, L0_attn_w_o,
           L0_ffn_select_weight, L0_ffn_select_mean_diff, L0_ffn_imp_center, L0_ffn_imp_slope, L0_ffn_lora_update,
           L0_ffn_lora_degen, L0_ffn_bias_w, L0_ffn_debias_w):
    import concourse.bacc as bacc
    from concourse.bass_utils import run_bass_kernel_spmd

    def a(v):
        return np.asarray(v)

    by_row = a(x).transpose(3, 2, 1, 0)
    wq = a(L0_attn_w_q).reshape(KC, P, NG, QH * HD).transpose(2, 0, 1, 3)
    wk = a(L0_attn_w_k).reshape(KC, P, NG, HD).transpose(2, 0, 1, 3)
    wv = a(L0_attn_w_v).reshape(KC, P, NG, HD).transpose(2, 0, 1, 3)

    def chunks(w):
        return w.reshape(KC, P, -1).transpose(1, 0, 2)

    arrays = {
        "mix_c": by_row.reshape(P, S, NB),
        "mix_s": by_row[::-1].reshape(P, S, NB),
        "log_dt": a(L0_tok_log_dt),
        "log_wr": a(L0_tok_log_w_real).reshape(2, P, NS).transpose(0, 2, 1).reshape(P, P),
        "w_im": a(L0_tok_w_imag).reshape(2, P, NS).transpose(0, 2, 1).reshape(P, P),
        "w_qkv": np.concatenate([wk, wv, wq], axis=-1),
        "w_o": a(L0_attn_w_o).reshape(NG, QH, HD, D),
        "w_gate": np.concatenate([chunks(a(L0_ffn_select_weight).transpose(1, 0, 2)),
                                  chunks(a(L0_ffn_select_mean_diff).T),
                                  chunks(a(L0_ffn_lora_update).transpose(1, 0, 2))], axis=-1),
        "w_gmul": chunks(a(L0_ffn_debias_w).T),
        "w_upd": np.concatenate([a(L0_ffn_lora_degen).transpose(0, 2, 1).reshape(NE * HE, D), a(L0_ffn_bias_w)]),
        "centers": a(L0_ffn_imp_center),
        "slopes": a(L0_ffn_imp_slope),
        "consts": constants(),
    }
    nc = bacc.Bacc("TRN2", target_bir_lowering=False, num_devices=1)
    args, sent = [], {}
    for name, v in arrays.items():
        v = np.ascontiguousarray(v)
        sent[f"in_{name}"] = v
        args.append(nc.dram_tensor(f"in_{name}", v.shape, mybir.dt.from_np(v.dtype), kind="ExternalInput").ap())
    out = nc.dram_tensor("out_0", (NB, S, D), F32, kind="ExternalOutput").ap()
    tower(nc, *args, out)
    r = run_bass_kernel_spmd(nc, [sent], core_ids=[0])
    return r.results[0]["out_0"]
```

```python
from contextlib import ExitStack

import numpy as np
import concourse.bass as bass
from concourse import mybir

F32 = mybir.dt.float32
F32R = mybir.dt.float32r
I32 = mybir.dt.int32
ALU = mybir.AluOpType
ACT = mybir.ActivationFunctionType
AX = mybir.AxisListType

P = 128
NB = 8
S = 256
D = 512
NS = 64
NH, NKV, HD = 16, 4, 128
NG = NKV
QH = NH // NKV
KC = D // P
TT = S // P
WC = HD + HD + QH * HD
NE, SE, HE = 8, 8, 8
FC = NE * SE + NE + NE * HE
MC = NE * HE + NE
LA, LB1, LB2 = 8, 8, 8
NL = LA + LB1 + LB2
CH = 16
NCH = S // CH
G1_DVE = 6
EPS = 1e-5
SCALE = float(HD) ** -0.5
MASKED = -1e30
ROUND = 1.5 * 2.0 ** 23

C_COS, C_SIN, C_MASK, C_ID, C_L, C_RANK, C_ONES, C_QUARTER, C_POW = 0, 256, 512, 768, 896, 920, 928, 1056, 1057
C_ALL = 1059


def constants():
    inv = (1.0 / 10000.0 ** (np.arange(0, HD, 2) / HD)).astype(np.float32)
    ang = (np.arange(S, dtype=np.float32)[None, :] * np.concatenate([inv, inv])[:, None]).astype(np.float32)
    c = np.zeros((P, C_ALL), np.float32)
    c[:, C_COS:C_COS + S] = np.cos(ang.astype(np.float64))
    sign = np.where(np.arange(HD) < HD // 2, -1.0, 1.0)[:, None]
    c[:, C_SIN:C_SIN + S] = sign * np.sin(ang.astype(np.float64))
    q, k = np.arange(P)[:, None], np.arange(P)[None, :]
    c[:, C_MASK + P:C_MASK + 2 * P] = np.where(k <= q, 0.0, MASKED)
    c[:, C_ID:C_ID + P] = np.eye(P)
    c[:, C_L:C_L + NL] = np.concatenate([np.arange(8), 8 * np.arange(8), 64 * np.arange(8)])[None, :]
    c[:, C_RANK:C_RANK + NE] = (NE - np.arange(NE))[None, :]
    c[:, C_ONES:C_ONES + P] = 1.0
    c[:, C_QUARTER] = np.pi / 2
    c[:, C_POW:C_POW + TT] = -0.5
    return c


NCK = KC + QH

CH_RHO, CH_TURN = 16, 21
GATE, GATE_Z = 15, 7


def rope_view(j):
    if j == 0:
        return (lambda t: t[:, 0, :]), (lambda c: c), (lambda t: t[:, 0, :]), (lambda t: t[:, 0:S])
    h = slice(2 * j - 1, 2 * j + 1)
    return ((lambda t: t[:, h, :]), (lambda c: c.unsqueeze(1).to_broadcast([P, 2, S])), (lambda t: t[:, h, P:S]),
            (lambda t: t[:, j * S:(j + 1) * S].rearrange("p (h q) -> p h q", h=2)))


RUNS = [
    [(0, 1), (1, 2), (2, 5), (5, 6), (6, 7), (7, 8)],
    [(0, 1), (1, 6), (6, 7), (7, 8)],
    [(0, 1), (1, 6), (6, 7), (7, 8)],
    [(0, 1), (1, 2), (2, 3), (3, 7), (7, 8)],
]


def steps(engine, body):
    for g in range(NG):
        for lo, hi in RUNS[g]:
            if hi - lo == 1:
                body(g, lo, lo)
            else:
                with engine.Fori(lo, hi) as b:
                    body(g, b, lo)


def needs_xt(g, at):
    return g == 0 and at <= 5


def needs_norm1(g, at):
    return g == 0 and at <= 4


def needs_ffn(g, at):
    return g == NG - 1 and at >= 2


def needs_norm2(g, at):
    return g == NG - 1 and at >= 1


def needs_finish(g, at):
    return g == NG - 1 and at >= 3


def tower(nc, mix_c, mix_s, log_dt, log_wr, w_im, w_qkv, w_o, w_gate, w_gmul, w_upd, centers, slopes, consts, out):
    x_dram = nc.dram_tensor("mixed", [S, NB, D], F32, kind="Internal").ap()
    top = ExitStack()
    with top:
        def sem(name):
            return top.enter_context(nc.semaphore(name))

        def sb(name, shape, dt=F32, stack=top):
            return stack.enter_context(nc.sbuf_tensor(name, shape, dt))

        banks = [top.enter_context(nc.psum_tensor(f"bank{k}", [P, 512], F32)) for k in range(8)]

        x = sb("x", [P, TT, NB, D])
        wk = sb("w_hi", [P, KC, WC], F32R)
        wl = sb("w_lo", [P, KC, WC], F32R)
        raw = sb("raw", [P, 2, WC])
        cst = sb("cst", [P, C_ALL])
        cosT = cst[:, C_COS:C_COS + S]
        sinT = cst[:, C_SIN:C_SIN + S]
        mask = cst[:, C_MASK:C_MASK + 2 * P]
        ident = cst[:, C_ID:C_ID + P]
        ones = cst[:, C_ONES:C_ONES + P]
        fw = sb("fw", [P, KC, FC])
        dw = sb("dw", [MC, D])
        cw = sb("cw", [P, FC])
        dbs = sb("dbs", [P, KC, NE])
        spare = sb("spare", [1, 9])
        ctr = sb("ctr", [P, NE])
        slp = sb("slp", [P, NE])

        mixer = ExitStack()
        ta = [sb(f"ta{k}", [P, 8, S], F32, mixer) for k in range(6)]
        re1, im1, u2, v2, pre, pim = ta
        mc = sb("mc", [P, S, NB], F32, mixer)
        ms = sb("ms", [P, S, NB], F32, mixer)
        ang = sb("ang", [P, NL, P], F32, mixer)
        sn = sb("sn", [P, NL, P], F32, mixer)
        mag = sb("mag", [P, NL, P], F32, mixer)
        bt = [sb(f"bt{k}", [P, CH, 64], F32, mixer) for k in range(2)]
        g1 = [sb(f"g1{k}", [P, CH, 64], F32, mixer) for k in range(2)]
        g2 = [sb(f"g2{k}", [P, CH, 64], F32, mixer) for k in range(2)]
        tmp = sb("tmp", [P, CH, 64], F32, mixer)
        st = [sb(f"st{k}", [P, CH // 2, 64], F32, mixer) for k in range(2)]
        mixer.close()

        small = ExitStack()
        hold = [sb(f"hold{k}", [P, 8, S], F32, small) for k in range(6)]
        hold += [sb(f"holdm{k}", [P, S, NB], F32, small) for k in range(2)]
        hold += [sb(f"holdn{k}", [P, NL, P], F32, small) for k in range(3)]
        lg = sb("lg", [P, 2, P], F32, small)
        ex = sb("ex", [P, 2, P], F32, small)
        kk = sb("kk", [P, 2, P], F32, small)
        rr = sb("rr", [P, 2, P], F32, small)
        qq = sb("qq", [P, 2, P], F32, small)
        ki = sb("ki", [P, 2, P], I32, small)
        wim = sb("wim", [P, P], F32, small)
        rho = sb("rho", [P, P], F32, small)
        turn = sb("turn", [P, P], F32, small)
        em1 = sb("em1", [P, P], F32, small)
        half = sb("half", [P, P], F32, small)
        ar = sb("ar", [P, P], F32, small)
        ai = sb("ai", [P, P], F32, small)
        dr = sb("dr", [P, P], F32, small)
        di = sb("di", [P, P], F32, small)
        nrm = sb("nrm", [P, P], F32, small)
        t0 = sb("t0", [P, P], F32, small)
        pt2 = sb("pt2", [P, 8, P], F32, small)
        pt3 = sb("pt3", [P, 8, P], F32, small)
        small.close()

        xt_h = sb("xt_hi", [P, NB, KC, S], F32R)
        xt_l = sb("xt_lo", [P, NB, KC, S], F32R)
        woh = sb("wo_hi", [P, QH, D], F32R)
        wol = sb("wo_lo", [P, QH, D], F32R)
        kq = sb("kq", [P, 1 + QH, S])
        kh = sb("kq_hi", [P, S + QH * P], F32R)
        kl = sb("kq_lo", [P, S + QH * P], F32R)
        sw = sb("swap", [P, 1 + QH, S])
        sm = sb("sm", [P, QH, 3 * P])
        pth = sb("pt_hi", [P, 3, 512], F32R)
        ptl = sb("pt_lo", [P, 3, 512], F32R)
        vt = sb("vt", [P, S])
        vh = sb("v_hi", [P, TT, HD], F32R)
        vl = sb("v_lo", [P, TT, HD], F32R)
        oth = sb("ot_hi", [P, QH, S], F32R)
        otl = sb("ot_lo", [P, QH, S], F32R)
        norm_mem = sb("norm_mem", [P, 2 * TT * D])
        xn = norm_mem[:, 0:TT * D].rearrange("p (t d) -> p t d", t=TT)
        xnt = norm_mem[:, TT * D:2 * TT * D].rearrange("p (k s) -> p k s", k=KC)
        stats = sb("stats", [P, TT, 6])
        mv = sb("mv", [P, TT, 2])
        rstd = sb("rstd", [P, TT])
        mx = sb("mx", [P, 2 * QH])
        rsum = sb("rsum", [P, 2 * QH])
        rinv = sb("rinv", [P, 2 * QH])
        gu = sb("gu", [P, TT, NE * SE])
        gm = sb("gm", [P, TT, NE * HE])
        mm = sb("mm", [P, TT, MC])
        mt = sb("mt", [MC, S])
        gs = [sb(f"gs{k}", [P, TT, NE]) for k in range(3)]
        g1x = [sb(f"gx{k}", [P, TT]) for k in range(4)]

        pw = x[:, TT - 1, NB - KC:NB, 0:FC]
        neg2 = x[:, TT - 1, 0:LB2 * P // D, :].rearrange("p c (e h) -> p (c e) h", h=P)

        def raw_slot(n):
            if n < NCK:
                return n % 2
            return (n - NCK) % 4

        def raw_chunk(n):
            width = WC if n % NCK < KC else D
            k = raw_slot(n)
            return raw[:, k, 0:width] if k < 2 else norm_mem[:, (k - 2) * WC:(k - 2) * WC + width]

        def raw_turn(n):
            return sum(raw_slot(m) == raw_slot(n) for m in range(n + 1))

        cst_in, par_in, mix_in, gate_in = sem("cst_in"), sem("par_in"), sem("mix_in"), sem("gate_in")
        raw_in = [sem(f"raw_in{k}") for k in range(4)]
        w_hi, w_lo = sem("w_hi_done"), sem("w_lo_done")
        chain = sem("dve_chain")
        act_tab, tab_ready, neg_ready, p_ready, d_ready0 = (
            sem("act_tables"), sem("tables_ready"), sem("negatives_ready"), sem("p_ready"), sem("d_of_poles_ready"))
        tab_in = [sem("tables_in0"), sem("tables_in1")]
        pool_ready = sem("pool_powers_ready")
        pool_tab = sem("pool_tables")
        t2_done = sem("t2_done")
        t1_done = sem("t1_done")
        b_ready, g2_ready, mixed, evac, xd_out = (
            sem("b_ready"), sem("g2_ready"), sem("mixed_ready"), sem("evacuated"), [sem("xd_out0"), sem("xd_out1")])
        x_tile0, x_first, x_rest = sem("x_tile0"), sem("x_first"), sem("x_rest")
        pw_done, cw_mm, cw_done = sem("pw_done"), sem("cw_mm"), sem("cw_done")
        ln_st, ln_var, ln_pool, ln_rstd, xn_ready = (
            sem("ln_stats"), sem("ln_var"), sem("ln_pool"), sem("ln_rstd"), sem("xn_ready"))
        xt_ready, xt_hi, xt_lo = sem("xt_ready"), sem("xt_hi_done"), sem("xt_lo_done")
        proj, swapped, kq_cos, rot_sin, kq_rot, kq_hi, kq_lo = (
            sem("proj_ready"), sem("swapped"), sem("kq_cos"), sem("rot_sin"), sem("kq_rotated"), sem("kq_hi_done"),
            sem("kq_lo_done"))
        s_ready, s_masked, p_exp, r_ready, p_norm = (
            sem("scores_ready"), sem("scores_masked"), sem("p_exp"), sem("rinv_ready"), sem("p_norm"))
        tr_ready, pt_hi, pt_lo = sem("tr_ready"), sem("pt_hi_done"), sem("pt_lo_done")
        vt_ready, v_hi, v_lo = sem("vt_ready"), sem("v_hi_done"), sem("v_lo_done")
        pv_ready, ot_hi, ot_lo = sem("pv_ready"), sem("ot_hi_done"), sem("ot_lo_done")
        o_ready, x_added = sem("o_ready"), sem("x_added")
        f_ready, f_read, gate, e_ready, m_ready = (
            sem("f_ready"), sem("f_read"), sem("gate_chain"), sem("gate_exp"), sem("m_ready"))
        xn_scaled, xn_added = sem("xn_scaled"), sem("xn_added")
        mt_ready, mt_done, d_ready, out_ready, stored = (
            sem("mt_ready"), sem("mt_done"), sem("d_ready"), sem("out_ready"), sem("stored"))

        block = top.enter_context(nc.Block())

        def wait_apart(engine, signal, value, slot):
            engine.wait_ge(signal, value)
            if signal in (ln_var, r_ready, gate):
                nc.gpsimd.tensor_tensor(spare[:, slot:slot + 1], cst[0:1, 0:1], cst[0:1, 0:1], ALU.add)
            else:
                nc.vector.tensor_copy(spare[:, slot:slot + 1], cst[0:1, 0:1])

        @block.sync
        def _(sp):
            sp.dma_start(cst[:], consts).then_inc(cst_in, 16)
            for hh in range(2):
                sp.dma_start(lg[hh * NS:(hh + 1) * NS, 0, :],
                             log_dt[hh * P:(hh + 1) * P].unsqueeze(0).to_broadcast([NS, P])).then_inc(par_in, 16)
            sp.dma_start(lg[:, 1, :], log_wr).then_inc(par_in, 16)
            sp.dma_start(wim[:], w_im).then_inc(par_in, 16)

            def load_raw(n):
                g, k = divmod(n, NCK)
                before = [m for m in range(n) if raw_slot(m) == raw_slot(n)]
                if before:
                    sp.wait_ge(w_lo, before[-1] + 1)
                elif n >= NCK:
                    sp.wait_ge(xt_ready, 2 * NB)
                src = w_qkv[g, k] if k < KC else w_o[g, k - KC]
                sp.dma_start(raw_chunk(n), src).then_inc(raw_in[raw_slot(n)], 16)

            load_raw(0)
            load_raw(1)
            sp.dma_start(mc[:], mix_c).then_inc(mix_in, 16)
            sp.dma_start(ms[:], mix_s).then_inc(mix_in, 16)
            sp.dma_start(fw[:], w_gate).then_inc(gate_in, 16)
            sp.dma_start(dw[:], w_upd).then_inc(gate_in, 16)
            sp.dma_start(dbs[:], w_gmul).then_inc(gate_in, 16)
            sp.dma_start(ctr[:], centers.unsqueeze(0).to_broadcast([P, NE])).then_inc(gate_in, 16)
            sp.dma_start(slp[:], slopes.unsqueeze(0).to_broadcast([P, NE])).then_inc(gate_in, 16)
            load_raw(2)
            load_raw(3)

            def spread(dst, src, e0, ri, hh, signal):
                sp.dma_start(dst[ri * NS:(ri + 1) * NS, :, hh * P:(hh + 1) * P],
                             src[hh * NS:(hh + 1) * NS, e0:e0 + 8, :]).then_inc(signal, 16)

            for hh in range(2):
                if hh == 0:
                    sp.wait_ge(tab_ready, 1)
                for ri in range(2):
                    spread(re1, ang, 8, ri, hh, tab_in[hh])
                spread(u2, ang, 0, 0, hh, tab_in[hh])
                spread(v2, ang, 0, 1, hh, tab_in[hh])
                if hh == 0:
                    sp.wait_ge(tab_ready, 2)
                for ri in range(2):
                    spread(im1, sn, 8, ri, hh, tab_in[hh])
                spread(u2, sn, 0, 1, hh, tab_in[hh])
                if hh == 0:
                    sp.wait_ge(neg_ready, 1)
                spread(v2, neg2, 0, 0, hh, tab_in[hh])
                if hh == 0:
                    sp.wait_ge(p_ready, 1)
                spread(pre, mag, 16, 0, hh, tab_in[hh])
                if hh == 0:
                    sp.wait_ge(neg_ready, 2)
                spread(pre, ang, 16, 1, hh, tab_in[hh])
                if hh == 0:
                    sp.wait_ge(p_ready, 2)
                for ri in range(2):
                    spread(pim, sn, 16, ri, hh, tab_in[hh])

            load_raw(KC)
            load_raw(KC + 1)
            sp.wait_ge(cw_mm, 1)
            for t in range(TT):
                with sp.Fori(t * NCH // 4, (t + 1) * NCH // 4) as it:
                    for s in range(2):
                        sp.wait_ge(evac, it * 2 + (s + 1))
                        for h2 in range(2):
                            rows = x_dram.rearrange("(q m t) c (a j) -> q t (c a) m j", m=CH // 2, t=2, j=64)
                            sp.dma_start(rows[it * 2 + s, h2],
                                         st[s][h2 * 64:(h2 + 1) * 64, :, :]).then_inc(xd_out[s], 16)
                for s in range(2):
                    sp.wait_ge(xd_out[s], 16 * NCH * (t + 1) // TT)
                rows = x_dram[t * P:(t + 1) * P]
                if t == 0:
                    sp.dma_start(x[:, t, :, :], rows).then_inc(x_tile0, 16)
                else:
                    sp.dma_start(x[:, t, 0:2, :], rows[:, 0:2, :]).then_inc(x_first, 16)
                    sp.dma_start(x[:, t, 2:NB, :], rows[:, 2:NB, :]).then_inc(x_rest, 16)

            for n in range(KC + 2, NCK * NG):
                load_raw(n)
            with sp.Fori(0, NB) as bb:
                for t in range(TT):
                    sp.wait_ge(out_ready, bb * 2 + (t + 1))
                    sp.dma_start(out[bb, t * P:(t + 1) * P, :], x[:, t, bb, :]).then_inc(stored, 16)
            sp.wait_ge(stored, 16 * NB * TT)

        @block.gpsimd
        def _(pool):
            def split_lo(n):
                k = n % NCK
                pool.wait_ge(w_hi, n + 1)
                if k < KC:
                    hi, lo = wk[:, k, :], wl[:, k, :]
                else:
                    hi, lo = woh[:, k - KC, :], wol[:, k - KC, :]
                nc.gpsimd.tensor_tensor(lo, raw_chunk(n), hi.bitcast(F32), ALU.subtract).then_inc(w_lo, 1)

            for n in range(2):
                split_lo(n)
            pool.wait_ge(chain, CH_RHO)
            nc.gpsimd.tensor_tensor(mag[:], rho[:].unsqueeze(1).to_broadcast([P, NL, P]),
                                    cst[:, C_L:C_L + NL].unsqueeze(2).to_broadcast([P, NL, P]),
                                    ALU.mult).then_inc(pool_tab, 1)
            la = slice(LB1 + LB2, NL)
            pool.wait_ge(act_tab, 5)
            nc.gpsimd.tensor_tensor(ang[:, la, :], ang[:, la, :], mag[:, la, :], ALU.mult).then_inc(pool_ready, 1)
            nc.gpsimd.tensor_tensor(sn[:, la, :], sn[:, la, :], mag[:, la, :], ALU.mult).then_inc(pool_ready, 1)
            for n in range(2, KC):
                split_lo(n)
            pool.wait_ge(d_ready0, 1)
            pool.wait_ge(pool_ready, 2)
            nc.gpsimd.tensor_tensor(pt2[:], ang[:, la, :], di[:].unsqueeze(1).to_broadcast([P, LA, P]),
                                    ALU.mult).then_inc(pool_ready, 1)

            def chunk(it, s):
                hs = bass.ds(it * (2 * CH) + s * CH, CH)
                rest = bass.ds(it * (2 * CH) + (s * CH + G1_DVE), CH - G1_DVE)
                nc.gpsimd.tensor_tensor(
                    g2[s][:].rearrange("p h (c a) -> p h c a", c=NB),
                    ms[:, hs, :].unsqueeze(3).to_broadcast([P, CH, NB, LA]),
                    pim[:, :, hs].rearrange("p a h -> p h a").unsqueeze(2).to_broadcast([P, CH, NB, LA]),
                    ALU.mult)
                nc.gpsimd.tensor_tensor(
                    g1[s][:, G1_DVE:CH, :].rearrange("p h (c a) -> p h c a", c=NB),
                    mc[:, rest, :].unsqueeze(3).to_broadcast([P, CH - G1_DVE, NB, LA]),
                    pre[:, :, rest].rearrange("p a h -> p h a").unsqueeze(2).to_broadcast([P, CH - G1_DVE, NB, LA]),
                    ALU.mult).then_inc(g2_ready, 1)

            pool.wait_ge(mix_in, 32)
            pool.wait_ge(tab_in[0], 16 * 12)
            for s in range(2):
                chunk(0, s)
            for hh in range(2):
                if hh:
                    pool.wait_ge(tab_in[1], 16 * 12)
                with pool.Fori(hh * NCH // 4 or 1, (hh + 1) * NCH // 4) as it:
                    for s in range(2):
                        pool.wait_ge(mixed, it * 4 + (2 * s - 2))
                        chunk(it, s)

            pool.wait_ge(x_first, 16)

            def norm(m):
                wait_apart(pool, ln_var, m + 1, 8)
                nc.gpsimd.tensor_scalar(rstd[:], mv[:, :, 1], EPS, 1.0, ALU.add, ALU.mult).then_inc(ln_pool, 1)
                pool.wait_ge(ln_pool, m + 1)
                nc.gpsimd.tensor_tensor(rstd[:], rstd[:], cst[:, C_POW:C_POW + TT], ALU.pow).then_inc(ln_rstd, 1)

            def rotate(s):
                for j in range(3):
                    view, table, _, _ = rope_view(j)
                    pool.wait_ge(swapped, s * 3 + (j + 1))
                    nc.gpsimd.tensor_tensor(view(sw), view(sw), table(sinT), ALU.mult).then_inc(rot_sin, 1)
                for j in range(3):
                    _, _, part, flat = rope_view(j)
                    pool.wait_ge(kq_hi, s * 3 + (j + 1))
                    nc.gpsimd.tensor_tensor(flat(kl), part(kq), flat(kh).bitcast(F32), ALU.subtract).then_inc(kq_lo, 1)

            norm(0)
            split_lo(KC)
            norm(1)
            split_lo(KC + 1)
            rotate(0)
            norm(2)

            def add_normed(bb):
                wait_apart(pool, gate, bb * GATE + GATE, 8)
                for t in range(TT):
                    nc.gpsimd.tensor_scalar(xn[:, t, :], xn[:, t, :], g1x[0][:, t:t + 1], 1.0, ALU.mult,
                                            ALU.mult).then_inc(xn_scaled, 1)
                for t in range(TT):
                    pool.wait_ge(xn_scaled, bb * 2 + (t + 1))
                    nc.gpsimd.tensor_tensor(x[:, t, bb, :], x[:, t, bb, :], xn[:, t, :], ALU.add).then_inc(xn_added, 1)

            def step(g, b, at):
                i = b + 8 * g
                if needs_norm1(g, at):
                    norm(b + 3)
                for j in range(QH):
                    if j % 2 == 0:
                        wait_apart(pool, r_ready, i * 2 + (j // 2 + 1), 6 + j // 2)
                    for t, cols in ((0, slice(0, P)), (1, slice(P, 3 * P))):
                        last = nc.gpsimd.tensor_scalar(sm[:, j, cols], sm[:, j, cols], rinv[:, 2 * j + t:2 * j + t + 1],
                                                       1.0, ALU.mult, ALU.mult)
                    last.then_inc(p_norm, 1)
                if not (g == NG - 1 and at == NB - 1):
                    rotate(i + 1)
                if needs_ffn(g, at):
                    add_normed(b - 2)
                if needs_norm2(g, at):
                    norm(b + (NB - 1))
                if g < NG - 1 and at == NB - 2:
                    for k in range(KC):
                        split_lo((g + 1) * NCK + k)
                if at == 0:
                    for k in range(KC if g else KC + 2, NCK):
                        split_lo(g * NCK + k)

            steps(pool, step)
            add_normed(NB - 2)
            norm(2 * NB - 1)
            add_normed(NB - 1)

        @block.scalar
        def _(act):
            def split_hi(n):
                k = n % NCK
                act.wait_ge(raw_in[raw_slot(n)], 16 * raw_turn(n))
                dst = wk[:, k, :] if k < KC else woh[:, k - KC, :]
                nc.scalar.activation(dst, raw_chunk(n), ACT.Copy).then_inc(w_hi, 1)

            for n in range(2):
                split_hi(n)
            TWO_PI = 6.283185
            act.wait_ge(pool_tab, 1)
            nc.scalar.activation(mag[:], mag[:], ACT.Exp).then_inc(act_tab, 1)
            act.wait_ge(chain, CH_TURN)
            nc.scalar.activation(sn[:], ang[:], ACT.Sin, scale=TWO_PI).then_inc(act_tab, 1)
            nc.scalar.activation(half[:], ang[:, 1, :], ACT.Sin, scale=TWO_PI / 2).then_inc(act_tab, 1)
            act.wait_ge(act_tab, 3)
            nc.scalar.activation(ang[:], ang[:], ACT.Abs).then_inc(act_tab, 1)
            act.wait_ge(act_tab, 4)
            nc.scalar.activation(ang[:], ang[:], ACT.Sin, scale=-TWO_PI, bias=cst[:, C_QUARTER:C_QUARTER + 1]).then_inc(act_tab, 1)
            for n in range(2, KC):
                split_hi(n)
            act.wait_ge(tab_ready, 2)
            nc.scalar.activation(neg2[:], sn[:, 0:LB2, :], ACT.Copy, scale=-1.0).then_inc(neg_ready, 1)
            act.wait_ge(p_ready, 1)
            act.wait_ge(pool_ready, 3)
            nc.scalar.activation(ang[:, LB1 + LB2:NL, :], mag[:, LB1 + LB2:NL, :], ACT.Copy, scale=-1.0).then_inc(neg_ready, 1)

            def evacuate(it, s):
                for q in range(2):
                    act.wait_ge(mixed, it * 4 + (s * 2 + q + 1))
                    for h2 in range(2):
                        rows = slice(h2 * 64, h2 * 64 + 64)
                        src = banks[2 * s + q][rows, :].rearrange("p (m t j) -> p m t j", t=2, j=64)[:, :, h2, :]
                        last = nc.scalar.activation(st[s][rows, q * 4:q * 4 + 4, :], src, ACT.Copy)
                last.then_inc(evac, 1)

            act.wait_ge(cw_mm, 1)
            nc.scalar.activation(cw[:], banks[7][:, 0:FC], ACT.Copy).then_inc(cw_done, 1)
            for s in range(2):
                evacuate(0, s)
            with act.Fori(1, NCH // 2) as it:
                for s in range(2):
                    act.wait_ge(xd_out[s], it * 32)
                    evacuate(it, s)

            def xt1(b):
                for q in range(2):
                    act.wait_ge(xt_ready, b * 2 + (q + 1))
                    nc.scalar.activation(xt_h[:, b, 2 * q:2 * q + 2, :].rearrange("p k s -> p (k s)"),
                                         banks[5 + q][:], ACT.Copy).then_inc(xt_hi, 1)

            def xt2(bb):
                for q in range(2):
                    act.wait_ge(xt_ready, bb * 2 + (2 * NB + q + 1))
                    nc.scalar.activation(xnt[:, 2 * q:2 * q + 2, :].rearrange("p k s -> p (k s)"),
                                         banks[5 + q][:], ACT.Copy).then_inc(xt_hi, 1)

            def swap(s, parts=range(3)):
                for j in parts:
                    view, _, _, _ = rope_view(j)
                    act.wait_ge(proj, s * 3 + (j + 1))
                    if j == 0 and (not isinstance(s, int) or s):
                        act.wait_ge(kq_rot, s * 3)
                        act.wait_ge(vt_ready, s)
                    src = banks[j][:, 0:S] if j == 0 else banks[j][:].rearrange("p (h s) -> p h s", h=2)
                    nc.scalar.activation(view(sw)[0:64], src[64:128], ACT.Copy)
                    last = nc.scalar.activation(view(sw)[64:128], src[0:64], ACT.Copy)
                    if j == 0:
                        last = nc.scalar.activation(vt[:], banks[0][:, S:2 * S], ACT.Copy)
                    last.then_inc(swapped, 1)

            def round_kq(s):
                for j in range(3):
                    _, _, part, flat = rope_view(j)
                    act.wait_ge(kq_rot, s * 3 + (j + 1))
                    if j == 0 and (not isinstance(s, int) or s):
                        act.wait_ge(s_ready, s * 4)
                    nc.scalar.activation(flat(kh), part(kq), ACT.Copy).then_inc(kq_hi, 1)

            def round_v(s):
                act.wait_ge(vt_ready, s + 1)
                nc.scalar.activation(vh[:].rearrange("p t d -> p (t d)"), banks[2][:, 0:S], ACT.Copy).then_inc(v_hi, 1)

            act.wait_ge(x_first, 16)
            for n in (KC, KC + 1):
                split_hi(n)
            xt1(0)
            swap(0, range(2))
            xt1(1)
            swap(0, (2,))
            round_kq(0)
            round_v(0)

            def gate_exp(bb):
                act.wait_ge(gate, bb * GATE + GATE_Z)
                nc.scalar.activation(gs[1][:], gs[1][:], ACT.Exp, scale=-1.0).then_inc(e_ready, 1)

            def mt_evac(bb):
                act.wait_ge(mt_ready, bb + 1)
                nc.scalar.activation(mt[:], banks[7][0:MC, 0:S], ACT.Copy).then_inc(mt_done, 1)

            def step(g, b, at):
                i = b + 8 * g
                for j in range(QH):
                    act.wait_ge(s_masked, i * 4 + (j + 1))
                    for t, cols in ((0, slice(0, P)), (1, slice(P, 3 * P))):
                        n = 2 * j + t
                        last = nc.scalar.activation(sm[:, j, cols], sm[:, j, cols], ACT.Exp, scale=-1.0,
                                                    bias=mx[:, n:n + 1], accum_out=rsum[:, n:n + 1])
                    last.then_inc(p_exp, 1)
                final = g == NG - 1 and at == NB - 1
                if not final:
                    swap(i + 1, range(2))
                if needs_xt(g, at):
                    xt1(b + 2)
                if needs_ffn(g, at):
                    xt2(b - 2)
                if not final:
                    swap(i + 1, (2,))
                for j in range(3):
                    act.wait_ge(tr_ready, i * 3 + (j + 1))
                    nc.scalar.activation(pth[:, j, :], banks[5 + j][:], ACT.Copy).then_inc(pt_hi, 1)
                if not final:
                    round_kq(i + 1)
                if g < NG - 1 and at == NB - 2:
                    act.wait_ge(proj, (8 * (g + 1)) * 3)
                    for k in range(KC):
                        split_hi((g + 1) * NCK + k)
                if at == 0:
                    if g > 0:
                        act.wait_ge(o_ready, 8 * g * 2)
                    for k in range(KC if g else KC + 2, NCK):
                        split_hi(g * NCK + k)
                if needs_ffn(g, at):
                    gate_exp(b - 2)
                for j in range(2):
                    act.wait_ge(pv_ready, i * 2 + (j + 1))
                    nc.scalar.activation(oth[:, 2 * j:2 * j + 2, :].rearrange("p h s -> p (h s)"),
                                         banks[j][:], ACT.Copy).then_inc(ot_hi, 1)
                if not final:
                    round_v(i + 1)
                if needs_ffn(g, at):
                    mt_evac(b - 2)

            steps(act, step)
            for bb in (NB - 2, NB - 1):
                xt2(bb)
                gate_exp(bb)
                mt_evac(bb)

        @block.vector
        def _(dve):
            links = [0]

            def link(ins):
                links[0] += 1
                ins.then_inc(chain, 1)
                dve.wait_ge(chain, links[0])

            v = nc.vector

            def expm1_parts(xin, n):
                k, r, q, p2 = (t[:].rearrange("p a b -> p (a b)")[:, 0:n] for t in (kk, rr, qq, ki))
                link(v.tensor_scalar(xin, xin, -87.0, 88.0, ALU.max, ALU.min))
                link(v.tensor_scalar(k, xin, 1.4426950408889634, ROUND, ALU.mult, ALU.add))
                link(v.tensor_scalar(k, k, ROUND, None, ALU.subtract))
                link(v.scalar_tensor_tensor(r, k, -0.693359375, xin, ALU.mult, ALU.add))
                link(v.scalar_tensor_tensor(r, k, 2.12194440e-4, r, ALU.mult, ALU.add))
                link(v.tensor_scalar(q, r, 1.0 / 5040, None, ALU.mult))
                for c in (1.0 / 720, 1.0 / 120, 1.0 / 24, 1.0 / 6, 0.5, 1.0):
                    link(v.scalar_tensor_tensor(q, q, c, r, ALU.add, ALU.mult))
                link(v.tensor_scalar(p2, k, 127.0, 8388608.0, ALU.add, ALU.mult))
                return q, p2.bitcast(F32)

            dve.wait_ge(par_in, 64)
            dve.wait_ge(cst_in, 16)
            flat = lg[:].rearrange("p a b -> p (a b)")
            q, p2 = expm1_parts(flat, 2 * P)
            exf = ex[:].rearrange("p a b -> p (a b)")
            link(v.tensor_tensor(exf, q, p2, ALU.mult))
            link(v.tensor_tensor(exf, exf, p2, ALU.add))
            dt, mw = ex[:, 0, :], ex[:, 1, :]
            link(v.scalar_tensor_tensor(rho[:], mw, -1.0, dt, ALU.mult, ALU.mult))
            assert links[0] == CH_RHO, links
            link(v.tensor_tensor(turn[:], wim[:], dt, ALU.mult))
            link(v.tensor_scalar(turn[:], turn[:], 0.15915494309189535, None, ALU.mult))
            link(v.tensor_tensor(ang[:], turn[:].unsqueeze(1).to_broadcast([P, NL, P]),
                                 cst[:, C_L:C_L + NL].unsqueeze(2).to_broadcast([P, NL, P]), ALU.mult))
            link(v.tensor_scalar(sn[:], ang[:], ROUND, ROUND, ALU.add, ALU.subtract))
            link(v.tensor_tensor(ang[:], ang[:], sn[:], ALU.subtract))
            assert links[0] == CH_TURN, links
            link(v.tensor_copy(t0[:], rho[:]))
            q, p2 = expm1_parts(t0[:], P)
            link(v.tensor_tensor(em1[:], q, p2, ALU.mult))
            link(v.scalar_tensor_tensor(em1[:], p2, -1.0, em1[:], ALU.add, ALU.add))
            link(v.tensor_tensor(nrm[:], mw, mw, ALU.mult))
            link(v.tensor_tensor(t0[:], wim[:], wim[:], ALU.mult))
            link(v.tensor_tensor(nrm[:], nrm[:], t0[:], ALU.add))
            link(v.reciprocal(nrm[:], nrm[:]))
            link(v.tensor_scalar(nrm[:], nrm[:], 2.0, None, ALU.mult))
            dve.wait_ge(act_tab, 3)
            link(v.tensor_tensor(t0[:], half[:], half[:], ALU.mult))
            link(v.scalar_tensor_tensor(ai[:], em1[:], 1.0, sn[:, 1, :], ALU.add, ALU.mult))
            dve.wait_ge(act_tab, 5)
            link(v.tensor_tensor(ar[:], em1[:], ang[:, 1, :], ALU.mult))
            lb = slice(0, LB1 + LB2)
            v.tensor_tensor(ang[:, lb, :], ang[:, lb, :], mag[:, lb, :], ALU.mult).then_inc(tab_ready, 1)
            v.tensor_tensor(sn[:, lb, :], sn[:, lb, :], mag[:, lb, :], ALU.mult).then_inc(tab_ready, 1)
            link(v.scalar_tensor_tensor(ar[:], t0[:], -2.0, ar[:], ALU.mult, ALU.add))
            v.tensor_tensor(dr[:], ai[:], wim[:], ALU.mult)
            v.tensor_tensor(t0[:], ar[:], mw, ALU.mult)
            v.tensor_tensor(di[:], ai[:], mw, ALU.mult)
            link(v.tensor_tensor(em1[:], ar[:], wim[:], ALU.mult))
            v.tensor_tensor(dr[:], dr[:], t0[:], ALU.subtract)
            link(v.tensor_tensor(di[:], di[:], em1[:], ALU.add))
            link(v.scalar_tensor_tensor(di[:], di[:], -1.0, nrm[:], ALU.mult, ALU.mult))
            v.tensor_tensor(dr[:], dr[:], nrm[:], ALU.mult).then_inc(d_ready0, 1)
            la = slice(LB1 + LB2, NL)
            drb = dr[:].unsqueeze(1).to_broadcast([P, LA, P])
            dib = di[:].unsqueeze(1).to_broadcast([P, LA, P])
            dve.wait_ge(d_ready0, 1)
            dve.wait_ge(pool_ready, 2)
            v.tensor_tensor(mag[:, la, :], ang[:, la, :], drb, ALU.mult)
            link(v.tensor_tensor(pt3[:], sn[:, la, :], dib, ALU.mult))
            v.tensor_tensor(mag[:, la, :], mag[:, la, :], pt3[:], ALU.subtract).then_inc(p_ready, 1)
            link(v.tensor_tensor(sn[:, la, :], sn[:, la, :], drb, ALU.mult))
            dve.wait_ge(pool_ready, 3)
            v.scalar_tensor_tensor(sn[:, la, :].rearrange("p a h -> p (a h)"), sn[:, la, :].rearrange("p a h -> p (a h)"),
                                   -1.0, pt2[:].rearrange("p a h -> p (a h)"), ALU.mult, ALU.subtract).then_inc(p_ready, 1)

            dve.wait_ge(gate_in, 80)
            for k in range(KC):
                sel = fw[:, k, 0:NE * SE].rearrange("p (n s) -> p n s", n=NE)
                mean = fw[:, k, NE * SE:NE * SE + NE]
                upd = fw[:, k, NE * SE + NE:FC].rearrange("p (n h) -> p n h", n=NE)
                row = pw[:, k, 0:FC]
                v.tensor_tensor(row[:, 0:64].rearrange("p (n s) -> p n s", n=NE), sel,
                                mean.unsqueeze(2).to_broadcast([P, NE, SE]), ALU.mult)
                v.tensor_tensor(row[:, 64:72], mean, mean, ALU.mult)
                v.tensor_tensor(row[:, 72:FC].rearrange("p (n h) -> p n h", n=NE), upd,
                                dbs[:, k, :].unsqueeze(2).to_broadcast([P, NE, HE]), ALU.mult).then_inc(pw_done, 1)

            dve.wait_ge(tab_in[0], 16 * 12)
            dve.wait_ge(mix_in, 32)
            def chunk(it, s):
                hs = bass.ds(it * (2 * CH) + s * CH, CH)

                def outer(left, right):
                    return (left[:, :, hs].rearrange("p e h -> p h e").unsqueeze(3).to_broadcast([P, CH, LB1, LB2]),
                            right[:, :, hs].rearrange("p e h -> p h e").unsqueeze(2).to_broadcast([P, CH, LB1, LB2]))

                grid = lambda t: t[:].rearrange("p h (i j) -> p h i j", i=LB1)
                v.tensor_tensor(grid(bt[s]), *outer(re1, u2), ALU.mult)
                if not isinstance(it, int) or s:
                    dve.wait_ge(b_ready, it * 2 + s)
                v.tensor_tensor(grid(tmp), *outer(im1, v2), ALU.mult).then_inc(t2_done, 1)
                first = bass.ds(it * (2 * CH) + s * CH, G1_DVE)
                v.tensor_tensor(g1[s][:, 0:G1_DVE, :].rearrange("p h (c a) -> p h c a", c=NB),
                                mc[:, first, :].unsqueeze(3).to_broadcast([P, G1_DVE, NB, LA]),
                                pre[:, :, first].rearrange("p a h -> p h a").unsqueeze(2).to_broadcast([P, G1_DVE, NB, LA]),
                                ALU.mult)
                dve.wait_ge(t2_done, it * 2 + (s + 1))
                v.tensor_tensor(bt[s][:], bt[s][:], tmp[:], ALU.add).then_inc(b_ready, 1)

            for s in range(2):
                chunk(0, s)
            for hh in range(2):
                if hh:
                    dve.wait_ge(tab_in[1], 16 * 12)
                with dve.Fori(hh * NCH // 4 or 1, (hh + 1) * NCH // 4) as it:
                    for s in range(2):
                        dve.wait_ge(mixed, it * 4 + (2 * s - 2))
                        chunk(it, s)

            dve.wait_ge(x_tile0, 16)
            dve.wait_ge(x_first, 16)
            def norm_stats(src, m):
                for t in range(TT):
                    v.bn_stats(stats[:, t, :], src(t)).then_inc(ln_st, 1)
                wait_apart(dve, ln_st, m * 2 + 2, 4)
                for t in range(TT):
                    last = v.bn_aggr(mv[:, t, :], stats[:, t, :])
                last.then_inc(ln_var, 1)

            def norm_apply(src, m, second=False):
                dve.wait_ge(ln_rstd, m + 1)
                if second:
                    if isinstance(m, int) and m == NB:
                        dve.wait_ge(w_lo, NCK * NG)
                    else:
                        dve.wait_ge(xn_added, m * 2 - 2 * NB)
                if not isinstance(m, int) or m:
                    dve.wait_ge(xt_ready, m * 2)
                for t in range(TT):
                    last = v.tensor_scalar(xn[:, t, :], src(t), mv[:, t, 0:1], rstd[:, t:t + 1], ALU.subtract, ALU.mult)
                last.then_inc(xn_ready, 1)

            def tokens(b):
                return lambda t: x[:, t, b, :]

            def xt_rest(b):
                for q in range(2):
                    dve.wait_ge(xt_hi, b * 2 + (q + 1))
                    v.tensor_tensor(xt_l[:, b, 2 * q:2 * q + 2, :].rearrange("p k s -> p (k s)"), banks[5 + q][:],
                                    xt_h[:, b, 2 * q:2 * q + 2, :].rearrange("p k s -> p (k s)").bitcast(F32),
                                    ALU.subtract).then_inc(xt_lo, 1)

            def rope(s, j):
                view, table, _, _ = rope_view(j)
                src = banks[j][:, 0:S] if j == 0 else banks[j][:].rearrange("p (h s) -> p h s", h=2)
                dve.wait_ge(swapped, s * 3 + (j + 1))
                v.tensor_tensor(view(kq), src, table(cosT), ALU.mult).then_inc(kq_cos, 1)

            def rope_add(s, j):
                view, _, _, _ = rope_view(j)
                dve.wait_ge(rot_sin, s * 3 + (j + 1))
                dve.wait_ge(kq_cos, s * 3 + (j + 1))
                v.tensor_tensor(view(kq), view(kq), view(sw), ALU.add).then_inc(kq_rot, 1)

            def v_rest(s):
                dve.wait_ge(v_hi, s + 1)
                v.tensor_tensor(vl[:].rearrange("p t d -> p (t d)"), banks[2][:, 0:S],
                                vh[:].rearrange("p t d -> p (t d)").bitcast(F32), ALU.subtract).then_inc(v_lo, 1)

            norm_stats(tokens(0), 0)
            norm_apply(tokens(0), 0)
            xt_rest(0)
            norm_stats(tokens(1), 1)
            norm_apply(tokens(1), 1)
            rope(0, 0)
            rope(0, 1)
            rope_add(0, 0)
            xt_rest(1)
            rope(0, 2)
            rope_add(0, 1)
            rope_add(0, 2)
            dve.wait_ge(x_rest, 16)
            norm_stats(tokens(2), 2)
            norm_apply(tokens(2), 2)

            def add_output(i, b):
                for t in range(TT):
                    dve.wait_ge(o_ready, i * 2 + (t + 1))
                    v.tensor_tensor(x[:, t, b, :], banks[3 + t][:], x[:, t, b, :], ALU.add).then_inc(x_added, 1)

            def gate_read(bb):
                f = banks[0][:].rearrange("p (t c) -> p t c", t=TT)
                dve.wait_ge(cw_done, 1)
                dve.wait_ge(f_ready, bb + 1)
                v.tensor_tensor(gu[:], f[:, :, 0:64], cw[:, 0:64].unsqueeze(1).to_broadcast([P, TT, 64]), ALU.subtract)
                v.scalar_tensor_tensor(gs[0][:], f[:, :, 64:72], -2.0, cw[:, 64:72].unsqueeze(1).to_broadcast([P, TT, NE]),
                                       ALU.mult, ALU.add)
                v.tensor_tensor(gm[:], f[:, :, 72:FC], cw[:, 72:FC].unsqueeze(1).to_broadcast([P, TT, 64]),
                                ALU.subtract).then_inc(f_read, 1)

            def gates(bb):
                n = [0]

                def then(ins):
                    n[0] += 1
                    ins.then_inc(gate, 1)
                    dve.wait_ge(gate, bb * GATE + n[0])

                score, z, rank = gs[0][:], gs[1][:], gs[2][:]
                one_minus, ssq, best, first = (t[:] for t in g1x)
                bc = lambda t: t.unsqueeze(2).to_broadcast([P, TT, NE])
                dve.wait_ge(f_read, bb + 1)
                v.tensor_tensor(gu[:], gu[:], gu[:], ALU.mult)
                then(v.tensor_tensor(ssq, rstd[:], rstd[:], ALU.mult))
                v.tensor_reduce(z, gu[:].rearrange("p t (n s) -> p t n s", n=NE), AX.X, ALU.add)
                then(v.scalar_tensor_tensor(ssq, mv[:, :, 1], float(D), ssq, ALU.mult, ALU.mult))
                then(v.tensor_tensor(score, score, bc(ssq), ALU.add))
                then(v.reciprocal(score, score))
                then(v.tensor_tensor(z, z, score, ALU.mult))
                then(v.tensor_tensor(z, z, ctr[:].unsqueeze(1).to_broadcast([P, TT, NE]), ALU.subtract))
                then(v.tensor_tensor(z, z, slp[:].unsqueeze(1).to_broadcast([P, TT, NE]), ALU.mult))
                assert n[0] == GATE_Z
                dve.wait_ge(e_ready, bb + 1)
                then(v.tensor_scalar(z, z, 1.0, None, ALU.add))
                then(v.reciprocal(z, z))
                then(v.tensor_reduce(best, z, AX.X, ALU.max))
                then(v.tensor_tensor(rank, z, bc(best), ALU.is_equal))
                then(v.tensor_tensor(rank, rank, cst[:, C_RANK:C_RANK + NE].unsqueeze(1).to_broadcast([P, TT, NE]),
                                     ALU.mult))
                then(v.tensor_reduce(first, rank, AX.X, ALU.max))
                onehot = mm[:, :, 64:72]
                then(v.tensor_tensor(onehot, rank, bc(first), ALU.is_equal))
                then(v.tensor_scalar(one_minus, best, -1.0, 1.0, ALU.mult, ALU.add))
                v.tensor_tensor(mm[:, :, 0:64].rearrange("p t (n h) -> p t n h", n=NE),
                                gm[:].rearrange("p t (n h) -> p t n h", n=NE),
                                onehot.unsqueeze(3).to_broadcast([P, TT, NE, HE]), ALU.mult).then_inc(m_ready, 1)
                assert n[0] == GATE, n

            def finish(bb):
                best = g1x[2]
                dve.wait_ge(xn_added, bb * 2 + 2)
                for t in range(TT):
                    dve.wait_ge(d_ready, bb * 2 + (t + 1))
                    v.scalar_tensor_tensor(x[:, t, bb, :], banks[5 + t][:], best[:, t:t + 1], x[:, t, bb, :],
                                           ALU.mult, ALU.add).then_inc(out_ready, 1)

            def attn_rest(i, j):
                dve.wait_ge(ot_hi, i * 2 + (j + 1))
                hs = slice(2 * j, 2 * j + 2)
                v.tensor_tensor(otl[:, hs, :].rearrange("p h s -> p (h s)"), banks[j][:],
                                oth[:, hs, :].rearrange("p h s -> p (h s)").bitcast(F32),
                                ALU.subtract).then_inc(ot_lo, 1)

            def step(g, b, at):
                i = b + 8 * g
                final = g == NG - 1 and at == NB - 1
                for j in range(QH):
                    wait_apart(dve, s_ready, i * 4 + (j + 1), j)
                    for t, cols, m in ((0, slice(0, P), mask[:, P:2 * P]), (1, slice(P, 3 * P), mask)):
                        n = 2 * j + t
                        last = v.tensor_tensor_reduce(out=sm[:, j, cols], in0=banks[3 + j][:, cols], in1=m,
                                                      scale=-SCALE, scalar=3.0e38, op0=ALU.add, op1=ALU.min,
                                                      accum_out=mx[:, n:n + 1])
                    last.then_inc(s_masked, 1)
                    if j == 1 and (g or at):
                        attn_rest(i - 1, 1)
                v_rest(i)
                if needs_norm1(g, at):
                    norm_stats(tokens(b + 3), b + 3)
                if needs_ffn(g, at):
                    norm_apply(tokens(b - 2), b + (NB - 2), second=True)
                dve.wait_ge(p_exp, i * 4 + 2)
                v.reciprocal(rinv[:, 0:4], rsum[:, 0:4]).then_inc(r_ready, 1)
                dve.wait_ge(p_exp, i * 4 + 4)
                v.reciprocal(rinv[:, 4:8], rsum[:, 4:8]).then_inc(r_ready, 1)
                if not final:
                    rope(i + 1, 0)
                if needs_finish(g, at):
                    finish(b - 3)
                if not final:
                    rope(i + 1, 1)
                    rope_add(i + 1, 0)
                if needs_xt(g, at):
                    xt_rest(b + 2)
                if not final:
                    rope(i + 1, 2)
                    rope_add(i + 1, 1)
                    rope_add(i + 1, 2)
                if needs_norm1(g, at):
                    norm_apply(tokens(b + 3), b + 3)
                if needs_ffn(g, at):
                    gate_read(b - 2)
                for j in range(3):
                    dve.wait_ge(pt_hi, i * 3 + (j + 1))
                    v.tensor_tensor(ptl[:, j, :], banks[5 + j][:], pth[:, j, :].bitcast(F32),
                                    ALU.subtract).then_inc(pt_lo, 1)
                if needs_ffn(g, at):
                    gates(b - 2)
                if not (g == 0 and at == 0):
                    add_output(i - 1, (b - 1) if at else NB - 1)
                if needs_norm2(g, at):
                    wait_apart(dve, x_added, i * 2, 5)
                    norm_stats(tokens(b - 1), b + (NB - 1))
                attn_rest(i, 0)

            steps(dve, step)
            last = NG * NB - 1
            attn_rest(last, 1)
            norm_apply(tokens(NB - 2), 2 * NB - 2, second=True)
            finish(NB - 3)
            gate_read(NB - 2)
            gates(NB - 2)
            add_output(last, NB - 1)
            dve.wait_ge(x_added, 2 * last + 2)
            norm_stats(tokens(NB - 1), 2 * NB - 1)
            norm_apply(tokens(NB - 1), 2 * NB - 1, second=True)
            finish(NB - 2)
            gate_read(NB - 1)
            gates(NB - 1)
            finish(NB - 1)

        @block.tensor
        def _(pe):
            mmul = nc.tensor.matmul

            def split_product(dst, parts, start=True, stop=True):
                n = len(parts)
                for k, (lh, ll, rh, rl) in enumerate(parts):
                    mmul(dst, lh, rh, start=start and k == 0, stop=False, skip_group_check=True)
                    mmul(dst, ll, rh, start=False, stop=False, skip_group_check=True)
                    last = mmul(dst, lh, rl, start=False, stop=stop and k == n - 1, skip_group_check=True)
                return last

            pe.wait_ge(pw_done, KC)
            for k in range(KC):
                last = mmul(banks[7][:, 0:FC], ones[:], pw[:, k, 0:FC], start=k == 0, stop=k == KC - 1)
            last.then_inc(cw_mm, 1)

            def chunk(s):
                for m in range(CH // 2):
                    hs = slice(2 * m, 2 * m + 2)
                    flat = lambda t: t[:, hs, :].rearrange("p h j -> p (h j)")
                    dst = banks[2 * s + m // 4][:, (m % 4) * P:(m % 4 + 1) * P]
                    mmul(dst, flat(g1[s]), flat(bt[s]), start=m % 4 == 0, stop=False, skip_group_check=True)
                    last = mmul(dst, flat(g2[s]), flat(bt[s]), start=False, stop=m % 4 == 3, skip_group_check=True)
                    if m % 4 == 3:
                        last.then_inc(mixed, 1)

            for s in range(2):
                pe.wait_ge(b_ready, s + 1)
                pe.wait_ge(g2_ready, s + 1)
                chunk(s)
            with pe.Fori(1, NCH // 2) as it:
                for s in range(2):
                    pe.wait_ge(b_ready, it * 2 + (s + 1))
                    pe.wait_ge(g2_ready, it * 2 + (s + 1))
                    pe.wait_ge(evac, it * 2 + (s - 1))
                    chunk(s)

            def transpose_tokens(m):
                for q in range(2):
                    for k in range(2):
                        for t in range(TT):
                            col = (2 * q + k) * P
                            last = nc.tensor.transpose(banks[5 + q][:, k * S + t * P:k * S + (t + 1) * P],
                                                       xn[:, t, col:col + P], ident)
                    last.then_inc(xt_ready, 1)

            def project(s, b, first, after_kv, before_last):
                def parts(c):
                    cols = slice(c * HD, (c + 1) * HD)
                    return [(wk[:, k, cols], wl[:, k, cols], xt_h[:, b, k, :], xt_l[:, b, k, :]) for k in range(KC)]
                if not first:
                    pe.wait_ge(ot_lo, s * 2 - 3)
                split_product(banks[0][:, 0:S], parts(0))
                split_product(banks[0][:, S:2 * S], parts(1)).then_inc(proj, 1)
                after_kv()
                for j in range(2):
                    if j == 0 and not first:
                        pe.wait_ge(ot_lo, s * 2 - 2)
                    if j == 1 and (not isinstance(s, int) or s):
                        pe.wait_ge(v_lo, s)
                    if j == 1:
                        before_last()
                    for h in range(2):
                        last = split_product(banks[1 + j][:, h * S:(h + 1) * S], parts(2 + 2 * j + h))
                    last.then_inc(proj, 1)

            def transpose_v(s):
                pe.wait_ge(swapped, s * 3 + 3)
                pe.wait_ge(kq_cos, s * 3 + 3)
                for t in range(TT):
                    last = nc.tensor.transpose(banks[2][:, t * P:(t + 1) * P], vt[:, t * P:(t + 1) * P], ident)
                last.then_inc(vt_ready, 1)

            def gate_product(bb):
                for t in range(TT):
                    for k in range(KC):
                        last = mmul(banks[0][:, t * S:t * S + FC], xnt[:, k, t * P:(t + 1) * P], fw[:, k, :],
                                    start=k == 0, stop=k == KC - 1)
                last.then_inc(f_ready, 1)

            def update_rows(bb):
                pe.wait_ge(m_ready, bb + 1)
                for t in range(TT):
                    last = nc.tensor.transpose(banks[7][0:MC, t * P:(t + 1) * P], mm[:, t, :], ident)
                last.then_inc(mt_ready, 1)

            def update_product(bb):
                pe.wait_ge(mt_done, bb + 1)
                for t in range(TT):
                    mmul(banks[5 + t][:], mt[:, t * P:(t + 1) * P], dw[:], start=True, stop=True).then_inc(d_ready, 1)

            def out_product(i):
                for t in range(TT):
                    parts = [(oth[:, h, t * P:(t + 1) * P], otl[:, h, t * P:(t + 1) * P], woh[:, h, :], wol[:, h, :])
                             for h in range(QH)]
                    split_product(banks[3 + t][:], parts).then_inc(o_ready, 1)

            pe.wait_ge(cst_in, 16)
            def first_tokens(b):
                pe.wait_ge(xn_ready, b + 1)
                if b:
                    pe.wait_ge(xt_lo, 2 * b)
                transpose_tokens(b)

            first_tokens(0)
            pe.wait_ge(w_lo, KC)
            pe.wait_ge(xt_lo, 2)
            project(0, 0, True, lambda: None, lambda: first_tokens(1))
            transpose_v(0)

            def step(g, b, at):
                i = b + 8 * g
                final = g == NG - 1 and at == NB - 1
                pe.wait_ge(kq_lo, i * 3 + 3)
                for j in range(QH):
                    if j == 0 and (g or at > 1):
                        pe.wait_ge(x_added, i * 2 - 2)
                    if j == 2:
                        if g or at:
                            pe.wait_ge(pt_lo, i * 3)
                        else:
                            pe.wait_ge(xt_lo, 4)
                    bank = banks[3 + j]
                    mmul(bank[:, 0:P], kq[:, 1 + j, 0:P], kq[:, 0, 0:P], start=True, stop=True, skip_group_check=True)
                    qs = slice(S + j * P, S + (j + 1) * P)
                    split_product(bank[:, P:3 * P], [(kh[:, qs], kl[:, qs], kh[:, 0:S], kl[:, 0:S])]).then_inc(s_ready, 1)

                def tokens():
                    if needs_xt(g, at):
                        pe.wait_ge(xn_ready, b + 3)
                        pe.wait_ge(s_masked, i * 4 + 4)
                        transpose_tokens(b + 2)
                    if needs_ffn(g, at):
                        pe.wait_ge(xn_ready, b + (NB - 1))
                        pe.wait_ge(s_masked, i * 4 + 4)
                        if at > 2:
                            pe.wait_ge(out_ready, b * 2 - 4)
                        transpose_tokens(b + (NB - 2))

                def last_update():
                    if needs_finish(g, at):
                        pe.wait_ge(s_masked, i * 4 + 4)
                        update_product(b - 3)

                if not final:
                    if g == 0 and at < NB - 1:
                        pe.wait_ge(xt_lo, b * 2 + 4)
                    if at == NB - 1:
                        pe.wait_ge(w_lo, (g + 1) * NCK + KC)
                    project(i + 1, (b + 1) if at < NB - 1 else 0, g == 0 and at == 0, last_update, tokens)
                else:
                    last_update()
                    tokens()
                if needs_ffn(g, at):
                    pe.wait_ge(xt_hi, b * 2 + (2 * NB - 2))
                    if final:
                        pe.wait_ge(ot_lo, i * 2)
                    else:
                        pe.wait_ge(swapped, i * 3 + 4)
                        pe.wait_ge(kq_cos, i * 3 + 4)
                    gate_product(b - 2)
                for j in range(2):
                    pe.wait_ge(p_norm, i * 4 + (2 * j + 2))
                    if j == 0:
                        if g or at:
                            pe.wait_ge(pt_lo, i * 3)
                        if needs_xt(g, at):
                            pe.wait_ge(xt_lo, b * 2 + 6)
                        if needs_ffn(g, at):
                            pe.wait_ge(xt_hi, b * 2 + (2 * NB - 2))
                    for h in range(2):
                        for t in range(2):
                            last = nc.tensor.transpose(banks[5 + j][:, h * S + t * P:h * S + (t + 1) * P],
                                                       sm[:, 2 * j + h, t * P:(t + 1) * P], ident)
                    last.then_inc(tr_ready, 1)
                for h in range(QH):
                    last = nc.tensor.transpose(banks[7][:, h * P:(h + 1) * P], sm[:, h, 2 * P:3 * P], ident)
                last.then_inc(tr_ready, 1)
                if g or at:
                    pe.wait_ge(s_masked, i * 4 + 4)
                    pe.wait_ge(ot_lo, i * 2)
                    if at == 1:
                        pe.wait_ge(w_lo, g * NCK + NCK)
                    out_product(i - 1)
                if not final:
                    transpose_v(i + 1)
                pe.wait_ge(pt_lo, i * 3 + 3)
                pe.wait_ge(v_lo, i + 1)
                if not final:
                    pe.wait_ge(swapped, i * 3 + 6)
                    pe.wait_ge(kq_cos, i * 3 + 6)
                elif g or at:
                    pe.wait_ge(ot_lo, i * 2)
                if needs_ffn(g, at):
                    pe.wait_ge(f_read, b - 1)
                for j in range(2):
                    split_product(banks[j][:], [(vh[:, 0, :], vl[:, 0, :], pth[:, j, :], ptl[:, j, :])], stop=False)
                    second = banks[j][:].rearrange("p (h s) -> p h s", h=2)[:, :, P:S]
                    cols = slice(j * S, (j + 1) * S)
                    split_product(second, [(vh[:, 1, :], vl[:, 1, :], pth[:, 2, cols].rearrange("p (h s) -> p h s", h=2),
                                            ptl[:, 2, cols].rearrange("p (h s) -> p h s", h=2))],
                                  start=False).then_inc(pv_ready, 1)
                if needs_ffn(g, at):
                    update_rows(b - 2)

            steps(pe, step)
            last = NG * NB - 1
            update_product(NB - 3)
            for bb in (NB - 2, NB - 1):
                pe.wait_ge(xn_ready, NB + bb + 1)
                pe.wait_ge(out_ready, 2 * bb)
                transpose_tokens(NB + bb)
                pe.wait_ge(xt_hi, 2 * (NB + bb) + 2)
                pe.wait_ge(ot_lo, 2 * last + 2)
                pe.wait_ge(f_read, bb)
                gate_product(bb)
                if bb == NB - 2:
                    out_product(last)
                update_rows(bb)
                update_product(bb)


def kernel(x, L0_tok_log_dt, L0_tok_log_w_real, L0_tok_w_imag, L0_attn_w_q, L0_attn_w_k, L0_attn_w_v, L0_attn_w_o,
           L0_ffn_select_weight, L0_ffn_select_mean_diff, L0_ffn_imp_center, L0_ffn_imp_slope, L0_ffn_lora_update,
           L0_ffn_lora_degen, L0_ffn_bias_w, L0_ffn_debias_w):
    import concourse.bacc as bacc
    from concourse.bass_utils import run_bass_kernel_spmd

    def a(v):
        return np.asarray(v)

    by_row = a(x).transpose(3, 2, 1, 0)
    wq = a(L0_attn_w_q).reshape(KC, P, NG, QH * HD).transpose(2, 0, 1, 3)
    wk = a(L0_attn_w_k).reshape(KC, P, NG, HD).transpose(2, 0, 1, 3)
    wv = a(L0_attn_w_v).reshape(KC, P, NG, HD).transpose(2, 0, 1, 3)

    def chunks(w):
        return w.reshape(KC, P, -1).transpose(1, 0, 2)

    arrays = {
        "mix_c": by_row.reshape(P, S, NB),
        "mix_s": by_row[::-1].reshape(P, S, NB),
        "log_dt": a(L0_tok_log_dt),
        "log_wr": a(L0_tok_log_w_real).reshape(2, P, NS).transpose(0, 2, 1).reshape(P, P),
        "w_im": a(L0_tok_w_imag).reshape(2, P, NS).transpose(0, 2, 1).reshape(P, P),
        "w_qkv": np.concatenate([wk, wv, wq], axis=-1),
        "w_o": a(L0_attn_w_o).reshape(NG, QH, HD, D),
        "w_gate": np.concatenate([chunks(a(L0_ffn_select_weight).transpose(1, 0, 2)),
                                  chunks(a(L0_ffn_select_mean_diff).T),
                                  chunks(a(L0_ffn_lora_update).transpose(1, 0, 2))], axis=-1),
        "w_gmul": chunks(a(L0_ffn_debias_w).T),
        "w_upd": np.concatenate([a(L0_ffn_lora_degen).transpose(0, 2, 1).reshape(NE * HE, D), a(L0_ffn_bias_w)]),
        "centers": a(L0_ffn_imp_center),
        "slopes": a(L0_ffn_imp_slope),
        "consts": constants(),
    }
    nc = bacc.Bacc("TRN2", target_bir_lowering=False, num_devices=1)
    args, sent = [], {}
    for name, v in arrays.items():
        v = np.ascontiguousarray(v)
        sent[f"in_{name}"] = v
        args.append(nc.dram_tensor(f"in_{name}", v.shape, mybir.dt.from_np(v.dtype), kind="ExternalInput").ap())
    out = nc.dram_tensor("out_0", (NB, S, D), F32, kind="ExternalOutput").ap()
    tower(nc, *args, out)
    r = run_bass_kernel_spmd(nc, [sent], core_ids=[0])
    return r.results[0]["out_0"]
```

```python
from contextlib import ExitStack

import numpy as np
import concourse.bass as bass
from concourse import mybir

F32 = mybir.dt.float32
F32R = mybir.dt.float32r
I32 = mybir.dt.int32
ALU = mybir.AluOpType
ACT = mybir.ActivationFunctionType
AX = mybir.AxisListType

P = 128
NB = 8
S = 256
D = 512
NS = 64
NH, NKV, HD = 16, 4, 128
NG = NKV
QH = NH // NKV
KC = D // P
TT = S // P
WC = HD + HD + QH * HD
NE, SE, HE = 8, 8, 8
FC = NE * SE + NE + NE * HE
MC = NE * HE + NE
LA, LB1, LB2 = 8, 8, 8
NL = LA + LB1 + LB2
ROWS_B, ROWS_A = slice(0, LB1 + LB2), slice(LB1 + LB2, NL)
CH = 16
NCH = S // CH
G1_DVE = 6
EPS = 1e-5
SCALE = float(HD) ** -0.5
MASKED = -1e30
ROUND = 1.5 * 2.0 ** 23

C_COS, C_SIN, C_MASK, C_ID, C_L, C_RANK, C_ONES, C_QUARTER, C_POW = 0, 256, 512, 768, 896, 920, 928, 1056, 1057
C_ALL = 1059


def constants():
    inv = (1.0 / 10000.0 ** (np.arange(0, HD, 2) / HD)).astype(np.float32)
    ang = (np.arange(S, dtype=np.float32)[None, :] * np.concatenate([inv, inv])[:, None]).astype(np.float32)
    c = np.zeros((P, C_ALL), np.float32)
    c[:, C_COS:C_COS + S] = np.cos(ang.astype(np.float64))
    sign = np.where(np.arange(HD) < HD // 2, -1.0, 1.0)[:, None]
    c[:, C_SIN:C_SIN + S] = sign * np.sin(ang.astype(np.float64))
    q, k = np.arange(P)[:, None], np.arange(P)[None, :]
    c[:, C_MASK + P:C_MASK + 2 * P] = np.where(k <= q, 0.0, MASKED)
    c[:, C_ID:C_ID + P] = np.eye(P)
    c[:, C_L:C_L + NL] = np.concatenate([np.arange(8), 8 * np.arange(8), 64 * np.arange(8)])[None, :]
    c[:, C_RANK:C_RANK + NE] = (NE - np.arange(NE))[None, :]
    c[:, C_ONES:C_ONES + P] = 1.0
    c[:, C_QUARTER] = np.pi / 2
    c[:, C_POW:C_POW + TT] = -0.5
    return c


NCK = KC + QH

CH_RHO, CH_TURN, CH_FRACTION, CH_ROUND_A = 16, 18, 21, 23
GATE, GATE_Z = 15, 7


def rope_view(j):
    if j == 0:
        return (lambda t: t[:, 0, :]), (lambda c: c), (lambda t: t[:, 0, :]), (lambda t: t[:, 0:S])
    h = slice(2 * j - 1, 2 * j + 1)
    return ((lambda t: t[:, h, :]), (lambda c: c.unsqueeze(1).to_broadcast([P, 2, S])), (lambda t: t[:, h, P:S]),
            (lambda t: t[:, j * S:(j + 1) * S].rearrange("p (h q) -> p h q", h=2)))


RUNS = [
    [(0, 1), (1, 2), (2, 5), (5, 6), (6, 7), (7, 8)],
    [(0, 1), (1, 6), (6, 7), (7, 8)],
    [(0, 1), (1, 6), (6, 7), (7, 8)],
    [(0, 1), (1, 2), (2, 3), (3, 7)],
]


def steps(engine, body):
    for g in range(NG):
        for lo, hi in RUNS[g]:
            if hi - lo == 1:
                body(g, lo, lo)
            else:
                with engine.Fori(lo, hi) as b:
                    body(g, b, lo)


def needs_xt(g, at):
    return g == 0 and at <= 5


def needs_norm1(g, at):
    return g == 0 and at <= 4


def needs_ffn(g, at):
    return g == NG - 1 and at >= 2


def needs_norm2(g, at):
    return g == NG - 1 and at >= 1


def needs_finish(g, at):
    return g == NG - 1 and at >= 3


def tower(nc, mix_c, mix_s, log_dt, log_wr, w_im, w_qkv, w_o, w_gate, w_gmul, w_upd, centers, slopes, consts, out):
    x_dram = nc.dram_tensor("mixed", [S, NB, D], F32, kind="Internal").ap()
    top = ExitStack()
    with top:
        def sem(name):
            return top.enter_context(nc.semaphore(name))

        def sb(name, shape, dt=F32, stack=top):
            return stack.enter_context(nc.sbuf_tensor(name, shape, dt))

        banks = [top.enter_context(nc.psum_tensor(f"bank{k}", [P, 512], F32)) for k in range(8)]

        x = sb("x", [P, TT, NB, D])
        wk = sb("w_hi", [P, KC, WC], F32R)
        wl = sb("w_lo", [P, KC, WC], F32R)
        raw = sb("raw", [P, 2, WC])
        cst = sb("cst", [P, C_ALL])
        cosT = cst[:, C_COS:C_COS + S]
        sinT = cst[:, C_SIN:C_SIN + S]
        mask = cst[:, C_MASK:C_MASK + 2 * P]
        ident = cst[:, C_ID:C_ID + P]
        ones = cst[:, C_ONES:C_ONES + P]
        fw = sb("fw", [P, KC, FC])
        dw = sb("dw", [MC, D])
        cw = sb("cw", [P, FC])
        dbs = sb("dbs", [P, KC, NE])
        spare = sb("spare", [1, 9])
        ctr = sb("ctr", [P, NE])
        slp = sb("slp", [P, NE])

        mixer = ExitStack()
        ta = [sb(f"ta{k}", [P, 8, S], F32, mixer) for k in range(6)]
        re1, im1, u2, v2, pre, pim = ta
        mc = sb("mc", [P, S, NB], F32, mixer)
        ms = sb("ms", [P, S, NB], F32, mixer)
        ang = sb("ang", [P, NL, P], F32, mixer)
        sn = sb("sn", [P, NL, P], F32, mixer)
        mag = sb("mag", [P, NL, P], F32, mixer)
        bt = [sb(f"bt{k}", [P, CH, 64], F32, mixer) for k in range(2)]
        g1 = [sb(f"g1{k}", [P, CH, 64], F32, mixer) for k in range(2)]
        g2 = [sb(f"g2{k}", [P, CH, 64], F32, mixer) for k in range(2)]
        tmp = sb("tmp", [P, CH, 64], F32, mixer)
        st = [sb(f"st{k}", [P, CH // 2, 64], F32, mixer) for k in range(2)]
        mixer.close()

        small = ExitStack()
        hold = [sb(f"hold{k}", [P, 8, S], F32, small) for k in range(6)]
        hold += [sb(f"holdm{k}", [P, S, NB], F32, small) for k in range(2)]
        hold += [sb(f"holdn{k}", [P, NL, P], F32, small) for k in range(3)]
        lg = sb("lg", [P, 2, P], F32, small)
        ex = sb("ex", [P, 2, P], F32, small)
        kk = sb("kk", [P, 2, P], F32, small)
        rr = sb("rr", [P, 2, P], F32, small)
        qq = sb("qq", [P, 2, P], F32, small)
        ki = sb("ki", [P, 2, P], I32, small)
        wim = sb("wim", [P, P], F32, small)
        rho = sb("rho", [P, P], F32, small)
        turn = sb("turn", [P, P], F32, small)
        em1 = sb("em1", [P, P], F32, small)
        half = sb("half", [P, P], F32, small)
        ar = sb("ar", [P, P], F32, small)
        ai = sb("ai", [P, P], F32, small)
        dr = sb("dr", [P, P], F32, small)
        di = sb("di", [P, P], F32, small)
        nrm = sb("nrm", [P, P], F32, small)
        wsq = sb("wsq", [P, P], F32, small)
        t0 = sb("t0", [P, P], F32, small)
        pt2 = sb("pt2", [P, 8, P], F32, small)
        pt3 = sb("pt3", [P, 8, P], F32, small)
        small.close()

        sizes = {"mv": [TT, 2], "rstd": [TT], "gu": [TT, NE * SE], "gm": [TT, NE * HE], "mm": [TT, MC],
                 "score": [TT, NE], "z": [TT, NE], "rank": [TT, NE],
                 "one_minus": [TT], "ssq": [TT], "best": [TT], "first": [TT]}
        SET_SIZE = sum(int(np.prod(n)) for n in sizes.values())

        def carve(flat):
            views, at = {}, 0
            for name, shape in sizes.items():
                n = int(np.prod(shape))
                part = flat[:, at:at + n]
                views[name] = part if len(shape) == 1 else part.rearrange("p (t c) -> p t c", t=TT)
                at += n
            return views

        late = ExitStack()
        late_sets = []
        for k in range(2):
            views = carve(sb(f"late_set{k}", [P, SET_SIZE], F32, late)[:])
            views["xn"] = sb(f"late_xn{k}", [P, TT, D], F32, late)[:]
            late_sets.append(views)
        late.close()
        xt_h = sb("xt_hi", [P, NB, KC, S], F32R)
        xt_l = sb("xt_lo", [P, NB, KC, S], F32R)
        woh = sb("wo_hi", [P, QH, D], F32R)
        wol = sb("wo_lo", [P, QH, D], F32R)
        kq = sb("kq", [P, 1 + QH, S])
        kh = sb("kq_hi", [P, S + QH * P], F32R)
        kl = sb("kq_lo", [P, S + QH * P], F32R)
        sw = sb("swap", [P, 1 + QH, S])
        sm = sb("sm", [P, QH, 3 * P])
        pth = sb("pt_hi", [P, 3, 512], F32R)
        ptl = sb("pt_lo", [P, 3, 512], F32R)
        vt = sb("vt", [P, S])
        vh = sb("v_hi", [P, TT, HD], F32R)
        vl = sb("v_lo", [P, TT, HD], F32R)
        oth = sb("ot_hi", [P, QH, S], F32R)
        otl = sb("ot_lo", [P, QH, S], F32R)
        norm_mem = sb("norm_mem", [P, 2 * TT * D])
        xn = norm_mem[:, 0:TT * D].rearrange("p (t d) -> p t d", t=TT)
        xnt = norm_mem[:, TT * D:2 * TT * D].rearrange("p (k s) -> p k s", k=KC)
        stats = sb("stats", [P, TT, 6])
        mx = sb("mx", [P, 2 * QH])
        rsum = sb("rsum", [P, 2 * QH])
        rinv = sb("rinv", [P, 2 * QH])
        mt = sb("mt", [MC, S])

        norm_sets = [carve(sb("norm_set", [P, SET_SIZE])[:])] + late_sets
        norm_sets[0]["xn"] = xn

        def norm_set(m):
            return norm_sets[m - (2 * NB - 3)] if isinstance(m, int) and m > 2 * NB - 3 else norm_sets[0]

        pw = x[:, TT - 1, NB - KC:NB, 0:FC]
        neg2 = x[:, TT - 1, 0:LB2 * P // D, :].rearrange("p c (e h) -> p (c e) h", h=P)

        def raw_slot(n):
            if n < NCK:
                return n % 2
            return (n - NCK) % 4

        def raw_chunk(n):
            width = WC if n % NCK < KC else D
            k = raw_slot(n)
            return raw[:, k, 0:width] if k < 2 else norm_mem[:, (k - 2) * WC:(k - 2) * WC + width]

        def dve_splits(n):
            return n >= NCK and n % NCK == KC - 1

        def wait_split(engine, n):
            by_dve = sum(dve_splits(m) for m in range(n + 1))
            engine.wait_ge(w_lo, n + 1 - by_dve)
            if by_dve:
                engine.wait_ge(w_lo_dve, by_dve)

        def raw_turn(n):
            return sum(raw_slot(m) == raw_slot(n) for m in range(n + 1))

        cst_in, par_in, mix_in, gate_in = sem("cst_in"), sem("par_in"), sem("mix_in"), sem("gate_in")
        raw_in = [sem(f"raw_in{k}") for k in range(4)]
        w_hi, w_lo, w_lo_dve = sem("w_hi_done"), sem("w_lo_done"), sem("w_lo_dve_done")
        chain = sem("dve_chain")
        act_tab, tab_ready, neg_ready, p_ready, poles_d_ready = (
            sem("act_tables"), sem("tables_ready"), sem("negatives_ready"), sem("p_ready"), sem("d_of_poles_ready"))
        tab_in = [sem("tables_in0"), sem("tables_in1")]
        pool_ready, pool_norm = sem("pool_powers_ready"), sem("pool_norm_ready")
        pool_tab = sem("pool_tables")
        t2_done = sem("t2_done")
        b_ready, g2_ready, mixed, evac, xd_out = (
            sem("b_ready"), sem("g2_ready"), sem("mixed_ready"), sem("evacuated"), [sem("xd_out0"), sem("xd_out1")])
        x_tile0, x_first, x_second, x_rest = sem("x_tile0"), sem("x_first"), sem("x_second"), sem("x_rest")
        pw_done, cw_mm, cw_done = sem("pw_done"), sem("cw_mm"), sem("cw_done")
        ln_st, ln_var, ln_pool, ln_rstd, xn_ready = (
            sem("ln_stats"), sem("ln_var"), sem("ln_pool"), sem("ln_rstd"), sem("xn_ready"))
        xt_ready, xt_hi, xt_lo = sem("xt_ready"), sem("xt_hi_done"), sem("xt_lo_done")
        proj, swapped, kq_cos, rot_sin, kq_rot, kq_hi, kq_lo = (
            sem("proj_ready"), sem("swapped"), sem("kq_cos"), sem("rot_sin"), sem("kq_rotated"), sem("kq_hi_done"),
            sem("kq_lo_done"))
        s_ready, s_masked, p_exp, r_ready, p_norm = (
            sem("scores_ready"), sem("scores_masked"), sem("p_exp"), sem("rinv_ready"), sem("p_norm"))
        tr_ready, pt_hi, pt_lo = sem("tr_ready"), sem("pt_hi_done"), sem("pt_lo_done")
        vt_ready, v_hi, v_lo = sem("vt_ready"), sem("v_hi_done"), sem("v_lo_done")
        pv_ready, ot_hi, ot_lo = sem("pv_ready"), sem("ot_hi_done"), sem("ot_lo_done")
        o_ready, x_added = sem("o_ready"), sem("x_added")
        f_ready, f_read, gate, e_ready, m_ready = (
            sem("f_ready"), sem("f_read"), sem("gate_chain"), sem("gate_exp"), sem("m_ready"))
        xn_scaled, xn_added, x7_added = sem("xn_scaled"), sem("xn_added"), sem("last_xn_added")
        mt_ready, mt_done, d_ready, out_ready, stored = (
            sem("mt_ready"), sem("mt_done"), sem("d_ready"), sem("out_ready"), sem("stored"))

        block = top.enter_context(nc.Block())

        def wait_apart(engine, signal, value, slot):
            engine.wait_ge(signal, value)
            if signal in (ln_var, r_ready, gate):
                nc.gpsimd.tensor_tensor(spare[:, slot:slot + 1], cst[0:1, 0:1], cst[0:1, 0:1], ALU.add)
            else:
                nc.vector.tensor_copy(spare[:, slot:slot + 1], cst[0:1, 0:1])

        @block.sync
        def _(sp):
            sp.dma_start(cst[:], consts).then_inc(cst_in, 16)
            for hh in range(2):
                sp.dma_start(lg[hh * NS:(hh + 1) * NS, 0, :],
                             log_dt[hh * P:(hh + 1) * P].unsqueeze(0).to_broadcast([NS, P])).then_inc(par_in, 16)
            sp.dma_start(lg[:, 1, :], log_wr).then_inc(par_in, 16)
            sp.dma_start(wim[:], w_im).then_inc(par_in, 16)

            def load_raw(n):
                g, k = divmod(n, NCK)
                before = [m for m in range(n) if raw_slot(m) == raw_slot(n)]
                if before:
                    wait_split(sp, before[-1])
                elif n >= NCK:
                    sp.wait_ge(xt_ready, 2 * NB)
                src = w_qkv[g, k] if k < KC else w_o[g, k - KC]
                sp.dma_start(raw_chunk(n), src).then_inc(raw_in[raw_slot(n)], 16)

            load_raw(0)
            load_raw(1)
            sp.dma_start(mc[:], mix_c).then_inc(mix_in, 16)
            sp.dma_start(ms[:], mix_s).then_inc(mix_in, 16)
            sp.dma_start(fw[:], w_gate).then_inc(gate_in, 16)
            sp.dma_start(dw[:], w_upd).then_inc(gate_in, 16)
            sp.dma_start(dbs[:], w_gmul).then_inc(gate_in, 16)
            sp.dma_start(ctr[:], centers.unsqueeze(0).to_broadcast([P, NE])).then_inc(gate_in, 16)
            sp.dma_start(slp[:], slopes.unsqueeze(0).to_broadcast([P, NE])).then_inc(gate_in, 16)
            load_raw(2)
            load_raw(3)

            def spread(dst, src, e0, ri, hh, signal):
                sp.dma_start(dst[ri * NS:(ri + 1) * NS, :, hh * P:(hh + 1) * P],
                             src[hh * NS:(hh + 1) * NS, e0:e0 + 8, :]).then_inc(signal, 16)

            for hh in range(2):
                if hh == 0:
                    sp.wait_ge(tab_ready, 1)
                for ri in range(2):
                    spread(re1, ang, 8, ri, hh, tab_in[hh])
                spread(u2, ang, 0, 0, hh, tab_in[hh])
                spread(v2, ang, 0, 1, hh, tab_in[hh])
                if hh == 0:
                    sp.wait_ge(tab_ready, 2)
                for ri in range(2):
                    spread(im1, sn, 8, ri, hh, tab_in[hh])
                spread(u2, sn, 0, 1, hh, tab_in[hh])
                if hh == 0:
                    sp.wait_ge(neg_ready, 1)
                spread(v2, neg2, 0, 0, hh, tab_in[hh])
                if hh == 0:
                    sp.wait_ge(p_ready, 1)
                spread(pre, mag, 16, 0, hh, tab_in[hh])
                if hh == 0:
                    sp.wait_ge(neg_ready, 2)
                spread(pre, ang, 16, 1, hh, tab_in[hh])
                if hh == 0:
                    sp.wait_ge(p_ready, 2)
                for ri in range(2):
                    spread(pim, sn, 16, ri, hh, tab_in[hh])

            load_raw(KC)
            load_raw(KC + 1)
            sp.wait_ge(cw_mm, 1)
            for t in range(TT):
                with sp.Fori(t * NCH // 4, (t + 1) * NCH // 4) as it:
                    for s in range(2):
                        sp.wait_ge(evac, it * 2 + (s + 1))
                        for h2 in range(2):
                            rows = x_dram.rearrange("(q m t) c (a j) -> q t (c a) m j", m=CH // 2, t=2, j=64)
                            sp.dma_start(rows[it * 2 + s, h2],
                                         st[s][h2 * 64:(h2 + 1) * 64, :, :]).then_inc(xd_out[s], 16)
                for s in range(2):
                    sp.wait_ge(xd_out[s], 16 * NCH * (t + 1) // TT)
                rows = x_dram[t * P:(t + 1) * P]
                if t == 0:
                    sp.dma_start(x[:, t, :, :], rows).then_inc(x_tile0, 16)
                else:
                    sp.dma_start(x[:, t, 0, :], rows[:, 0, :]).then_inc(x_first, 16)
                    sp.dma_start(x[:, t, 1, :], rows[:, 1, :]).then_inc(x_second, 16)
                    sp.dma_start(x[:, t, 2:NB, :], rows[:, 2:NB, :]).then_inc(x_rest, 16)

            for n in range(KC + 2, NCK * NG):
                load_raw(n)
            with sp.Fori(0, NB) as bb:
                for t in range(TT):
                    sp.wait_ge(out_ready, bb * 2 + (t + 1))
                    sp.dma_start(out[bb, t * P:(t + 1) * P, :], x[:, t, bb, :]).then_inc(stored, 16)
            sp.wait_ge(stored, 16 * NB * TT)

        @block.gpsimd
        def _(pool):
            def split_lo(n):
                k = n % NCK
                pool.wait_ge(w_hi, n + 1)
                if k < KC:
                    hi, lo = wk[:, k, :], wl[:, k, :]
                else:
                    hi, lo = woh[:, k - KC, :], wol[:, k - KC, :]
                nc.gpsimd.tensor_tensor(lo, raw_chunk(n), hi.bitcast(F32), ALU.subtract).then_inc(w_lo, 1)

            for n in range(2):
                split_lo(n)
            pool.wait_ge(chain, CH_RHO)

            def times_power(dst, per_pole, rows):
                n = rows.stop - rows.start
                return nc.gpsimd.tensor_tensor(
                    dst[:, rows, :], per_pole[:].unsqueeze(1).to_broadcast([P, n, P]),
                    cst[:, C_L + rows.start:C_L + rows.stop].unsqueeze(2).to_broadcast([P, n, P]), ALU.mult)

            times_power(mag, rho, ROWS_B).then_inc(pool_tab, 1)
            times_power(mag, rho, ROWS_A).then_inc(pool_tab, 1)
            pool.wait_ge(chain, CH_TURN)
            times_power(ang, turn, ROWS_A).then_inc(pool_tab, 1)
            mw = ex[:, 1, :]
            nc.gpsimd.tensor_tensor(nrm[:], mw, mw, ALU.mult).then_inc(pool_norm, 1)
            nc.gpsimd.tensor_tensor(wsq[:], wim[:], wim[:], ALU.mult).then_inc(pool_norm, 1)
            pool.wait_ge(pool_norm, 2)
            nc.gpsimd.tensor_tensor(nrm[:], nrm[:], wsq[:], ALU.add).then_inc(pool_norm, 1)
            pool.wait_ge(pool_norm, 3)
            nc.gpsimd.tensor_scalar(nrm[:], nrm[:], 0.5, 1.0, ALU.mult, ALU.mult).then_inc(pool_norm, 1)
            pool.wait_ge(chain, CH_ROUND_A)
            nc.gpsimd.tensor_tensor(ang[:, ROWS_A, :], ang[:, ROWS_A, :], sn[:, ROWS_A, :],
                                    ALU.subtract).then_inc(pool_tab, 1)
            la = ROWS_A
            pool.wait_ge(act_tab, 9)
            nc.gpsimd.tensor_tensor(ang[:, la, :], ang[:, la, :], mag[:, la, :], ALU.mult).then_inc(pool_ready, 1)
            nc.gpsimd.tensor_tensor(sn[:, la, :], sn[:, la, :], mag[:, la, :], ALU.mult).then_inc(pool_ready, 1)
            pool.wait_ge(poles_d_ready, 1)
            pool.wait_ge(pool_ready, 2)
            nc.gpsimd.tensor_tensor(pt2[:], ang[:, la, :], di[:].unsqueeze(1).to_broadcast([P, LA, P]),
                                    ALU.mult).then_inc(pool_ready, 1)
            for n in range(2, KC):
                split_lo(n)

            def chunk(it, s):
                hs = bass.ds(it * (2 * CH) + s * CH, CH)
                rest = bass.ds(it * (2 * CH) + (s * CH + G1_DVE), CH - G1_DVE)
                nc.gpsimd.tensor_tensor(
                    g2[s][:].rearrange("p h (c a) -> p h c a", c=NB),
                    ms[:, hs, :].unsqueeze(3).to_broadcast([P, CH, NB, LA]),
                    pim[:, :, hs].rearrange("p a h -> p h a").unsqueeze(2).to_broadcast([P, CH, NB, LA]),
                    ALU.mult)
                nc.gpsimd.tensor_tensor(
                    g1[s][:, G1_DVE:CH, :].rearrange("p h (c a) -> p h c a", c=NB),
                    mc[:, rest, :].unsqueeze(3).to_broadcast([P, CH - G1_DVE, NB, LA]),
                    pre[:, :, rest].rearrange("p a h -> p h a").unsqueeze(2).to_broadcast([P, CH - G1_DVE, NB, LA]),
                    ALU.mult).then_inc(g2_ready, 1)

            pool.wait_ge(mix_in, 32)
            pool.wait_ge(tab_in[0], 16 * 12)
            for s in range(2):
                chunk(0, s)
            for hh in range(2):
                if hh:
                    pool.wait_ge(tab_in[1], 16 * 12)
                with pool.Fori(hh * NCH // 4 or 1, (hh + 1) * NCH // 4) as it:
                    for s in range(2):
                        pool.wait_ge(mixed, it * 4 + (2 * s - 2))
                        chunk(it, s)

            pool.wait_ge(x_first, 16)

            def norm(m):
                rstd = norm_set(m)["rstd"]
                wait_apart(pool, ln_var, m + 1, 8)
                nc.gpsimd.tensor_scalar(rstd, norm_set(m)["mv"][:, :, 1], EPS, 1.0, ALU.add, ALU.mult).then_inc(ln_pool, 1)
                pool.wait_ge(ln_pool, m + 1)
                nc.gpsimd.tensor_tensor(rstd, rstd, cst[:, C_POW:C_POW + TT], ALU.pow).then_inc(ln_rstd, 1)

            def rotate(s, rests=True):
                for j in range(3):
                    view, table, _, _ = rope_view(j)
                    pool.wait_ge(swapped, s * 3 + (j + 1))
                    nc.gpsimd.tensor_tensor(view(sw), view(sw), table(sinT), ALU.mult).then_inc(rot_sin, 1)
                for j in range(3 if rests else 0):
                    _, _, part, flat = rope_view(j)
                    pool.wait_ge(kq_hi, s * 3 + (j + 1))
                    nc.gpsimd.tensor_tensor(flat(kl), part(kq), flat(kh).bitcast(F32), ALU.subtract).then_inc(kq_lo, 1)

            norm(0)
            split_lo(KC)
            norm(1)
            split_lo(KC + 1)
            rotate(0, rests=False)
            norm(2)

            def add_normed(bb):
                mem = norm_set(NB + bb)
                normed = mem["xn"]
                wait_apart(pool, gate, bb * GATE + GATE, 8)
                for t in range(TT):
                    nc.gpsimd.tensor_scalar(normed[:, t, :], normed[:, t, :], mem["one_minus"][:, t:t + 1], 1.0, ALU.mult,
                                            ALU.mult).then_inc(xn_scaled, 1)
                for t in range(TT):
                    pool.wait_ge(xn_scaled, bb * 2 + (t + 1))
                    nc.gpsimd.tensor_tensor(x[:, t, bb, :], x[:, t, bb, :], normed[:, t, :], ALU.add).then_inc(xn_added, 1)

            def normalise_probs(i):
                for j in range(QH):
                    if j % 2 == 0:
                        wait_apart(pool, r_ready, i * 2 + (j // 2 + 1), 6 + j // 2)
                    for t, cols in ((0, slice(0, P)), (1, slice(P, 3 * P))):
                        last = nc.gpsimd.tensor_scalar(sm[:, j, cols], sm[:, j, cols], rinv[:, 2 * j + t:2 * j + t + 1],
                                                       1.0, ALU.mult, ALU.mult)
                    last.then_inc(p_norm, 1)

            def step(g, b, at):
                i = b + 8 * g
                if needs_norm1(g, at):
                    norm(b + 3)
                normalise_probs(i)
                rotate(i + 1)
                if needs_ffn(g, at):
                    add_normed(b - 2)
                if needs_norm2(g, at):
                    norm(b + (NB - 1))
                if g < NG - 1 and at == NB - 2:
                    for k in range(KC):
                        if not dve_splits((g + 1) * NCK + k):
                            split_lo((g + 1) * NCK + k)
                if at == 0:
                    for k in range(KC if g else KC + 2, NCK):
                        split_lo(g * NCK + k)

            steps(pool, step)
            normalise_probs(NG * NB - 1)
            norm(2 * NB - 2)
            norm(2 * NB - 1)
            add_normed(NB - 3)
            add_normed(NB - 2)

        @block.scalar
        def _(act):
            def split_hi(n):
                k = n % NCK
                act.wait_ge(raw_in[raw_slot(n)], 16 * raw_turn(n))
                dst = wk[:, k, :] if k < KC else woh[:, k - KC, :]
                nc.scalar.activation(dst, raw_chunk(n), ACT.Copy).then_inc(w_hi, 1)

            for n in range(2):
                split_hi(n)
            TWO_PI = 6.283185
            for k, rows in enumerate((ROWS_B, ROWS_A)):
                act.wait_ge(pool_tab, k + 1)
                nc.scalar.activation(mag[:, rows, :], mag[:, rows, :], ACT.Exp).then_inc(act_tab, 1)
            count = 2
            for rows in (ROWS_B, ROWS_A):
                if rows == ROWS_B:
                    act.wait_ge(chain, CH_FRACTION)
                else:
                    act.wait_ge(pool_tab, 4)
                nc.scalar.activation(sn[:, rows, :], ang[:, rows, :], ACT.Sin, scale=TWO_PI).then_inc(act_tab, 1)
                if rows == ROWS_B:
                    nc.scalar.activation(half[:], ang[:, 1, :], ACT.Sin, scale=TWO_PI / 2).then_inc(act_tab, 1)
                    count += 1
                act.wait_ge(act_tab, count + 1)
                nc.scalar.activation(ang[:, rows, :], ang[:, rows, :], ACT.Abs).then_inc(act_tab, 1)
                act.wait_ge(act_tab, count + 2)
                nc.scalar.activation(ang[:, rows, :], ang[:, rows, :], ACT.Sin, scale=-TWO_PI,
                                     bias=cst[:, C_QUARTER:C_QUARTER + 1]).then_inc(act_tab, 1)
                count += 3
            for n in range(2, KC):
                split_hi(n)
            act.wait_ge(tab_ready, 2)
            nc.scalar.activation(neg2[:], sn[:, 0:LB2, :], ACT.Copy, scale=-1.0).then_inc(neg_ready, 1)
            act.wait_ge(p_ready, 1)
            act.wait_ge(pool_ready, 3)
            nc.scalar.activation(ang[:, ROWS_A, :], mag[:, ROWS_A, :], ACT.Copy, scale=-1.0).then_inc(neg_ready, 1)

            def evacuate(it, s):
                for q in range(2):
                    act.wait_ge(mixed, it * 4 + (s * 2 + q + 1))
                    for h2 in range(2):
                        rows = slice(h2 * 64, h2 * 64 + 64)
                        src = banks[2 * s + q][rows, :].rearrange("p (m t j) -> p m t j", t=2, j=64)[:, :, h2, :]
                        last = nc.scalar.activation(st[s][rows, q * 4:q * 4 + 4, :], src, ACT.Copy)
                last.then_inc(evac, 1)

            act.wait_ge(cw_mm, 1)
            nc.scalar.activation(cw[:], banks[7][:, 0:FC], ACT.Copy).then_inc(cw_done, 1)
            for s in range(2):
                evacuate(0, s)
            with act.Fori(1, NCH // 2) as it:
                for s in range(2):
                    act.wait_ge(xd_out[s], it * 32)
                    evacuate(it, s)

            def xt1(b):
                for q in range(2):
                    act.wait_ge(xt_ready, b * 2 + (q + 1))
                    nc.scalar.activation(xt_h[:, b, 2 * q:2 * q + 2, :].rearrange("p k s -> p (k s)"),
                                         banks[5 + q][:], ACT.Copy).then_inc(xt_hi, 1)

            def xt2(bb, first_bank=5):
                for q in range(2):
                    act.wait_ge(xt_ready, bb * 2 + (2 * NB + q + 1))
                    nc.scalar.activation(xnt[:, 2 * q:2 * q + 2, :].rearrange("p k s -> p (k s)"),
                                         banks[first_bank + q][:], ACT.Copy).then_inc(xt_hi, 1)

            def swap(s, parts=range(3)):
                for j in parts:
                    view, _, _, _ = rope_view(j)
                    act.wait_ge(proj, s * 3 + (j + 1))
                    if j == 0 and (not isinstance(s, int) or s):
                        act.wait_ge(kq_rot, s * 3)
                        act.wait_ge(vt_ready, s)
                    src = banks[j][:, 0:S] if j == 0 else banks[j][:].rearrange("p (h s) -> p h s", h=2)
                    nc.scalar.activation(view(sw)[0:64], src[64:128], ACT.Copy)
                    last = nc.scalar.activation(view(sw)[64:128], src[0:64], ACT.Copy)
                    if j == 0:
                        last = nc.scalar.activation(vt[:], banks[0][:, S:2 * S], ACT.Copy)
                    last.then_inc(swapped, 1)

            def round_kq(s):
                for j in range(3):
                    _, _, part, flat = rope_view(j)
                    act.wait_ge(kq_rot, s * 3 + (j + 1))
                    if j == 0 and (not isinstance(s, int) or s):
                        act.wait_ge(s_ready, s * 4)
                    nc.scalar.activation(flat(kh), part(kq), ACT.Copy).then_inc(kq_hi, 1)

            def round_v(s):
                act.wait_ge(vt_ready, s + 1)
                nc.scalar.activation(vh[:].rearrange("p t d -> p (t d)"), banks[2][:, 0:S], ACT.Copy).then_inc(v_hi, 1)

            act.wait_ge(x_first, 16)
            for n in (KC, KC + 1):
                split_hi(n)
            xt1(0)
            swap(0, range(2))
            xt1(1)
            swap(0, (2,))
            round_kq(0)
            round_v(0)

            def gate_exp(bb):
                act.wait_ge(gate, bb * GATE + GATE_Z)
                z = norm_set(NB + bb)["z"]
                nc.scalar.activation(z, z, ACT.Exp, scale=-1.0).then_inc(e_ready, 1)

            def mt_evac(bb):
                act.wait_ge(mt_ready, bb + 1)
                nc.scalar.activation(mt[:], banks[7][0:MC, 0:S], ACT.Copy).then_inc(mt_done, 1)

            def exponents(i):
                for j in range(QH):
                    act.wait_ge(s_masked, i * 4 + (j + 1))
                    for t, cols in ((0, slice(0, P)), (1, slice(P, 3 * P))):
                        n = 2 * j + t
                        last = nc.scalar.activation(sm[:, j, cols], sm[:, j, cols], ACT.Exp, scale=-1.0,
                                                    bias=mx[:, n:n + 1], accum_out=rsum[:, n:n + 1])
                    last.then_inc(p_exp, 1)

            def round_probs(i):
                for j in range(3):
                    act.wait_ge(tr_ready, i * 3 + (j + 1))
                    nc.scalar.activation(pth[:, j, :], banks[5 + j][:], ACT.Copy).then_inc(pt_hi, 1)

            def round_attn(i):
                for j in range(2):
                    act.wait_ge(pv_ready, i * 2 + (j + 1))
                    nc.scalar.activation(oth[:, 2 * j:2 * j + 2, :].rearrange("p h s -> p (h s)"),
                                         banks[j][:], ACT.Copy).then_inc(ot_hi, 1)

            def step(g, b, at):
                i = b + 8 * g
                exponents(i)
                swap(i + 1, (0,))
                if needs_xt(g, at):
                    xt1(b + 2)
                if needs_ffn(g, at):
                    xt2(b - 2, 3)
                swap(i + 1, (1, 2))
                if needs_ffn(g, at):
                    gate_exp(b - 2)
                round_probs(i)
                round_kq(i + 1)
                if g < NG - 1 and at == NB - 2:
                    act.wait_ge(proj, (8 * (g + 1)) * 3)
                    for k in range(KC):
                        split_hi((g + 1) * NCK + k)
                if at == 0:
                    if g > 0:
                        act.wait_ge(o_ready, 8 * g * 2)
                    for k in range(KC if g else KC + 2, NCK):
                        split_hi(g * NCK + k)
                round_attn(i)
                round_v(i + 1)
                if needs_ffn(g, at):
                    mt_evac(b - 2)

            steps(act, step)
            last = NG * NB - 1
            exponents(last)
            xt2(NB - 3, 1)
            round_probs(last)
            round_attn(last)
            xt2(NB - 2)
            gate_exp(NB - 3)
            mt_evac(NB - 3)
            xt2(NB - 1, 1)
            gate_exp(NB - 2)
            mt_evac(NB - 2)
            gate_exp(NB - 1)
            mt_evac(NB - 1)

        @block.vector
        def _(dve):
            links = [0]

            def link(ins):
                links[0] += 1
                ins.then_inc(chain, 1)
                dve.wait_ge(chain, links[0])

            v = nc.vector

            def expm1_parts(xin, n):
                k, r, q, p2 = (t[:].rearrange("p a b -> p (a b)")[:, 0:n] for t in (kk, rr, qq, ki))
                link(v.tensor_scalar(xin, xin, -87.0, 88.0, ALU.max, ALU.min))
                link(v.tensor_scalar(k, xin, 1.4426950408889634, ROUND, ALU.mult, ALU.add))
                link(v.tensor_scalar(k, k, ROUND, None, ALU.subtract))
                link(v.scalar_tensor_tensor(r, k, -0.693359375, xin, ALU.mult, ALU.add))
                link(v.scalar_tensor_tensor(r, k, 2.12194440e-4, r, ALU.mult, ALU.add))
                link(v.tensor_scalar(q, r, 1.0 / 5040, None, ALU.mult))
                for c in (1.0 / 720, 1.0 / 120, 1.0 / 24, 1.0 / 6, 0.5, 1.0):
                    link(v.scalar_tensor_tensor(q, q, c, r, ALU.add, ALU.mult))
                link(v.tensor_scalar(p2, k, 127.0, 8388608.0, ALU.add, ALU.mult))
                return q, p2.bitcast(F32)

            dve.wait_ge(par_in, 64)
            dve.wait_ge(cst_in, 16)
            flat = lg[:].rearrange("p a b -> p (a b)")
            q, p2 = expm1_parts(flat, 2 * P)
            exf = ex[:].rearrange("p a b -> p (a b)")
            link(v.tensor_tensor(exf, q, p2, ALU.mult))
            link(v.tensor_tensor(exf, exf, p2, ALU.add))
            dt, mw = ex[:, 0, :], ex[:, 1, :]
            link(v.scalar_tensor_tensor(rho[:], mw, -1.0, dt, ALU.mult, ALU.mult))
            assert links[0] == CH_RHO, links
            link(v.tensor_tensor(turn[:], wim[:], dt, ALU.mult))
            link(v.tensor_scalar(turn[:], turn[:], 0.15915494309189535, None, ALU.mult))
            assert links[0] == CH_TURN, links
            lb = ROWS_B
            link(v.tensor_tensor(ang[:, lb, :], turn[:].unsqueeze(1).to_broadcast([P, LB1 + LB2, P]),
                                 cst[:, C_L:C_L + LB1 + LB2].unsqueeze(2).to_broadcast([P, LB1 + LB2, P]), ALU.mult))
            link(v.tensor_scalar(sn[:, lb, :], ang[:, lb, :], ROUND, ROUND, ALU.add, ALU.subtract))
            link(v.tensor_tensor(ang[:, lb, :], ang[:, lb, :], sn[:, lb, :], ALU.subtract))
            assert links[0] == CH_FRACTION, links
            link(v.tensor_copy(t0[:], rho[:]))
            dve.wait_ge(pool_tab, 3)
            link(v.tensor_scalar(sn[:, ROWS_A, :], ang[:, ROWS_A, :], ROUND, ROUND, ALU.add, ALU.subtract))
            assert links[0] == CH_ROUND_A, links
            q, p2 = expm1_parts(t0[:], P)
            link(v.tensor_tensor(em1[:], q, p2, ALU.mult))
            link(v.scalar_tensor_tensor(em1[:], p2, -1.0, em1[:], ALU.add, ALU.add))
            dve.wait_ge(pool_norm, 4)
            link(v.reciprocal(nrm[:], nrm[:]))
            dve.wait_ge(act_tab, 4)
            link(v.tensor_tensor(t0[:], half[:], half[:], ALU.mult))
            link(v.scalar_tensor_tensor(ai[:], em1[:], 1.0, sn[:, 1, :], ALU.add, ALU.mult))
            dve.wait_ge(act_tab, 6)
            link(v.tensor_tensor(ar[:], em1[:], ang[:, 1, :], ALU.mult))
            link(v.scalar_tensor_tensor(ar[:], t0[:], -2.0, ar[:], ALU.mult, ALU.add))
            v.tensor_tensor(dr[:], ai[:], wim[:], ALU.mult)
            v.tensor_tensor(t0[:], ar[:], mw, ALU.mult)
            v.tensor_tensor(di[:], ai[:], mw, ALU.mult)
            link(v.tensor_tensor(em1[:], ar[:], wim[:], ALU.mult))
            v.tensor_tensor(dr[:], dr[:], t0[:], ALU.subtract)
            link(v.tensor_tensor(di[:], di[:], em1[:], ALU.add))
            link(v.scalar_tensor_tensor(di[:], di[:], -1.0, nrm[:], ALU.mult, ALU.mult))
            v.tensor_tensor(dr[:], dr[:], nrm[:], ALU.mult).then_inc(poles_d_ready, 1)
            v.tensor_tensor(ang[:, lb, :], ang[:, lb, :], mag[:, lb, :], ALU.mult).then_inc(tab_ready, 1)
            v.tensor_tensor(sn[:, lb, :], sn[:, lb, :], mag[:, lb, :], ALU.mult).then_inc(tab_ready, 1)
            la = ROWS_A
            drb = dr[:].unsqueeze(1).to_broadcast([P, LA, P])
            dib = di[:].unsqueeze(1).to_broadcast([P, LA, P])
            dve.wait_ge(poles_d_ready, 1)
            dve.wait_ge(pool_ready, 2)
            v.tensor_tensor(mag[:, la, :], ang[:, la, :], drb, ALU.mult)
            link(v.tensor_tensor(pt3[:], sn[:, la, :], dib, ALU.mult))
            v.tensor_tensor(mag[:, la, :], mag[:, la, :], pt3[:], ALU.subtract).then_inc(p_ready, 1)
            link(v.tensor_tensor(sn[:, la, :], sn[:, la, :], drb, ALU.mult))
            dve.wait_ge(pool_ready, 3)
            v.scalar_tensor_tensor(sn[:, la, :].rearrange("p a h -> p (a h)"), sn[:, la, :].rearrange("p a h -> p (a h)"),
                                   -1.0, pt2[:].rearrange("p a h -> p (a h)"), ALU.mult, ALU.subtract).then_inc(p_ready, 1)

            dve.wait_ge(gate_in, 80)
            for k in range(KC):
                sel = fw[:, k, 0:NE * SE].rearrange("p (n s) -> p n s", n=NE)
                mean = fw[:, k, NE * SE:NE * SE + NE]
                upd = fw[:, k, NE * SE + NE:FC].rearrange("p (n h) -> p n h", n=NE)
                row = pw[:, k, 0:FC]
                v.tensor_tensor(row[:, 0:64].rearrange("p (n s) -> p n s", n=NE), sel,
                                mean.unsqueeze(2).to_broadcast([P, NE, SE]), ALU.mult)
                v.tensor_tensor(row[:, 64:72], mean, mean, ALU.mult)
                v.tensor_tensor(row[:, 72:FC].rearrange("p (n h) -> p n h", n=NE), upd,
                                dbs[:, k, :].unsqueeze(2).to_broadcast([P, NE, HE]), ALU.mult).then_inc(pw_done, 1)

            dve.wait_ge(tab_in[0], 16 * 12)
            dve.wait_ge(mix_in, 32)
            def chunk(it, s):
                hs = bass.ds(it * (2 * CH) + s * CH, CH)

                def outer(left, right):
                    return (left[:, :, hs].rearrange("p e h -> p h e").unsqueeze(3).to_broadcast([P, CH, LB1, LB2]),
                            right[:, :, hs].rearrange("p e h -> p h e").unsqueeze(2).to_broadcast([P, CH, LB1, LB2]))

                grid = lambda t: t[:].rearrange("p h (i j) -> p h i j", i=LB1)
                v.tensor_tensor(grid(bt[s]), *outer(re1, u2), ALU.mult)
                if not isinstance(it, int) or s:
                    dve.wait_ge(b_ready, it * 2 + s)
                v.tensor_tensor(grid(tmp), *outer(im1, v2), ALU.mult).then_inc(t2_done, 1)
                first = bass.ds(it * (2 * CH) + s * CH, G1_DVE)
                v.tensor_tensor(g1[s][:, 0:G1_DVE, :].rearrange("p h (c a) -> p h c a", c=NB),
                                mc[:, first, :].unsqueeze(3).to_broadcast([P, G1_DVE, NB, LA]),
                                pre[:, :, first].rearrange("p a h -> p h a").unsqueeze(2).to_broadcast([P, G1_DVE, NB, LA]),
                                ALU.mult)
                dve.wait_ge(t2_done, it * 2 + (s + 1))
                v.tensor_tensor(bt[s][:], bt[s][:], tmp[:], ALU.add).then_inc(b_ready, 1)

            for s in range(2):
                chunk(0, s)
            for hh in range(2):
                if hh:
                    dve.wait_ge(tab_in[1], 16 * 12)
                with dve.Fori(hh * NCH // 4 or 1, (hh + 1) * NCH // 4) as it:
                    for s in range(2):
                        dve.wait_ge(mixed, it * 4 + (2 * s - 2))
                        chunk(it, s)

            dve.wait_ge(x_tile0, 16)
            dve.wait_ge(x_first, 16)
            def norm_stats(src, m):
                for t in range(TT):
                    v.bn_stats(stats[:, t, :], src(t)).then_inc(ln_st, 1)
                wait_apart(dve, ln_st, m * 2 + 2, 4)
                for t in range(TT):
                    last = v.bn_aggr(norm_set(m)["mv"][:, t, :], stats[:, t, :])
                last.then_inc(ln_var, 1)

            def norm_apply(src, m, second=False):
                mem = norm_set(m)
                dve.wait_ge(ln_rstd, m + 1)
                if second and isinstance(m, int) and m == NB:
                    wait_split(dve, NCK * NG - 1)
                elif second and mem is norm_sets[0]:
                    dve.wait_ge(xn_added, m * 2 - 2 * NB)
                if not isinstance(m, int) or m:
                    dve.wait_ge(xt_ready, m * 2)
                for t in range(TT):
                    last = v.tensor_scalar(mem["xn"][:, t, :], src(t), mem["mv"][:, t, 0:1], mem["rstd"][:, t:t + 1],
                                           ALU.subtract, ALU.mult)
                last.then_inc(xn_ready, 1)

            def tokens(b):
                return lambda t: x[:, t, b, :]

            def xt_rest(b):
                for q in range(2):
                    dve.wait_ge(xt_hi, b * 2 + (q + 1))
                    v.tensor_tensor(xt_l[:, b, 2 * q:2 * q + 2, :].rearrange("p k s -> p (k s)"), banks[5 + q][:],
                                    xt_h[:, b, 2 * q:2 * q + 2, :].rearrange("p k s -> p (k s)").bitcast(F32),
                                    ALU.subtract).then_inc(xt_lo, 1)

            def rope(s, j):
                view, table, _, _ = rope_view(j)
                src = banks[j][:, 0:S] if j == 0 else banks[j][:].rearrange("p (h s) -> p h s", h=2)
                dve.wait_ge(swapped, s * 3 + (j + 1))
                v.tensor_tensor(view(kq), src, table(cosT), ALU.mult).then_inc(kq_cos, 1)

            def rope_add(s, j):
                view, _, _, _ = rope_view(j)
                dve.wait_ge(rot_sin, s * 3 + (j + 1))
                dve.wait_ge(kq_cos, s * 3 + (j + 1))
                v.tensor_tensor(view(kq), view(kq), view(sw), ALU.add).then_inc(kq_rot, 1)

            def v_rest(s):
                dve.wait_ge(v_hi, s + 1)
                v.tensor_tensor(vl[:].rearrange("p t d -> p (t d)"), banks[2][:, 0:S],
                                vh[:].rearrange("p t d -> p (t d)").bitcast(F32), ALU.subtract).then_inc(v_lo, 1)

            norm_stats(tokens(0), 0)
            norm_apply(tokens(0), 0)
            xt_rest(0)
            dve.wait_ge(x_second, 16)
            norm_stats(tokens(1), 1)
            norm_apply(tokens(1), 1)
            rope(0, 0)
            rope(0, 1)
            rope_add(0, 0)
            xt_rest(1)
            rope(0, 2)
            rope_add(0, 1)
            rope_add(0, 2)
            for j in range(3):
                _, _, part, flat = rope_view(j)
                dve.wait_ge(kq_hi, j + 1)
                v.tensor_tensor(flat(kl), part(kq), flat(kh).bitcast(F32), ALU.subtract).then_inc(kq_lo, 1)
            dve.wait_ge(x_rest, 16)
            norm_stats(tokens(2), 2)

            def add_output(i, b, tiles=range(TT)):
                for t in tiles:
                    dve.wait_ge(o_ready, i * 2 + (t + 1))
                    v.tensor_tensor(x[:, t, b, :], banks[3 + t][:], x[:, t, b, :], ALU.add).then_inc(x_added, 1)

            def gate_read(bb, bank=0):
                mem = norm_set(NB + bb)
                f = banks[bank][:].rearrange("p (t c) -> p t c", t=TT)
                dve.wait_ge(cw_done, 1)
                dve.wait_ge(f_ready, bb + 1)
                v.tensor_tensor(mem["gu"], f[:, :, 0:64], cw[:, 0:64].unsqueeze(1).to_broadcast([P, TT, 64]), ALU.subtract)
                v.scalar_tensor_tensor(mem["score"], f[:, :, 64:72], -2.0,
                                       cw[:, 64:72].unsqueeze(1).to_broadcast([P, TT, NE]), ALU.mult, ALU.add)
                v.tensor_tensor(mem["gm"], f[:, :, 72:FC], cw[:, 72:FC].unsqueeze(1).to_broadcast([P, TT, 64]),
                                ALU.subtract).then_inc(f_read, 1)

            def gate_link(bb, n):
                def then(ins):
                    n[0] += 1
                    ins.then_inc(gate, 1)
                    dve.wait_ge(gate, bb * GATE + n[0])
                return then

            bc = lambda t: t.unsqueeze(2).to_broadcast([P, TT, NE])

            def gate_scores(bb):
                mem, n = norm_set(NB + bb), [0]
                then = gate_link(bb, n)
                score, z, ssq, gu = mem["score"], mem["z"], mem["ssq"], mem["gu"]
                dve.wait_ge(f_read, bb + 1)
                v.tensor_tensor(gu, gu, gu, ALU.mult)
                then(v.tensor_tensor(ssq, mem["rstd"], mem["rstd"], ALU.mult))
                v.tensor_reduce(z, gu.rearrange("p t (n s) -> p t n s", n=NE), AX.X, ALU.add)
                then(v.scalar_tensor_tensor(ssq, mem["mv"][:, :, 1], float(D), ssq, ALU.mult, ALU.mult))
                then(v.tensor_tensor(score, score, bc(ssq), ALU.add))
                then(v.reciprocal(score, score))
                then(v.tensor_tensor(z, z, score, ALU.mult))
                then(v.tensor_tensor(z, z, ctr[:].unsqueeze(1).to_broadcast([P, TT, NE]), ALU.subtract))
                then(v.tensor_tensor(z, z, slp[:].unsqueeze(1).to_broadcast([P, TT, NE]), ALU.mult))
                assert n[0] == GATE_Z

            def gates(bb):
                mem, n = norm_set(NB + bb), [GATE_Z]
                then = gate_link(bb, n)
                z, rank, mm = mem["z"], mem["rank"], mem["mm"]
                one_minus, best, first = mem["one_minus"], mem["best"], mem["first"]
                dve.wait_ge(e_ready, bb + 1)
                then(v.tensor_scalar(z, z, 1.0, None, ALU.add))
                then(v.reciprocal(z, z))
                then(v.tensor_reduce(best, z, AX.X, ALU.max))
                then(v.tensor_tensor(rank, z, bc(best), ALU.is_equal))
                then(v.tensor_tensor(rank, rank, cst[:, C_RANK:C_RANK + NE].unsqueeze(1).to_broadcast([P, TT, NE]),
                                     ALU.mult))
                then(v.tensor_reduce(first, rank, AX.X, ALU.max))
                onehot = mm[:, :, 64:72]
                then(v.tensor_tensor(onehot, rank, bc(first), ALU.is_equal))
                then(v.tensor_scalar(one_minus, best, -1.0, 1.0, ALU.mult, ALU.add))
                v.tensor_tensor(mm[:, :, 0:64].rearrange("p t (n h) -> p t n h", n=NE),
                                mem["gm"].rearrange("p t (n h) -> p t n h", n=NE),
                                onehot.unsqueeze(3).to_broadcast([P, TT, NE, HE]), ALU.mult).then_inc(m_ready, 1)
                assert n[0] == GATE, n

            def finish(bb, first_bank=5):
                mem = norm_set(NB + bb)
                if isinstance(bb, int) and bb == NB - 1:
                    dve.wait_ge(x7_added, 2)
                else:
                    dve.wait_ge(xn_added, bb * 2 + 2)
                for t in range(TT):
                    dve.wait_ge(d_ready, bb * 2 + (t + 1))
                    v.scalar_tensor_tensor(x[:, t, bb, :], banks[first_bank + t][:], mem["best"][:, t:t + 1],
                                           x[:, t, bb, :], ALU.mult, ALU.add).then_inc(out_ready, 1)

            def attn_rest(i, j):
                dve.wait_ge(ot_hi, i * 2 + (j + 1))
                hs = slice(2 * j, 2 * j + 2)
                v.tensor_tensor(otl[:, hs, :].rearrange("p h s -> p (h s)"), banks[j][:],
                                oth[:, hs, :].rearrange("p h s -> p (h s)").bitcast(F32),
                                ALU.subtract).then_inc(ot_lo, 1)

            def masked_scores(i, first=False):
                for j in range(QH):
                    wait_apart(dve, s_ready, i * 4 + (j + 1), j)
                    for t, cols, m in ((0, slice(0, P), mask[:, P:2 * P]), (1, slice(P, 3 * P), mask)):
                        n = 2 * j + t
                        last = v.tensor_tensor_reduce(out=sm[:, j, cols], in0=banks[3 + j][:, cols], in1=m,
                                                      scale=-SCALE, scalar=3.0e38, op0=ALU.add, op1=ALU.min,
                                                      accum_out=mx[:, n:n + 1])
                    last.then_inc(s_masked, 1)
                    if j == 1 and not first:
                        attn_rest(i - 1, 1)
                v_rest(i)

            def reciprocals(i):
                dve.wait_ge(p_exp, i * 4 + 2)
                v.reciprocal(rinv[:, 0:4], rsum[:, 0:4]).then_inc(r_ready, 1)
                dve.wait_ge(p_exp, i * 4 + 4)
                v.reciprocal(rinv[:, 4:8], rsum[:, 4:8]).then_inc(r_ready, 1)

            def probs_rest(i):
                for j in range(3):
                    dve.wait_ge(pt_hi, i * 3 + (j + 1))
                    v.tensor_tensor(ptl[:, j, :], banks[5 + j][:], pth[:, j, :].bitcast(F32),
                                    ALU.subtract).then_inc(pt_lo, 1)

            def step(g, b, at):
                i = b + 8 * g
                masked_scores(i, g == 0 and at == 0)
                if g == 0 and at == 0:
                    norm_apply(tokens(2), 2)
                if needs_norm1(g, at):
                    norm_stats(tokens(b + 3), b + 3)
                if needs_ffn(g, at):
                    norm_apply(tokens(b - 2), b + (NB - 2), second=True)
                reciprocals(i)
                rope(i + 1, 0)
                if needs_finish(g, at):
                    finish(b - 3)
                if needs_xt(g, at):
                    xt_rest(b + 2)
                rope(i + 1, 1)
                rope_add(i + 1, 0)
                if needs_ffn(g, at):
                    gate_read(b - 2)
                    gate_scores(b - 2)
                rope(i + 1, 2)
                rope_add(i + 1, 1)
                rope_add(i + 1, 2)
                probs_rest(i)
                if needs_norm1(g, at):
                    norm_apply(tokens(b + 3), b + 3)
                if needs_ffn(g, at):
                    gates(b - 2)
                if not (g == 0 and at == 0):
                    add_output(i - 1, (b - 1) if at else NB - 1, (0,))
                    if g < NG - 1 and at == NB - 2:
                        n = (g + 1) * NCK + KC - 1
                        dve.wait_ge(w_hi, n + 1)
                        v.tensor_tensor(wl[:, KC - 1, :], raw_chunk(n), wk[:, KC - 1, :].bitcast(F32),
                                        ALU.subtract).then_inc(w_lo_dve, 1)
                    add_output(i - 1, (b - 1) if at else NB - 1, (1,))
                if needs_norm2(g, at):
                    wait_apart(dve, x_added, i * 2, 5)
                    norm_stats(tokens(b - 1), b + (NB - 1))
                attn_rest(i, 0)

            steps(dve, step)
            last = NG * NB - 1
            masked_scores(last)
            norm_apply(tokens(NB - 3), 2 * NB - 3, second=True)
            reciprocals(last)
            add_output(last - 1, NB - 2)
            dve.wait_ge(x_added, 2 * last)
            norm_stats(tokens(NB - 2), 2 * NB - 2)
            finish(NB - 4)
            probs_rest(last)
            gate_read(NB - 3, 2)
            norm_apply(tokens(NB - 2), 2 * NB - 2, second=True)
            for j in range(2):
                attn_rest(last, j)
            gate_scores(NB - 3)
            gates(NB - 3)
            add_output(last, NB - 1)
            dve.wait_ge(x_added, 2 * last + 2)
            norm_stats(tokens(NB - 1), 2 * NB - 1)
            gate_read(NB - 2)
            norm_apply(tokens(NB - 1), 2 * NB - 1, second=True)
            gate_scores(NB - 2)
            gates(NB - 2)
            gate_read(NB - 1)
            gate_scores(NB - 1)
            gates(NB - 1)
            mem = norm_set(2 * NB - 1)
            for t in range(TT):
                v.scalar_tensor_tensor(x[:, t, NB - 1, :], mem["xn"][:, t, :], mem["one_minus"][:, t:t + 1],
                                       x[:, t, NB - 1, :], ALU.mult, ALU.add).then_inc(x7_added, 1)
            finish(NB - 3)
            finish(NB - 2, 1)
            finish(NB - 1, 3)

        @block.tensor
        def _(pe):
            mmul = nc.tensor.matmul

            def split_product(dst, parts, start=True, stop=True):
                n = len(parts)
                for k, (lh, ll, rh, rl) in enumerate(parts):
                    mmul(dst, lh, rh, start=start and k == 0, stop=False, skip_group_check=True)
                    mmul(dst, ll, rh, start=False, stop=False, skip_group_check=True)
                    last = mmul(dst, lh, rl, start=False, stop=stop and k == n - 1, skip_group_check=True)
                return last

            pe.wait_ge(pw_done, KC)
            for k in range(KC):
                last = mmul(banks[7][:, 0:FC], ones[:], pw[:, k, 0:FC], start=k == 0, stop=k == KC - 1)
            last.then_inc(cw_mm, 1)

            def chunk(s):
                for m in range(CH // 2):
                    hs = slice(2 * m, 2 * m + 2)
                    flat = lambda t: t[:, hs, :].rearrange("p h j -> p (h j)")
                    dst = banks[2 * s + m // 4][:, (m % 4) * P:(m % 4 + 1) * P]
                    mmul(dst, flat(g1[s]), flat(bt[s]), start=m % 4 == 0, stop=False, skip_group_check=True)
                    last = mmul(dst, flat(g2[s]), flat(bt[s]), start=False, stop=m % 4 == 3, skip_group_check=True)
                    if m % 4 == 3:
                        last.then_inc(mixed, 1)

            for s in range(2):
                pe.wait_ge(b_ready, s + 1)
                pe.wait_ge(g2_ready, s + 1)
                chunk(s)
            with pe.Fori(1, NCH // 2) as it:
                for s in range(2):
                    pe.wait_ge(b_ready, it * 2 + (s + 1))
                    pe.wait_ge(g2_ready, it * 2 + (s + 1))
                    pe.wait_ge(evac, it * 2 + (s - 1))
                    chunk(s)

            def transpose_tokens(m, first_bank=5):
                normed = norm_set(m)["xn"]
                for q in range(2):
                    for k in range(2):
                        for t in range(TT):
                            col = (2 * q + k) * P
                            last = nc.tensor.transpose(banks[first_bank + q][:, k * S + t * P:k * S + (t + 1) * P],
                                                       normed[:, t, col:col + P], ident)
                    last.then_inc(xt_ready, 1)

            def project(s, b, first, after_kv, before_last):
                def parts(c):
                    cols = slice(c * HD, (c + 1) * HD)
                    return [(wk[:, k, cols], wl[:, k, cols], xt_h[:, b, k, :], xt_l[:, b, k, :]) for k in range(KC)]
                if not first:
                    pe.wait_ge(ot_lo, s * 2 - 3)
                split_product(banks[0][:, 0:S], parts(0))
                split_product(banks[0][:, S:2 * S], parts(1)).then_inc(proj, 1)
                after_kv()
                for j in range(2):
                    if j == 0 and not first:
                        pe.wait_ge(ot_lo, s * 2 - 2)
                    if j == 1 and (not isinstance(s, int) or s):
                        pe.wait_ge(v_lo, s)
                    if j == 1:
                        before_last()
                    for h in range(2):
                        last = split_product(banks[1 + j][:, h * S:(h + 1) * S], parts(2 + 2 * j + h))
                    last.then_inc(proj, 1)

            def transpose_v(s):
                pe.wait_ge(swapped, s * 3 + 3)
                pe.wait_ge(kq_cos, s * 3 + 3)
                for t in range(TT):
                    last = nc.tensor.transpose(banks[2][:, t * P:(t + 1) * P], vt[:, t * P:(t + 1) * P], ident)
                last.then_inc(vt_ready, 1)

            def gate_product(bb, bank=0):
                for t in range(TT):
                    for k in range(KC):
                        last = mmul(banks[bank][:, t * S:t * S + FC], xnt[:, k, t * P:(t + 1) * P], fw[:, k, :],
                                    start=k == 0, stop=k == KC - 1)
                last.then_inc(f_ready, 1)

            def update_rows(bb):
                pe.wait_ge(m_ready, bb + 1)
                for t in range(TT):
                    last = nc.tensor.transpose(banks[7][0:MC, t * P:(t + 1) * P], norm_set(NB + bb)["mm"][:, t, :], ident)
                last.then_inc(mt_ready, 1)

            def update_product(bb, first_bank=5):
                pe.wait_ge(mt_done, bb + 1)
                for t in range(TT):
                    mmul(banks[first_bank + t][:], mt[:, t * P:(t + 1) * P], dw[:], start=True, stop=True).then_inc(d_ready, 1)

            def out_product(i):
                for t in range(TT):
                    parts = [(oth[:, h, t * P:(t + 1) * P], otl[:, h, t * P:(t + 1) * P], woh[:, h, :], wol[:, h, :])
                             for h in range(QH)]
                    split_product(banks[3 + t][:], parts).then_inc(o_ready, 1)

            pe.wait_ge(cst_in, 16)
            def first_tokens(b):
                pe.wait_ge(xn_ready, b + 1)
                if b:
                    pe.wait_ge(xt_lo, 2 * b)
                transpose_tokens(b)

            first_tokens(0)
            wait_split(pe, KC - 1)
            pe.wait_ge(xt_lo, 2)
            project(0, 0, True, lambda: None, lambda: first_tokens(1))
            transpose_v(0)

            def scores(i, g, at):
                pe.wait_ge(kq_lo, i * 3 + 2)
                for j in range(QH):
                    if j == 0 and (g or at > 1):
                        pe.wait_ge(x_added, i * 2 - 2)
                    if j == 2:
                        pe.wait_ge(kq_lo, i * 3 + 3)
                        if g or at:
                            pe.wait_ge(pt_lo, i * 3)
                        else:
                            pe.wait_ge(xt_lo, 4)
                    bank = banks[3 + j]
                    mmul(bank[:, 0:P], kq[:, 1 + j, 0:P], kq[:, 0, 0:P], start=True, stop=True, skip_group_check=True)
                    qs = slice(S + j * P, S + (j + 1) * P)
                    split_product(bank[:, P:3 * P], [(kh[:, qs], kl[:, qs], kh[:, 0:S], kl[:, 0:S])]).then_inc(s_ready, 1)

            def transpose_probs(i):
                for j in range(2):
                    pe.wait_ge(p_norm, i * 4 + (2 * j + 2))
                    for h in range(2):
                        for t in range(2):
                            last = nc.tensor.transpose(banks[5 + j][:, h * S + t * P:h * S + (t + 1) * P],
                                                       sm[:, 2 * j + h, t * P:(t + 1) * P], ident)
                    last.then_inc(tr_ready, 1)
                for h in range(QH):
                    last = nc.tensor.transpose(banks[7][:, h * P:(h + 1) * P], sm[:, h, 2 * P:3 * P], ident)
                last.then_inc(tr_ready, 1)

            def attend(i):
                pe.wait_ge(pt_lo, i * 3 + 3)
                pe.wait_ge(v_lo, i + 1)
                for j in range(2):
                    split_product(banks[j][:], [(vh[:, 0, :], vl[:, 0, :], pth[:, j, :], ptl[:, j, :])], stop=False)
                    second = banks[j][:].rearrange("p (h s) -> p h s", h=2)[:, :, P:S]
                    cols = slice(j * S, (j + 1) * S)
                    split_product(second, [(vh[:, 1, :], vl[:, 1, :], pth[:, 2, cols].rearrange("p (h s) -> p h s", h=2),
                                            ptl[:, 2, cols].rearrange("p (h s) -> p h s", h=2))],
                                  start=False).then_inc(pv_ready, 1)

            def step(g, b, at):
                i = b + 8 * g
                scores(i, g, at)

                def after_kv():
                    if needs_xt(g, at):
                        pe.wait_ge(xn_ready, b + 3)
                        pe.wait_ge(s_masked, i * 4 + 4)
                        transpose_tokens(b + 2)
                    if needs_finish(g, at):
                        pe.wait_ge(s_masked, i * 4 + 4)
                        update_product(b - 3)
                    if needs_ffn(g, at):
                        pe.wait_ge(xn_ready, b + (NB - 1))
                        pe.wait_ge(s_masked, i * 4 + 2)
                        transpose_tokens(b + (NB - 2), 3)

                def before_last():
                    if needs_ffn(g, at):
                        pe.wait_ge(xt_hi, b * 2 + (2 * NB - 2))
                        pe.wait_ge(swapped, i * 3 + 4)
                        pe.wait_ge(kq_cos, i * 3 + 4)
                        gate_product(b - 2)

                if g == 0 and at < NB - 1:
                    pe.wait_ge(xt_lo, b * 2 + 4)
                if at == NB - 1:
                    wait_split(pe, (g + 1) * NCK + KC - 1)
                project(i + 1, (b + 1) if at < NB - 1 else 0, g == 0 and at == 0, after_kv, before_last)
                if g or at:
                    pe.wait_ge(pt_lo, i * 3)
                if needs_finish(g, at):
                    pe.wait_ge(out_ready, b * 2 - 4)
                if needs_xt(g, at):
                    pe.wait_ge(xt_lo, b * 2 + 6)
                transpose_probs(i)
                if g or at:
                    pe.wait_ge(s_masked, i * 4 + 4)
                    pe.wait_ge(ot_lo, i * 2)
                    if at == 1:
                        wait_split(pe, g * NCK + NCK - 1)
                    out_product(i - 1)
                transpose_v(i + 1)
                pe.wait_ge(swapped, i * 3 + 6)
                pe.wait_ge(kq_cos, i * 3 + 6)
                if needs_ffn(g, at):
                    pe.wait_ge(f_read, b - 1)
                attend(i)
                if needs_ffn(g, at):
                    update_rows(b - 2)

            steps(pe, step)
            last = NG * NB - 1
            scores(last, NG - 1, NB - 1)
            pe.wait_ge(s_masked, last * 4 + 2)
            pe.wait_ge(ot_lo, last * 2)
            out_product(last - 1)
            pe.wait_ge(s_masked, last * 4 + 4)
            update_product(NB - 4)
            pe.wait_ge(v_lo, last + 1)
            pe.wait_ge(xn_ready, 2 * NB - 2)
            transpose_tokens(2 * NB - 3, 1)
            pe.wait_ge(out_ready, 2 * (NB - 3))
            transpose_probs(last)
            pe.wait_ge(xt_hi, 2 * (2 * NB - 2))
            gate_product(NB - 3, 2)
            attend(last)
            pe.wait_ge(xn_ready, 2 * NB - 1)
            transpose_tokens(2 * NB - 2)
            pe.wait_ge(x_added, 2 * last)
            pe.wait_ge(ot_lo, 2 * last + 2)
            out_product(last)
            pe.wait_ge(xt_hi, 2 * (2 * NB - 1))
            gate_product(NB - 2)
            update_rows(NB - 3)
            update_product(NB - 3)
            pe.wait_ge(xn_ready, 2 * NB)
            pe.wait_ge(f_read, NB - 2)
            transpose_tokens(2 * NB - 1, 1)
            pe.wait_ge(f_read, NB - 1)
            pe.wait_ge(xt_hi, 2 * 2 * NB)
            gate_product(NB - 1)
            update_rows(NB - 2)
            update_product(NB - 2, 1)
            update_rows(NB - 1)
            pe.wait_ge(x_added, 2 * last + 2)
            update_product(NB - 1, 3)


def kernel(x, L0_tok_log_dt, L0_tok_log_w_real, L0_tok_w_imag, L0_attn_w_q, L0_attn_w_k, L0_attn_w_v, L0_attn_w_o,
           L0_ffn_select_weight, L0_ffn_select_mean_diff, L0_ffn_imp_center, L0_ffn_imp_slope, L0_ffn_lora_update,
           L0_ffn_lora_degen, L0_ffn_bias_w, L0_ffn_debias_w):
    import concourse.bacc as bacc
    from concourse.bass_utils import run_bass_kernel_spmd

    def a(v):
        return np.asarray(v)

    by_row = a(x).transpose(3, 2, 1, 0)
    wq = a(L0_attn_w_q).reshape(KC, P, NG, QH * HD).transpose(2, 0, 1, 3)
    wk = a(L0_attn_w_k).reshape(KC, P, NG, HD).transpose(2, 0, 1, 3)
    wv = a(L0_attn_w_v).reshape(KC, P, NG, HD).transpose(2, 0, 1, 3)

    def chunks(w):
        return w.reshape(KC, P, -1).transpose(1, 0, 2)

    arrays = {
        "mix_c": by_row.reshape(P, S, NB),
        "mix_s": by_row[::-1].reshape(P, S, NB),
        "log_dt": a(L0_tok_log_dt),
        "log_wr": a(L0_tok_log_w_real).reshape(2, P, NS).transpose(0, 2, 1).reshape(P, P),
        "w_im": a(L0_tok_w_imag).reshape(2, P, NS).transpose(0, 2, 1).reshape(P, P),
        "w_qkv": np.concatenate([wk, wv, wq], axis=-1),
        "w_o": a(L0_attn_w_o).reshape(NG, QH, HD, D),
        "w_gate": np.concatenate([chunks(a(L0_ffn_select_weight).transpose(1, 0, 2)),
                                  chunks(a(L0_ffn_select_mean_diff).T),
                                  chunks(a(L0_ffn_lora_update).transpose(1, 0, 2))], axis=-1),
        "w_gmul": chunks(a(L0_ffn_debias_w).T),
        "w_upd": np.concatenate([a(L0_ffn_lora_degen).transpose(0, 2, 1).reshape(NE * HE, D), a(L0_ffn_bias_w)]),
        "centers": a(L0_ffn_imp_center),
        "slopes": a(L0_ffn_imp_slope),
        "consts": constants(),
    }
    nc = bacc.Bacc("TRN2", target_bir_lowering=False, num_devices=1)
    args, sent = [], {}
    for name, v in arrays.items():
        v = np.ascontiguousarray(v)
        sent[f"in_{name}"] = v
        args.append(nc.dram_tensor(f"in_{name}", v.shape, mybir.dt.from_np(v.dtype), kind="ExternalInput").ap())
    out = nc.dram_tensor("out_0", (NB, S, D), F32, kind="ExternalOutput").ap()
    tower(nc, *args, out)
    r = run_bass_kernel_spmd(nc, [sent], core_ids=[0])
    return r.results[0]["out_0"]
```
